# Optimizing a Trainium2 kernel written in Bass

```python
import numpy as np
import jax
import jax.numpy as jnp

def _softmax(x, axis=-1):
    return jax.nn.softmax(x, axis=axis)

def _gelu(x):
    return jax.nn.gelu(x, approximate=True)

def _silu(x):
    return jax.nn.silu(x)

def _sigmoid(x):
    return jax.nn.sigmoid(x)

def _layernorm(x, axis=-1, eps=1e-05):
    m = jnp.mean(x, axis=axis, keepdims=True)
    v = jnp.var(x, axis=axis, keepdims=True)
    return (x - m) / jnp.sqrt(v + eps)

def _scatter_add(tgt, idx, src, axis=0):
    return tgt.at[idx].add(src)

def _segment_sum(src, seg, n):
    return jax.ops.segment_sum(src, seg, n)
kernel_name = 'mk_gnn_ffn_d2_gnn_r8_016902'

def setup_inputs(seed: int=0):
    np.random.seed(seed)
    _w = jnp.asarray

    def _rec_inputs():
        import jax
        import jax.numpy as jnp
        _gk = jax.random.key(seed)
        x = -0.0003713 + 1 * jax.random.normal(jax.random.fold_in(_gk, 1), (6250, 256), jnp.float32)
        src = jax.random.randint(jax.random.fold_in(_gk, 2), (100000,), 0, 6250, jnp.int32)
        dst = jax.random.randint(jax.random.fold_in(_gk, 3), (100000,), 0, 6250, jnp.int32)
        _o = jnp.argsort(dst, stable=True)
        src = src[_o]
        dst = dst[_o]
        return (x, src, dst)
    x, src, dst = _rec_inputs()

    def _L0_gnn_setup():
        import jax, jax.numpy as jnp
        import numpy as np
        N, E, DIN, HID, HEADS = (6250, 200000, 256, 256, 4)
        C = HID // 2 // HEADS
        NEG_SLOPE = 0.2
        BN_EPS = 1e-05

        def _gat(x, W, a_src, a_dst, b, src, dst):
            xl = (x @ W).reshape(N, HEADS, C)
            al = jnp.einsum('nhc,hc->nh', xl, a_src)
            ar = jnp.einsum('nhc,hc->nh', xl, a_dst)
            e = jax.nn.leaky_relu(al[src] + ar[dst], NEG_SLOPE)
            m = jax.ops.segment_max(e, dst, num_segments=N)
            w = jnp.exp(e - m[dst])
            den = jax.ops.segment_sum(w, dst, num_segments=N)
            alpha = w / (den[dst] + 1e-16)
            msg = xl[src] * alpha[..., None]
            out = jax.ops.segment_sum(msg, dst, num_segments=N)
            return out.reshape(N, HEADS * C) + b
        key = jax.random.key(seed)
        ks = jax.random.split(key, 16)
        s = lambda k, shp: jax.random.normal(k, shp, jnp.float32) * 0.05
        return {'x': jax.random.normal(ks[0], (N, DIN), jnp.float32), 'edge_index': jax.random.randint(ks[1], (2, E), 0, N, jnp.int32), 'W_f': s(ks[2], (DIN, HEADS * C)), 'a_src_f': s(ks[3], (HEADS, C)), 'a_dst_f': s(ks[4], (HEADS, C)), 'b_f': jnp.zeros((HEADS * C,), jnp.float32), 'W_b': s(ks[5], (DIN, HEADS * C)), 'a_src_b': s(ks[6], (HEADS, C)), 'a_dst_b': s(ks[7], (HEADS, C)), 'b_b': jnp.zeros((HEADS * C,), jnp.float32), 'W_fuse': s(ks[8], (HID, HID)), 'b_fuse': jnp.zeros((HID,), jnp.float32), 'gamma': jnp.ones((HID,), jnp.float32), 'beta': jnp.zeros((HID,), jnp.float32), 'run_mean': jnp.zeros((HID,), jnp.float32), 'run_var': jnp.ones((HID,), jnp.float32)}
    _L0_gnn_all = _L0_gnn_setup()
    _L0_gnn_in = {k: v for k, v in _L0_gnn_all.items() if k in ('W_f', 'a_src_f', 'a_dst_f', 'b_f', 'W_b', 'a_src_b', 'a_dst_b', 'b_b', 'W_fuse', 'b_fuse', 'gamma', 'beta', 'run_mean', 'run_var')}
    del _L0_gnn_all

    def _L0_ffn_setup():
        import jax, jax.numpy as jnp
        import numpy as np
        B, N, D = (16, 512, 256)
        NUM_EXPERTS, TOP_K, HEADS = (4, 2, 4)
        N_EDGES = 131072
        LN_EPS = 1e-05

        def _layernorm(x, g, b):
            mu = x.mean(-1, keepdims=True)
            var = ((x - mu) ** 2).mean(-1, keepdims=True)
            return (x - mu) * jax.lax.rsqrt(var + LN_EPS) * g + b

        def _forward(x, edge_index, W_gat, att_src, att_dst, b_gat, ln_gamma, ln_beta, W1, b1, W2, b2):
            Bc, Nc, Dc = x.shape
            M = Bc * Nc
            x_flat = x.reshape(M, Dc)
            h = (x_flat @ W_gat).reshape(M, HEADS, NUM_EXPERTS)
            loops = jnp.arange(M, dtype=edge_index.dtype)
            src = jnp.concatenate([edge_index[0], loops])
            dst = jnp.concatenate([edge_index[1], loops])
            a_src = (h * att_src).sum(-1)
            a_dst = (h * att_dst).sum(-1)
            e = jax.nn.leaky_relu(a_src[src] + a_dst[dst], negative_slope=0.2)
            e_max = jax.ops.segment_max(e, dst, num_segments=M)
            ee = jnp.exp(e - e_max[dst])
            denom = jax.ops.segment_sum(ee, dst, num_segments=M)
            alpha = ee / (denom[dst] + 1e-16)
            msg = h[src] * alpha[:, :, None]
            agg = jax.ops.segment_sum(msg, dst, num_segments=M).reshape(M, HEADS * NUM_EXPERTS) + b_gat
            scores = _layernorm(agg, ln_gamma, ln_beta).reshape(M, HEADS, NUM_EXPERTS).mean(1)
            scores = scores.reshape(Bc, Nc, NUM_EXPERTS)
            topk_s, topk_i = jax.lax.top_k(scores, TOP_K)
            w = jax.nn.softmax(topk_s, axis=-1)
            out = jnp.zeros_like(x)
            for ei in range(NUM_EXPERTS):
                g = jnp.where(topk_i == ei, w, 0.0).sum(-1)
                hh = jax.nn.gelu(x @ W1[ei] + b1[ei], approximate=False)
                out = out + g[..., None] * (hh @ W2[ei] + b2[ei])
            return out
        key = jax.random.key(seed)
        ks = jax.random.split(key, 8)
        s = 0.05
        return {'x': jax.random.normal(ks[0], (B, N, D), jnp.float32), 'W_gat': jax.random.normal(ks[1], (D, HEADS * NUM_EXPERTS), jnp.float32) * s, 'att_src': jax.random.normal(ks[2], (HEADS, NUM_EXPERTS), jnp.float32) * s, 'att_dst': jax.random.normal(ks[3], (HEADS, NUM_EXPERTS), jnp.float32) * s, 'b_gat': jnp.zeros((HEADS * NUM_EXPERTS,), jnp.float32), 'ln_gamma': jnp.ones((HEADS * NUM_EXPERTS,), jnp.float32), 'ln_beta': jnp.zeros((HEADS * NUM_EXPERTS,), jnp.float32), 'W1': jax.random.normal(ks[4], (NUM_EXPERTS, D, 2 * D), jnp.float32) * s, 'b1': jnp.zeros((NUM_EXPERTS, 2 * D), jnp.float32), 'W2': jax.random.normal(ks[5], (NUM_EXPERTS, 2 * D, D), jnp.float32) * s, 'b2': jnp.zeros((NUM_EXPERTS, D), jnp.float32), 'edge_index': jax.random.randint(ks[6], (2, N_EDGES), 0, B * N, jnp.int32)}
    _L0_ffn_all = _L0_ffn_setup()
    _L0_ffn_in = {k: v for k, v in _L0_ffn_all.items() if k in ('W_gat', 'att_src', 'att_dst', 'b_gat', 'ln_gamma', 'ln_beta', 'W1', 'b1', 'W2', 'b2', 'edge_index')}
    del _L0_ffn_all

    def _L1_gnn_setup():
        import jax, jax.numpy as jnp
        import numpy as np
        NUM_NODES = 6250
        NUM_EDGES = 2500
        NNZ = 100000
        DIM = 256

        def _layer(x, node_idx, edge_idx, norm_n2e, norm_e2n, W_n2e, W_e2n):
            h = x @ W_n2e
            msg = norm_n2e[:, None] * h[node_idx]
            e = jax.ops.segment_sum(msg, edge_idx, num_segments=NUM_EDGES)
            e = jax.nn.relu(e)
            h2 = e @ W_e2n
            msg2 = norm_e2n[:, None] * h2[edge_idx]
            n = jax.ops.segment_sum(msg2, node_idx, num_segments=NUM_NODES)
            return (n, e)
        key = jax.random.key(seed)
        ks = jax.random.split(key, 7)
        x = jax.random.normal(ks[0], (NUM_NODES, DIM), dtype=jnp.float32)
        node_idx = jax.random.randint(ks[1], (NNZ,), 0, NUM_NODES)
        edge_idx = jax.random.randint(ks[2], (NNZ,), 0, NUM_EDGES)
        hyperedge_index = jnp.stack([node_idx, edge_idx], axis=0)
        s = 1.0 / np.sqrt(DIM)
        W0_n2e = jax.random.uniform(ks[3], (DIM, DIM), jnp.float32, -s, s)
        W0_e2n = jax.random.uniform(ks[4], (DIM, DIM), jnp.float32, -s, s)
        W1_n2e = jax.random.uniform(ks[5], (DIM, DIM), jnp.float32, -s, s)
        W1_e2n = jax.random.uniform(ks[6], (DIM, DIM), jnp.float32, -s, s)
        return {'x': x, 'hyperedge_index': hyperedge_index, 'W0_n2e': W0_n2e, 'W0_e2n': W0_e2n, 'W1_n2e': W1_n2e, 'W1_e2n': W1_e2n}
    _L1_gnn_all = _L1_gnn_setup()
    _L1_gnn_in = {k: v for k, v in _L1_gnn_all.items() if k in ('W0_n2e', 'W0_e2n', 'W1_n2e', 'W1_e2n')}
    del _L1_gnn_all

    def _L1_ffn_setup():
        import math
        import jax, jax.numpy as jnp
        import numpy as np
        CAPACITY_FACTOR = 1.25
        key = jax.random.key(seed)
        ks = jax.random.split(key, 5)
        B, L, D, F, E = (8, 1024, 256, 1024, 8)
        h = jax.random.normal(ks[0], (B, L, D), dtype=jnp.float32)
        gate_w = jax.random.normal(ks[1], (D, E), dtype=jnp.float32) * 0.02
        gate_b = jnp.zeros((E,), dtype=jnp.float32)
        w1 = jax.random.normal(ks[2], (E, D, F), dtype=jnp.float32) * (1.0 / math.sqrt(D))
        b1 = jnp.zeros((E, F), dtype=jnp.float32)
        w2 = jax.random.normal(ks[3], (E, F, D), dtype=jnp.float32) * (1.0 / math.sqrt(F))
        b2 = jnp.zeros((E, D), dtype=jnp.float32)
        return {'h': h, 'gate_w': gate_w, 'gate_b': gate_b, 'w1': w1, 'b1': b1, 'w2': w2, 'b2': b2}
    _L1_ffn_all = _L1_ffn_setup()
    _L1_ffn_in = {k: v for k, v in _L1_ffn_all.items() if k in ('gate_w', 'gate_b', 'w1', 'b1', 'w2', 'b2')}
    del _L1_ffn_all
    return {'x': x, 'src': src, 'dst': dst, 'L0_gnn_W_f': _L0_gnn_in['W_f'], 'L0_gnn_a_src_f': _L0_gnn_in['a_src_f'], 'L0_gnn_a_dst_f': _L0_gnn_in['a_dst_f'], 'L0_gnn_b_f': _L0_gnn_in['b_f'], 'L0_gnn_W_b': _L0_gnn_in['W_b'], 'L0_gnn_a_src_b': _L0_gnn_in['a_src_b'], 'L0_gnn_a_dst_b': _L0_gnn_in['a_dst_b'], 'L0_gnn_b_b': _L0_gnn_in['b_b'], 'L0_gnn_W_fuse': _L0_gnn_in['W_fuse'], 'L0_gnn_b_fuse': _L0_gnn_in['b_fuse'], 'L0_gnn_gamma': _L0_gnn_in['gamma'], 'L0_gnn_beta': _L0_gnn_in['beta'], 'L0_gnn_run_mean': _L0_gnn_in['run_mean'], 'L0_gnn_run_var': _L0_gnn_in['run_var'], 'L0_ffn_W_gat': _L0_ffn_in['W_gat'], 'L0_ffn_att_src': _L0_ffn_in['att_src'], 'L0_ffn_att_dst': _L0_ffn_in['att_dst'], 'L0_ffn_b_gat': _L0_ffn_in['b_gat'], 'L0_ffn_ln_gamma': _L0_ffn_in['ln_gamma'], 'L0_ffn_ln_beta': _L0_ffn_in['ln_beta'], 'L0_ffn_W1': _L0_ffn_in['W1'], 'L0_ffn_b1': _L0_ffn_in['b1'], 'L0_ffn_W2': _L0_ffn_in['W2'], 'L0_ffn_b2': _L0_ffn_in['b2'], 'L0_ffn_edge_index': _L0_ffn_in['edge_index'], 'L1_gnn_W0_n2e': _L1_gnn_in['W0_n2e'], 'L1_gnn_W0_e2n': _L1_gnn_in['W0_e2n'], 'L1_gnn_W1_n2e': _L1_gnn_in['W1_n2e'], 'L1_gnn_W1_e2n': _L1_gnn_in['W1_e2n'], 'L1_ffn_gate_w': _L1_ffn_in['gate_w'], 'L1_ffn_gate_b': _L1_ffn_in['gate_b'], 'L1_ffn_w1': _L1_ffn_in['w1'], 'L1_ffn_b1': _L1_ffn_in['b1'], 'L1_ffn_w2': _L1_ffn_in['w2'], 'L1_ffn_b2': _L1_ffn_in['b2']}

def reference(x, src, dst, L0_gnn_W_f, L0_gnn_a_src_f, L0_gnn_a_dst_f, L0_gnn_b_f, L0_gnn_W_b, L0_gnn_a_src_b, L0_gnn_a_dst_b, L0_gnn_b_b, L0_gnn_W_fuse, L0_gnn_b_fuse, L0_gnn_gamma, L0_gnn_beta, L0_gnn_run_mean, L0_gnn_run_var, L0_ffn_W_gat, L0_ffn_att_src, L0_ffn_att_dst, L0_ffn_b_gat, L0_ffn_ln_gamma, L0_ffn_ln_beta, L0_ffn_W1, L0_ffn_b1, L0_ffn_W2, L0_ffn_b2, L0_ffn_edge_index, L1_gnn_W0_n2e, L1_gnn_W0_e2n, L1_gnn_W1_n2e, L1_gnn_W1_e2n, L1_ffn_gate_w, L1_ffn_gate_b, L1_ffn_w1, L1_ffn_b1, L1_ffn_w2, L1_ffn_b2):
    import jax
    import jax.numpy as jnp

    def _L0_gnn_ref(x, edge_index, W_f, a_src_f, a_dst_f, b_f, W_b, a_src_b, a_dst_b, b_b, W_fuse, b_fuse, gamma, beta, run_mean, run_var):
        import jax, jax.numpy as jnp
        import numpy as np
        N, E, DIN, HID, HEADS = (6250, 200000, 256, 256, 4)
        C = HID // 2 // HEADS
        NEG_SLOPE = 0.2
        BN_EPS = 1e-05

        def _gat(x, W, a_src, a_dst, b, src, dst):
            xl = (x @ W).reshape(N, HEADS, C)
            al = jnp.einsum('nhc,hc->nh', xl, a_src)
            ar = jnp.einsum('nhc,hc->nh', xl, a_dst)
            e = jax.nn.leaky_relu(al[src] + ar[dst], NEG_SLOPE)
            m = jax.ops.segment_max(e, dst, num_segments=N)
            w = jnp.exp(e - m[dst])
            den = jax.ops.segment_sum(w, dst, num_segments=N)
            alpha = w / (den[dst] + 1e-16)
            msg = xl[src] * alpha[..., None]
            out = jax.ops.segment_sum(msg, dst, num_segments=N)
            return out.reshape(N, HEADS * C) + b
        loop = jnp.arange(N, dtype=edge_index.dtype)
        src = jnp.concatenate([edge_index[0], loop])
        dst = jnp.concatenate([edge_index[1], loop])
        fwd = _gat(x, W_f, a_src_f, a_dst_f, b_f, src, dst)
        bwd = _gat(x, W_b, a_src_b, a_dst_b, b_b, dst, src)
        h = jnp.concatenate([fwd, bwd], axis=1) @ W_fuse + b_fuse
        h = (h - run_mean) * jax.lax.rsqrt(run_var + BN_EPS) * gamma + beta
        return jax.nn.relu(h)

    def _L0_ffn_ref(x, W_gat, att_src, att_dst, b_gat, ln_gamma, ln_beta, W1, b1, W2, b2, edge_index):
        import jax, jax.numpy as jnp
        import numpy as np
        B, N, D = (16, 512, 256)
        NUM_EXPERTS, TOP_K, HEADS = (4, 2, 4)
        N_EDGES = 131072
        LN_EPS = 1e-05

        def _layernorm(x, g, b):
            mu = x.mean(-1, keepdims=True)
            var = ((x - mu) ** 2).mean(-1, keepdims=True)
            return (x - mu) * jax.lax.rsqrt(var + LN_EPS) * g + b

        def _forward(x, edge_index, W_gat, att_src, att_dst, b_gat, ln_gamma, ln_beta, W1, b1, W2, b2):
            Bc, Nc, Dc = x.shape
            M = Bc * Nc
            x_flat = x.reshape(M, Dc)
            h = (x_flat @ W_gat).reshape(M, HEADS, NUM_EXPERTS)
            loops = jnp.arange(M, dtype=edge_index.dtype)
            src = jnp.concatenate([edge_index[0], loops])
            dst = jnp.concatenate([edge_index[1], loops])
            a_src = (h * att_src).sum(-1)
            a_dst = (h * att_dst).sum(-1)
            e = jax.nn.leaky_relu(a_src[src] + a_dst[dst], negative_slope=0.2)
            e_max = jax.ops.segment_max(e, dst, num_segments=M)
            ee = jnp.exp(e - e_max[dst])
            denom = jax.ops.segment_sum(ee, dst, num_segments=M)
            alpha = ee / (denom[dst] + 1e-16)
            msg = h[src] * alpha[:, :, None]
            agg = jax.ops.segment_sum(msg, dst, num_segments=M).reshape(M, HEADS * NUM_EXPERTS) + b_gat
            scores = _layernorm(agg, ln_gamma, ln_beta).reshape(M, HEADS, NUM_EXPERTS).mean(1)
            scores = scores.reshape(Bc, Nc, NUM_EXPERTS)
            topk_s, topk_i = jax.lax.top_k(scores, TOP_K)
            w = jax.nn.softmax(topk_s, axis=-1)
            out = jnp.zeros_like(x)
            for ei in range(NUM_EXPERTS):
                g = jnp.where(topk_i == ei, w, 0.0).sum(-1)
                hh = jax.nn.gelu(x @ W1[ei] + b1[ei], approximate=False)
                out = out + g[..., None] * (hh @ W2[ei] + b2[ei])
            return out
        return _forward(x, edge_index, W_gat, att_src, att_dst, b_gat, ln_gamma, ln_beta, W1, b1, W2, b2)

    def _L1_gnn_ref(x, hyperedge_index, W0_n2e, W0_e2n, W1_n2e, W1_e2n):
        import jax, jax.numpy as jnp
        import numpy as np
        NUM_NODES = 6250
        NUM_EDGES = 2500
        NNZ = 100000
        DIM = 256

        def _layer(x, node_idx, edge_idx, norm_n2e, norm_e2n, W_n2e, W_e2n):
            h = x @ W_n2e
            msg = norm_n2e[:, None] * h[node_idx]
            e = jax.ops.segment_sum(msg, edge_idx, num_segments=NUM_EDGES)
            e = jax.nn.relu(e)
            h2 = e @ W_e2n
            msg2 = norm_e2n[:, None] * h2[edge_idx]
            n = jax.ops.segment_sum(msg2, node_idx, num_segments=NUM_NODES)
            return (n, e)
        node_idx, edge_idx = (hyperedge_index[0], hyperedge_index[1])
        ones = jnp.ones((node_idx.shape[0],), dtype=x.dtype)
        Dn = jax.ops.segment_sum(ones, node_idx, num_segments=NUM_NODES)
        De = jax.ops.segment_sum(ones, edge_idx, num_segments=NUM_EDGES)
        Dn_inv = jnp.where(Dn > 0, 1.0 / Dn, 0.0)
        De_inv = jnp.where(De > 0, 1.0 / De, 0.0)
        norm_n2e = De_inv[edge_idx]
        norm_e2n = Dn_inv[node_idx]
        x1, _ = _layer(x, node_idx, edge_idx, norm_n2e, norm_e2n, W0_n2e, W0_e2n)
        x1 = jax.nn.relu(x1)
        x2, _ = _layer(x1, node_idx, edge_idx, norm_n2e, norm_e2n, W1_n2e, W1_e2n)
        return x2

    def _L1_ffn_ref(h, gate_w, gate_b, w1, b1, w2, b2):
        import math
        import jax, jax.numpy as jnp
        import numpy as np
        CAPACITY_FACTOR = 1.25
        B, L, D = h.shape
        E = gate_w.shape[1]
        T = B * L
        C = max(1, math.ceil(CAPACITY_FACTOR * T / E))
        x = h.reshape(T, D)
        logits = x @ gate_w + gate_b
        probs = jax.nn.softmax(logits, axis=-1)
        idx = jnp.argmax(probs, axis=-1)
        prb = jnp.take_along_axis(probs, idx[:, None], axis=1)[:, 0]
        one_hot = jax.nn.one_hot(idx, E, dtype=jnp.float32)
        pos = (jnp.cumsum(one_hot, axis=0) * one_hot).sum(-1).astype(jnp.int32) - 1
        kept = pos < C
        pos_safe = jnp.where(kept, pos, C)
        buf = jnp.zeros((E, C, D), dtype=h.dtype).at[idx, pos_safe].set(x, mode='drop')
        hmid = jax.nn.relu(jnp.einsum('ecd,edf->ecf', buf, w1) + b1[:, None, :])
        ybuf = jnp.einsum('ecf,efd->ecd', hmid, w2) + b2[:, None, :]
        pos_g = jnp.minimum(pos, C - 1)
        y_tok = ybuf[idx, pos_g] * (prb * kept)[:, None]
        y = y_tok.reshape(B, L, D)
        y = jnp.nan_to_num(y, nan=0.0, posinf=10000.0, neginf=-10000.0)
        return y
    edge_index = jnp.stack([src, dst])
    x = x + _L0_gnn_ref(_layernorm(x, axis=-1), edge_index, L0_gnn_W_f, L0_gnn_a_src_f, L0_gnn_a_dst_f, L0_gnn_b_f, L0_gnn_W_b, L0_gnn_a_src_b, L0_gnn_a_dst_b, L0_gnn_b_b, L0_gnn_W_fuse, L0_gnn_b_fuse, L0_gnn_gamma, L0_gnn_beta, L0_gnn_run_mean, L0_gnn_run_var)
    x = x + _L0_ffn_ref(_layernorm(x, axis=-1)[None], L0_ffn_W_gat, L0_ffn_att_src, L0_ffn_att_dst, L0_ffn_b_gat, L0_ffn_ln_gamma, L0_ffn_ln_beta, L0_ffn_W1, L0_ffn_b1, L0_ffn_W2, L0_ffn_b2, L0_ffn_edge_index)[0]
    x = x + _L1_gnn_ref(_layernorm(x, axis=-1), edge_index, L1_gnn_W0_n2e, L1_gnn_W0_e2n, L1_gnn_W1_n2e, L1_gnn_W1_e2n)
    x = x + _L1_ffn_ref(_layernorm(x, axis=-1)[None], L1_ffn_gate_w, L1_ffn_gate_b, L1_ffn_w1, L1_ffn_b1, L1_ffn_w2, L1_ffn_b2)[0]
    return x

_drawn_inputs = setup_inputs


def setup_inputs(seed=0):
    import zlib

    import numpy as np

    out = dict(_drawn_inputs(seed))
    spreads = {'L0_gnn_b_f': (0.0, 0.1),
     'L0_gnn_b_b': (0.0, 0.1),
     'L0_gnn_b_fuse': (0.0, 0.1),
     'L0_gnn_gamma': (1.0, 0.2),
     'L0_gnn_beta': (0.0, 0.1),
     'L0_gnn_run_mean': (0.0, 0.1),
     'L0_gnn_run_var': (1.0, 0.2),
     'L0_ffn_b_gat': (0.0, 0.1),
     'L0_ffn_ln_gamma': (1.0, 0.2),
     'L0_ffn_ln_beta': (0.0, 0.465),
     'L0_ffn_b1': (0.0, 0.1),
     'L0_ffn_b2': (0.0, 0.1),
     'L1_ffn_gate_b': (0.0, 2.0),
     'L1_ffn_b1': (0.0, 2.0),
     'L1_ffn_b2': (0.0, 2.0)}
    factors = {'L0_gnn_a_dst_f': 108.743,
     'L0_gnn_a_dst_b': 31.0,
     'L1_gnn_W0_n2e': 5.792,
     'L1_gnn_W0_e2n': 4.864,
     'L1_gnn_W1_n2e': 5.343,
     'L1_gnn_W1_e2n': 3.84,
     'L0_gnn_a_src_f': 2.863,
     'L1_ffn_gate_w': 4.102,
     'L1_ffn_w1': 7.084,
     'L1_ffn_w2': 4.765,
     'L0_ffn_att_dst': 8.0}
    for name, (base, spread) in spreads.items():
        noise = np.random.default_rng([zlib.crc32(name.encode()), seed]).standard_normal(out[name].shape)
        drawn = base * np.exp(spread * noise) if base else spread * noise
        out[name] = jnp.asarray(drawn.astype(out[name].dtype))
    for name, factor in factors.items():
        out[name] = (out[name] * factor).astype(out[name].dtype)
    return out
```

```python
import concourse.bass as bass
from concourse import mybir
from contextlib import ExitStack

F32 = mybir.dt.float32
I32 = mybir.dt.int32
ALU = mybir.AluOpType
ACT = mybir.ActivationFunctionType
AX = mybir.AxisListType

P = 128
N = 6250
D = 256
NT = -(-N // P)
NTP = NT + 1
NPAD = NTP * P
E1 = 100000
E2 = 131072
SORT = 1 << 17
ROW = SORT // P
ET1 = -(-E1 // P)
ET2 = E2 // P
ROUND = 16
GRP = ROUND // 2
MOST = lambda edge_tiles: -(-(edge_tiles + 2 * NT) // ROUND) * ROUND
ITEMS1 = MOST(ET1)
ITEMS2 = MOST(ET2 + 1)
PAIRS = GRP // 2
CH1 = -(-ITEMS1 // P)
CH2 = -(-ITEMS2 // P)
CHUNKS = [CH1, CH1, CH2, CH1]
LISTS = len(CHUNKS)
ITEMS = [ITEMS1, ITEMS1, ITEMS2, ITEMS1]
CHM = max(CHUNKS)
TURNS_ALL, TURNS_HYPER, LAST_TURN = 0, 1, 2
EXTRA = 3
KEY_SHIFT = 13
CODE_BASE = 1 << 28
FIELD = (1 << KEY_SHIFT) - 1
BIG = 1.0e30
HEADS = 4
CH = 32
HC = HEADS * CH
NEXP = 4
FH = 512
MEXP = 8
MF = 1024
NHYP = 2500
NHT = -(-NHYP // P)
CAP = -(-(5 * N) // (4 * MEXP))
CAPP = -(-CAP // P) * P
EPS = 1e-5


class Chain:

    def __init__(self, eng, sem):
        self.eng, self.sem, self.base, self.count = eng, sem, 0, 0

    def value(self):
        return self.base + self.count

    def mark(self, ins):
        ins.then_inc(self.sem, 1)
        self.count += 1

    def wait(self):
        self.eng.wait_ge(self.sem, self.value())

    def __call__(self, ins):
        self.mark(ins)
        self.wait()

    def enter(self, t, per_turn):
        self.outer = self.value()
        self.per_turn = per_turn
        self.base, self.count = t * per_turn + self.outer, 0

    def enter_last(self, t):
        self.leave(0)
        self.enter(t, self.per_turn)

    def leave(self, turns):
        assert self.count == self.per_turn, (self.count, self.per_turn)
        self.base, self.count = self.outer + turns * self.per_turn, 0


class Space:

    def __init__(self, nc, ctx, prefix):
        self.nc, self.ctx, self.prefix, self.sems = nc, ctx, prefix, []

    def sb(self, name, shape, dt=F32):
        return self.ctx.enter_context(self.nc.sbuf_tensor(f"{self.prefix}_{name}", shape, dt))

    def ps(self, name, shape, dt=F32):
        return self.ctx.enter_context(self.nc.psum_tensor(f"{self.prefix}_{name}", shape, dt))

    def sem(self, name):
        self.sems.append(self.ctx.enter_context(self.nc.semaphore(f"{self.prefix}_{name}")))
        return self.sems[-1]

    def gathered(self, i):
        self.sems.append(GATHERED[i])
        return self.sems[-1]

    def block(self):
        self.ctx.callback(self.clear)
        return self.ctx.enter_context(self.nc.Block())

    def clear(self):
        for s in self.sems:
            if s in GATHERED:
                self.nc.gpsimd.dma_reset(range(s.num, s.num + 1))
            self.nc.gpsimd.sem_clear(s)
        self.nc.all_engine_barrier(sem_only=True)


GATHERED = []


def constants(nc, c):
    ctx = ExitStack()
    with ctx:
        sp_ = Space(nc, ctx, "const")
        s_pool, s_dve = sp_.sem("pool"), sp_.sem("dve")
        ramp_i = sp_.sb("ramp_i", [P, CHM * P], I32)
        part_i = sp_.sb("part_i", [P, 1], I32)
        row_i = sp_.sb("row_i", [P, CHM], I32)
        bits = sp_.sb("bits", [P, 8], I32)
        block = sp_.block()

        @block.gpsimd
        def _(pool):
            nc.gpsimd.memset(c["ident"][:, :], 0.0).then_inc(s_pool, 1)
            nc.gpsimd.memset(c["ones"][:, :], 1.0).then_inc(s_pool, 1)
            nc.gpsimd.iota(ramp_i[:, :], pattern=[[1, CHM * P]], base=0, channel_multiplier=0).then_inc(s_pool, 1)
            nc.gpsimd.iota(part_i[:, :], pattern=[[1, 1]], base=0, channel_multiplier=1).then_inc(s_pool, 1)
            nc.gpsimd.iota(row_i[:, :], pattern=[[P, CHM]], base=0, channel_multiplier=1).then_inc(s_pool, 1)
            pool.wait_ge(s_pool, 5)
            nc.gpsimd.affine_select(out=c["ident"][:, :], in_=c["ident"][:, :], compare_op=ALU.not_equal, fill=1.0,
                                    base=0, pattern=[[-1, P]], channel_multiplier=1).then_inc(s_pool, 1)

        @block.vector
        def _(dve):
            done = Chain(dve, s_dve)
            dve.wait_ge(s_pool, 5)
            nc.vector.tensor_copy(c["ramp"][:, :], ramp_i[:, :])
            nc.vector.tensor_copy(c["part"][:, :], part_i[:, :])
            nc.vector.tensor_copy(c["item_of"][:, :], row_i[:, :])
            for b in range(7):
                done.mark(nc.vector.tensor_scalar(bits[:, b:b + 1], part_i[:, :], b, 1,
                                                  ALU.logical_shift_right, ALU.bitwise_and))
            done.wait()
            done(nc.vector.tensor_scalar(c["sign"][:, 0:7], bits[:, 0:7], -2.0, 1.0, ALU.mult, ALU.add))
            done.mark(nc.vector.tensor_tensor(c["turn"][:, 1:7], c["sign"][:, 0:6], c["sign"][:, 1:7], ALU.mult))
            done.mark(nc.vector.tensor_copy(c["turn"][:, 0:1], c["sign"][:, 0:1]))
            done(nc.vector.tensor_copy(c["turn"][:, 7:8], c["sign"][:, 6:7]))


def sort_edges(nc, c, src, dst, edges2, rec):
    ctx = ExitStack()
    with ctx:
        sp_ = Space(nc, ctx, "sort")
        ends = sp_.sb("ends", [P, 4, ROW], I32)
        pay = sp_.sb("pay", [P, LISTS, ROW], I32)
        beyond = sp_.sb("beyond", [P, ROW], I32)
        xy = [sp_.sb("x", [P, LISTS * ROW]), sp_.sb("y", [P, LISTS * ROW])]
        pad = sp_.sb("pad", [1, P], I32)
        flip = sp_.ps("flip", [P, LISTS * ROW])
        s_pad, s_load = sp_.sem("pad"), sp_.sem("load")
        s_dve, s_ready, s_flipped, s_half, s_out = (sp_.sem(x) for x in ("dve", "ready", "flipped", "half", "out"))
        HALF = LISTS * ROW // 2
        full = E1 // ROW * ROW // (16 * ROW) * 16
        rest = E1 - full * ROW
        block = sp_.block()

        @block.gpsimd
        def _(pool):
            nc.gpsimd.memset(ends[:, 0:2, :], N).then_inc(s_pad, 1)
            nc.gpsimd.memset(pad[:, :], CODE_BASE + (N << KEY_SHIFT)).then_inc(s_pad, 1)

        @block.sync
        def _(sp):
            for j in range(2):
                sp.dma_start(ends[:, 2 + j, :], edges2[1 - j, :].rearrange("(p c) -> p c", c=ROW)).then_inc(s_load, 16)
            sp.wait_ge(s_pad, 2)
            for j, a in ((0, dst), (1, src)):
                sp.dma_start(ends[0:full, j, :], a[0:full * ROW].rearrange("(p c) -> p c", c=ROW)).then_inc(s_load, 16)
                sp.dma_start(ends[full:full + rest // ROW, j, :],
                             a[full * ROW:full * ROW + rest // ROW * ROW].rearrange("(p c) -> p c", c=ROW)).then_inc(s_load, 16)
                sp.dma_start(ends[full + rest // ROW:full + rest // ROW + 1, j, 0:rest % ROW],
                             a[E1 - rest % ROW:E1].rearrange("(p c) -> p c", p=1)).then_inc(s_load, 16)
            for s in range(LISTS):
                sp.dma_start(rec[s][ET2:ET2 + 1, :], pad[:, :]).then_inc(s_out, 16)
            sp.wait_ge(s_ready, 15)
            for s in range(LISTS):
                sp.dma_start(rec[s][0:ET2, :].rearrange("(p a) b -> p (a b)", a=ROW // P),
                             xy[0][:, s * ROW:(s + 1) * ROW].bitcast(I32)).then_inc(s_out, 16)
            sp.wait_ge(s_out, 16 * 2 * LISTS)

        @block.vector
        def _(dve):
            done = Chain(dve, s_dve)
            at = [0]

            def swap():
                at[0] ^= 1
                return xy[at[0] ^ 1], xy[at[0]]

            dve.wait_ge(s_load, 16 * 8)
            for s, (k, v) in enumerate(((0, 1), (1, 0), (2, 3), (1, 0))):
                done.mark(nc.vector.tensor_scalar_min(pay[:, s, :], ends[:, v, :], float(N - 1)))
            done.wait()
            done(nc.vector.tensor_scalar_min(ends[:, :, :], ends[:, :, :], float(N)))
            done(nc.vector.tensor_scalar(beyond[:, :], ends[:, 0, :], float(NHYP), float(N), ALU.is_ge, ALU.mult))
            done(nc.vector.tensor_tensor(ends[:, 3, :], ends[:, 1, :], beyond[:, :], ALU.max))
            x = xy[0][:, :].bitcast(I32).rearrange("p (s c) -> p s c", s=LISTS)
            y = xy[1][:, :].bitcast(I32).rearrange("p (s c) -> p s c", s=LISTS)
            done(nc.vector.tensor_scalar(y, ends[:, :, :], KEY_SHIFT, CODE_BASE, ALU.logical_shift_left, ALU.bitwise_or))
            done(nc.vector.tensor_tensor(x, y, pay[:, :, :], ALU.bitwise_or))

            def exchange(gap):
                a, b = swap()
                a, b = (z[:, :].rearrange("p (m two j) -> p m two j", two=2, j=gap) for z in (a, b))
                done.mark(nc.vector.tensor_tensor(b[:, :, 0, :], a[:, :, 0, :], a[:, :, 1, :], ALU.min))
                done(nc.vector.tensor_tensor(b[:, :, 1, :], a[:, :, 0, :], a[:, :, 1, :], ALU.max))

            def exchange_both_ways(gap, run):
                a, b = swap()
                a, b = (z[:, :].rearrange("p (g d m two j) -> p g d m two j", d=2, m=run // (2 * gap), two=2, j=gap)
                        for z in (a, b))
                for d, lower, upper in ((0, ALU.min, ALU.max), (1, ALU.max, ALU.min)):
                    for half, op in ((0, lower), (1, upper)):
                        done.mark(nc.vector.tensor_tensor(b[:, :, d, :, half, :], a[:, :, d, :, 0, :],
                                                          a[:, :, d, :, 1, :], op))
                done.wait()

            def turn(b):
                a, z = swap()
                done(nc.vector.tensor_scalar(z[:, :], a[:, :], c["turn"][:, b:b + 1], None, ALU.mult))

            def change_layout(n):
                a, b = swap()
                dve.sem_inc(s_ready)
                dve.wait_ge(s_flipped, n)
                done(nc.vector.tensor_copy(b[:, 0:HALF], flip[:, 0:HALF]))
                dve.wait_ge(s_half, n)

            for k in range(1, 10):
                for j in range(k - 1, -1, -1):
                    exchange_both_ways(1 << j, 1 << k)
            turn(0)
            for j in range(9, -1, -1):
                exchange(1 << j)
            n = 0
            for k in range(11, 18):
                turn(k - 10)
                n += 1
                change_layout(n)
                for j in range(k - 1, 6, -1):
                    exchange(1 << (j - 10) if j >= 10 else P << (j - 7))
                n += 1
                change_layout(n)
                for j in range(6, -1, -1):
                    exchange(1 << j)
            if at[0]:
                a, b = swap()
                done(nc.vector.tensor_copy(b[:, :], a[:, :]))
            dve.sem_inc(s_ready)

        at = [0]

        @block.tensor
        def _(pe):
            for n, (x, _) in enumerate(layouts()):
                pe.wait_ge(s_ready, n + 1)
                for b in range(LISTS * ROW // P):
                    last = nc.tensor.transpose(flip[:, b * P:(b + 1) * P], xy[x][:, b * P:(b + 1) * P], c["ident"][:, :])
                last.then_inc(s_flipped, 1)

        @block.scalar
        def _(act):
            for n, (_, y) in enumerate(layouts()):
                act.wait_ge(s_flipped, n + 1)
                nc.scalar.copy(xy[y][:, HALF:], flip[:, HALF:]).then_inc(s_half, 1)


def layouts():
    at = sum(range(1, 10)) + 1 + 10
    for k in range(11, 18):
        at += 1
        yield at % 2, (at + 1) % 2
        at += 1 + (k - 7)
        yield at % 2, (at + 1) % 2
        at += 1 + 7


def make_items(nc, c, s, rec, local_rows, tables, node_rows):
    chunks, n_items = CHUNKS[s], CHUNKS[s] * P
    ctx = ExitStack()
    with ctx:
        sp_ = Space(nc, ctx, f"items{s}")
        last_code = sp_.sb("last_code", [P, ROW // P], I32)
        last_key_i = sp_.sb("last_key_i", [P, ROW // P], I32)
        last_key = sp_.sb("last_key", [P, ROW // P])
        bound = sp_.sb("bound", [P, NTP])
        below = sp_.sb("below", [P, NTP, ROW // P])
        count = sp_.sb("count", [P, NTP])
        first = sp_.sb("first", [1, NTP])
        items_i = sp_.sb("items_i", [1, NT], I32)
        items_f = sp_.sb("items_f", [1, NT])
        ones = sp_.sb("ones", [1, NT])
        start = sp_.sb("start", [1, NTP])
        ahead = sp_.sb("ahead", [1, NTP])
        step = sp_.sb("step", [1, NT])
        turns = sp_.sb("turns", [1, EXTRA])
        turns_i = sp_.sb("turns_i", [1, EXTRA], I32)
        start_c, step_c = sp_.sb("start_c", [NT, 1]), sp_.sb("step_c", [NT, 1])
        began = sp_.sb("began", [NT, n_items])
        node_of, off_of = sp_.sb("node_of", [P, chunks]), sp_.sb("off_of", [P, chunks])
        tile_f = sp_.sb("tile_f", [P, chunks])
        tile_i = sp_.sb("tile_i", [P, chunks], I32)
        rows = sp_.sb("rows", [P, chunks, P], I32)
        keys_r = sp_.sb("keys_r", [P, chunks, P], I32)
        local_r = sp_.sb("local_r", [P, chunks, P])
        code_t = sp_.sb("code_t", [P, n_items])
        keys_t = sp_.sb("keys_t", [P, n_items], I32)
        p_first = sp_.ps("p_first", [P, 512])
        p_node = sp_.ps("p_node", [P, 3, 512])
        p_flip = sp_.ps("p_flip", [P, 3, 512])
        s_load, s_dve, s_first, s_began, s_node, s_tile, s_out = (
            sp_.sem(x) for x in ("load", "dve", "first", "began", "node", "tile", "out"))
        s_flip, s_table, s_count, s_start, s_column = (sp_.sem(x) for x in ("flip", "table", "count", "start", "column"))
        s_rows = sp_.gathered(0)
        g = {"pay": sp_.sb("pay", [P, n_items], I32), "key": sp_.sb("key", [P, n_items]),
             "local": sp_.sb("local", [P, n_items]), "node_f": sp_.sb("node_f", [P, n_items]),
             "node_i": sp_.sb("node_i", [1, n_items + EXTRA], I32)}
        parts = [(a, min(a + 384, n_items)) for a in range(0, n_items, 384)]
        block = sp_.block()

        @block.sync
        def _(sp):
            with nc.allow_non_contiguous_dma(reason="the last code of every edge tile"):
                sp.dma_start(last_code[:, :], rec[s][0:ET2, P - 1].rearrange("(p a) -> p a", a=ROW // P)).then_inc(s_load, 16)
            sp.wait_ge(s_table, 1)
            for q in range(chunks):
                sp.dma_start(local_rows[s][q * P:(q + 1) * P, :], local_r[:, q, :]).then_inc(s_out, 16)
            sp.wait_ge(s_table, 2)
            sp.dma_start(tables[s][0, :, :], g["pay"][:, :]).then_inc(s_out, 16)
            sp.dma_start(tables[s][1, :, :], g["key"][:, :].bitcast(I32)).then_inc(s_out, 16)
            sp.dma_start(tables[s][2, :, :], g["local"][:, :].bitcast(I32)).then_inc(s_out, 16)
            sp.dma_start(node_rows[s], g["node_i"][:, :]).then_inc(s_out, 16)
            sp.wait_ge(s_out, 16 * (chunks + 4))

        @block.vector
        def _(dve):
            done = Chain(dve, s_dve)
            dve.wait_ge(s_load, 16)
            done(nc.vector.tensor_scalar(last_key_i[:, :], last_code[:, :], KEY_SHIFT, FIELD,
                                         ALU.logical_shift_right, ALU.bitwise_and))
            done.mark(nc.vector.tensor_copy(last_key[:, :], last_key_i[:, :]))
            done(nc.vector.tensor_scalar(bound[:, :], c["ramp"][:, 0:NTP], float(P), float(N), ALU.mult, ALU.min))
            done(nc.vector.tensor_tensor(below[:, :, :], last_key[:, None, :].to_broadcast([P, NTP, ROW // P]),
                                         bound[:, :, None].to_broadcast([P, NTP, ROW // P]), ALU.is_lt))
            done(nc.vector.tensor_reduce(count[:, :], below[:, :, :], axis=AX.X, op=ALU.add))
            dve.sem_inc(s_count)
            dve.wait_ge(s_first, 1)
            done(nc.vector.tensor_copy(first[:, :], p_first[0:1, 0:NTP]))
            done(nc.vector.tensor_tensor(items_f[:, :], first[:, 1:], first[:, 0:NT], ALU.subtract))
            done(nc.vector.tensor_scalar(items_i[:, :], items_f[:, :], 2.0, None, ALU.add))
            done(nc.vector.tensor_scalar(items_i[:, :], items_i[:, :], 1, 1, ALU.logical_shift_right, ALU.logical_shift_left))
            done.mark(nc.vector.tensor_copy(items_f[:, :], items_i[:, :]))
            done.mark(nc.vector.memset(ones[:, :], 1.0))
            done(nc.vector.memset(start[:, 0:1], 0.0))
            done(nc.vector.tensor_tensor_scan(start[:, 1:], ones[:, :], items_f[:, :], 0.0, ALU.mult, ALU.add))
            done(nc.vector.tensor_tensor(ahead[:, :], start[:, :], first[:, :], ALU.subtract))
            done.mark(nc.vector.memset(step[:, 0:1], 0.0))
            done.mark(nc.vector.tensor_tensor(step[:, 1:], ahead[:, 1:NT], ahead[:, 0:NT - 1], ALU.subtract))
            for at, b, more in ((TURNS_ALL, NT, ROUND - 1.0), (TURNS_HYPER, NHT, ROUND - 1.0), (LAST_TURN, NT, -1.0)):
                done.mark(nc.vector.tensor_scalar(turns[:, at:at + 1], start[:, b:b + 1], more, None, ALU.add))
            done.wait()
            done(nc.vector.tensor_copy(turns_i[:, :], turns[:, :]))
            done(nc.vector.tensor_scalar(g["node_i"][:, n_items:], turns_i[:, :], ROUND.bit_length() - 1, None,
                                         ALU.logical_shift_right))
            dve.sem_inc(s_start)
            dve.wait_ge(s_column, 1)
            done.mark(nc.vector.tensor_copy(start_c[:, :], p_first[0:NT, 64:65]))
            done(nc.vector.tensor_copy(step_c[:, :], p_first[0:NT, 65:66]))
            done(nc.vector.tensor_scalar(began[:, :], c["ramp"][0:NT, 0:n_items], start_c[:, 0:1], None, ALU.is_ge))
            done(nc.vector.memset(began[0:1, :], 0.0))
            dve.sem_inc(s_began)
            dve.wait_ge(s_node, 1)
            done.mark(nc.vector.tensor_copy(node_of[:, :], p_first[:, 128:128 + chunks]))
            done(nc.vector.tensor_copy(off_of[:, :], p_first[:, 192:192 + chunks]))
            done(nc.vector.tensor_tensor(tile_f[:, :], c["item_of"][:, 0:chunks], off_of[:, :], ALU.subtract))
            done(nc.vector.tensor_scalar_min(tile_f[:, :], tile_f[:, :], float(ET2)))
            done(nc.vector.tensor_copy(tile_i[:, :], tile_f[:, :]))
            dve.sem_inc(s_tile)
            for n, (a, b) in enumerate(parts):
                done.mark(nc.vector.tensor_copy(g["node_f"][:, a:b], p_node[:, n, 0:b - a]))
            done.wait()
            done(nc.vector.tensor_copy(g["node_i"][:, 0:n_items], g["node_f"][0:1, :]))
            dve.wait_ge(s_rows, 16 * chunks)
            done(nc.vector.tensor_scalar(keys_r[:, :, :], rows[:, :, :], KEY_SHIFT, FIELD,
                                         ALU.logical_shift_right, ALU.bitwise_and))
            done(nc.vector.tensor_copy(local_r[:, :, :], keys_r[:, :, :]))
            for q in range(chunks):
                done(nc.vector.scalar_tensor_tensor(local_r[:, q, :], node_of[:, q:q + 1].to_broadcast([P, P]), -float(P),
                                                    local_r[:, q, :], ALU.mult, ALU.add))
            dve.sem_inc(s_table)
            dve.wait_ge(s_flip, 1)
            for n, (a, b) in enumerate(parts):
                done.mark(nc.vector.tensor_copy(code_t[:, a:b], p_flip[:, n, 0:b - a]))
            done.wait()
            code = code_t[:, :].bitcast(I32)
            done.mark(nc.vector.tensor_scalar(g["pay"][:, :], code, FIELD, None, ALU.bitwise_and))
            done(nc.vector.tensor_scalar(keys_t[:, :], code, KEY_SHIFT, FIELD, ALU.logical_shift_right, ALU.bitwise_and))
            done(nc.vector.tensor_copy(g["key"][:, :], keys_t[:, :]))
            done(nc.vector.scalar_tensor_tensor(g["local"][:, :], g["node_f"][:, :], -float(P), g["key"][:, :],
                                                ALU.mult, ALU.add))
            dve.sem_inc(s_table)

        @block.tensor
        def _(pe):
            pe.wait_ge(s_count, 1)
            nc.tensor.matmul(p_first[:, 0:NTP], c["ones"][:, :], count[:, :], start=True, stop=True).then_inc(s_first, 1)
            pe.wait_ge(s_start, 1)
            nc.tensor.matmul(p_first[0:NT, 64:65], start[:, 0:NT], c["ones"][0:1, 0:1], start=True, stop=True)
            nc.tensor.matmul(p_first[0:NT, 65:66], step[:, :], c["ones"][0:1, 0:1], start=True, stop=True).then_inc(s_column, 1)
            pe.wait_ge(s_began, 1)
            for n, (a, b) in enumerate(parts):
                nc.tensor.matmul(p_node[:, n, 0:b - a], c["ones"][0:NT, :], began[:, a:b], start=True, stop=True)
            for q in range(chunks):
                nc.tensor.matmul(p_first[:, 128 + q:129 + q], began[:, q * P:(q + 1) * P], c["ones"][0:NT, 0:1],
                                 start=True, stop=True)
                last = nc.tensor.matmul(p_first[:, 192 + q:193 + q], began[:, q * P:(q + 1) * P], step_c[:, :],
                                        start=True, stop=True)
            last.then_inc(s_node, 1)
            pe.wait_ge(s_rows, 16 * chunks)
            for q in range(chunks):
                last = nc.tensor.transpose(p_flip[:, q // 3, q % 3 * P:(q % 3 + 1) * P],
                                           rows[:, q, :].bitcast(F32), c["ident"][:, :])
            last.then_inc(s_flip, 1)

        @block.gpsimd
        def _(pool):
            pool.wait_ge(s_tile, 1)
            for q in range(chunks):
                pool.indirect_dma_start(out=rows[:, q, :], out_offset=None, in_=rec[s][:, :],
                                        in_offset=bass.IndirectOffsetOnAxis(ap=tile_i[:, q:q + 1], axis=0)).then_inc(s_rows, 16)



def normalise(nc, c, name, x_in, xt, rows_out=None):
    ctx = ExitStack()
    with ctx:
        sp_ = Space(nc, ctx, name)
        x = sp_.sb("x", [P, NTP, D])
        stats = sp_.sb("stats", [P, NTP, 6])
        mean, dev, var, rstd = (sp_.sb(n, [P, NTP]) for n in ("mean", "dev", "var", "rstd"))
        y = sp_.sb("y", [P, 2, D])
        p_t = sp_.ps("p_t", [P, 2, 2, 256])
        s_load, s_dve, s_stats, s_var, s_std = (sp_.sem(n) for n in ("load", "dve", "stats", "var", "std"))
        s_y, s_t, s_xt = sp_.sem("y_ready"), sp_.sem("t_ready"), sp_.sem("t_free")
        s_out = [sp_.sem("out0"), sp_.sem("out1")]
        block = sp_.block()

        @block.sync
        def _(sp):
            sp.dma_start(x[:, :, :], x_in.rearrange("(t p) d -> p t d", p=P)).then_inc(s_load, 16)
            if rows_out is not None:
                for h in range(2):
                    sp.sem_inc(s_out[h], 16)
                with sp.Fori(0, NTP // 2) as t:
                    for h in range(2):
                        sp.wait_ge(s_y, 2 * t + (h + 1))
                        sp.dma_start(rows_out[bass.ds((2 * t + h) * P, P), :], y[:, h, :]).then_inc(s_out[h], 16)
                for h in range(2):
                    sp.wait_ge(s_out[h], 16 * (NTP // 2 + 1))

        @block.vector
        def _(dve):
            dve.wait_ge(s_load, 16)
            with dve.Fori(0, NTP // 2) as t:
                for h in range(2):
                    nc.vector.bn_stats(stats[:, bass.ds(2 * t + h, 1), :],
                                       x[:, bass.ds(2 * t + h, 1), :]).then_inc(s_stats, 1)
            done = Chain(dve, s_dve)
            dve.wait_ge(s_stats, NTP)
            even, odd = stats[:, :, 1], stats[:, :, 4]
            done.mark(nc.vector.tensor_tensor(mean[:, :], even, odd, ALU.add))
            done.mark(nc.vector.tensor_tensor(dev[:, :], even, odd, ALU.subtract))
            done(nc.vector.tensor_tensor(var[:, :], stats[:, :, 2], stats[:, :, 5], ALU.add))
            done.mark(nc.vector.tensor_scalar(mean[:, :], mean[:, :], 0.5, None, ALU.mult))
            done.mark(nc.vector.tensor_scalar(var[:, :], var[:, :], 1.0 / D, EPS, ALU.mult, ALU.add))
            done(nc.vector.tensor_tensor(dev[:, :], dev[:, :], dev[:, :], ALU.mult))
            done(nc.vector.scalar_tensor_tensor(var[:, :], dev[:, :], 0.25, var[:, :], ALU.mult, ALU.add))
            dve.sem_inc(s_var)
            dve.wait_ge(s_std, 1)
            done(nc.vector.reciprocal(rstd[:, :], rstd[:, :]))
            with dve.Fori(0, NTP // 2) as t:
                for h in range(2):
                    if rows_out is not None:
                        dve.wait_ge(s_out[h], 16 * t + 16)
                    dve.wait_ge(s_t, 2 * t + (h + 1))
                    nc.vector.tensor_scalar(y[:, h, :], x[:, bass.ds(2 * t + h, 1), :], mean[:, bass.ds(2 * t + h, 1)],
                                            rstd[:, bass.ds(2 * t + h, 1)], ALU.subtract, ALU.mult).then_inc(s_y, 1)

        @block.tensor
        def _(pe):
            pe.sem_inc(s_t, 2)
            with pe.Fori(0, NTP // 2) as t:
                for h in range(2):
                    pe.wait_ge(s_xt, 2 * t + (h + 1))
                    pe.wait_ge(s_y, 2 * t + (h + 1))
                    for k in range(2):
                        last = nc.tensor.transpose(p_t[:, h, k, 0:P], y[:, h, k * P:(k + 1) * P], c["ident"][:, :])
                    last.then_inc(s_t, 1)

        @block.scalar
        def _(act):
            act.wait_ge(s_var, 1)
            nc.scalar.activation(rstd[:, :], var[:, :], ACT.Sqrt).then_inc(s_std, 1)
            act.sem_inc(s_xt, 2)
            nc.scalar.mul(xt[:, :, NPAD:], c["ramp"][:, None, 0:2 * P].to_broadcast([P, 2, 2 * P]), 0.0)
            with act.Fori(0, NTP // 2) as t:
                for h in range(2):
                    act.wait_ge(s_t, 2 * t + (h + 3))
                    nc.scalar.copy(xt[:, :, bass.ds((2 * t + h) * P, P)], p_t[:, h, :, 0:P]).then_inc(s_xt, 1)


def project(nc, c, name, xt, weights, graphs):
    ctx = ExitStack()
    with ctx:
        sp_ = Space(nc, ctx, name)
        width = graphs[0]["width"]
        n_g = len(graphs)
        w = sp_.sb("w", [P, 2, n_g * width])
        att = sp_.sb("att", [P, 2, n_g * width])
        prod = sp_.sb("prod", [P, 2, n_g * width])
        rows = sp_.sb("rows", [P, 2, n_g, width + HEADS])
        scores = sp_.sb("scores", [P, 2, 2, n_g * HEADS])
        nodes = [sp_.sb(f"nodes{i}", [P, NTP, 2 * HEADS]) for i in range(n_g)]
        slot = sp_.sb("slot", [P, 2, 2, P])
        p_x = sp_.ps("p_x", [P, 2, 512])
        s_load, s_dve, s_x, s_scores, s_rows, s_fin, s_slot = (
            sp_.sem(n) for n in ("load", "dve", "x_ready", "scores", "rows", "fin", "slot"))
        s_out = [sp_.sem("out0"), sp_.sem("out1")]
        block = sp_.block()

        @block.sync
        def _(sp):
            for i, g in enumerate(graphs):
                for k in range(2):
                    sp.dma_start(w[:, k, i * width:(i + 1) * width], weights[i][k * P:(k + 1) * P, :]).then_inc(s_load, 16)
                for j, a in enumerate((g["a_dst"], g["a_src"])):
                    sp.dma_start(att[:, j, i * width:(i + 1) * width],
                                 a.rearrange("h c -> (h c)").partition_broadcast(P)).then_inc(s_load, 16)
            for h in range(2):
                sp.sem_inc(s_out[h], 16 * n_g)
            with sp.Fori(0, NTP // 2) as t:
                for h in range(2):
                    sp.wait_ge(s_scores, 2 * t + (h + 1))
                    for i, g in enumerate(graphs):
                        sp.dma_start(g["table"][bass.ds((2 * t + h) * P, P), :], rows[:, h, i, :]).then_inc(s_out[h], 16)
            for h in range(2):
                sp.wait_ge(s_out[h], 16 * n_g * (NTP // 2 + 1))
            for i, g in enumerate(graphs):
                sp.dma_start(g["nodes"], nodes[i][:, :, :]).then_inc(s_fin, 16)
            sp.wait_ge(s_fin, 16 * n_g)

        @block.tensor
        def _(pe):
            pe.wait_ge(s_load, 16 * 4 * n_g)
            with pe.Fori(0, NTP // 2) as t:
                for h in range(2):
                    pe.wait_ge(s_rows, 2 * t + (h + 1))
                    pe.wait_ge(s_slot, 2 * t + (h + 1))
                    for k in range(2):
                        last = nc.tensor.matmul(p_x[:, h, 0:n_g * width], slot[:, h, k, :],
                                                w[:, k, :], start=(k == 0), stop=(k == 1))
                    last.then_inc(s_x, 1)

        @block.scalar
        def _(act):
            act.sem_inc(s_rows, 2)
            for h in range(2):
                nc.scalar.copy(slot[:, h, :, :], xt[:, :, h * P:(h + 1) * P]).then_inc(s_slot, 1)
            with act.Fori(0, NTP // 2) as t:
                for h in range(2):
                    act.wait_ge(s_out[h], 16 * n_g * t + 16 * n_g)
                    act.wait_ge(s_x, 2 * t + (h + 1))
                    last = nc.scalar.copy(rows[:, h, :, 0:width],
                                          p_x[:, h, 0:n_g * width].rearrange("p (g c) -> p g c", g=n_g))
                    last.then_inc(s_rows, 1)
                    nc.scalar.copy(slot[:, h, :, :],
                                   xt[:, :, bass.ds((2 * t + (h + 2)) * P, P)]).then_inc(s_slot, 1)

        @block.vector
        def _(dve):
            done = Chain(dve, s_dve)
            dve.wait_ge(s_load, 16 * 4 * n_g)
            with dve.Fori(0, NTP // 2) as t:
                done.enter(t, 2 * 4)
                for h in range(2):
                    dve.wait_ge(s_rows, 2 * t + (h + 3))
                    for j in range(2):
                        done.mark(nc.vector.tensor_tensor(
                            prod[:, j, :].rearrange("p (g c) -> p g c", g=n_g), rows[:, h, :, 0:width],
                            att[:, j, :].rearrange("p (g c) -> p g c", g=n_g), ALU.mult))
                    done.wait()
                    for j in range(2):
                        done.mark(nc.vector.tensor_reduce(
                            scores[:, h, j, :], prod[:, j, :].rearrange("p (g c) -> p g c", g=n_g * HEADS),
                            axis=AX.X, op=ALU.add))
                    done.wait()
                    dve.wait_ge(s_out[h], 16 * n_g * t + 16 * n_g)
                    for i in range(n_g):
                        nc.vector.tensor_copy(
                            nodes[i][:, bass.ds(2 * t + h, 1), :].rearrange("p a (j e) -> p (a j) e", j=2),
                            scores[:, h, :, i * HEADS:(i + 1) * HEADS])
                        last = nc.vector.tensor_copy(rows[:, h, i, width:], scores[:, h, 1, i * HEADS:(i + 1) * HEADS])
                    last.then_inc(s_scores, 1)
                done.leave(NTP // 2)


def turns_of(eng, node_i, s, which=TURNS_ALL):
    at = CHUNKS[s] * P + which
    return eng.value_load(node_i[0:1, at:at + 1], min_val=int(which != LAST_TURN), max_val=ITEMS[s] // ROUND)


def attend_gather(nc, c, name, s, width, table, nodes_in, tables, local_rows, node_rows, rows_out, al, ard):
    ctx = ExitStack()
    with ctx:
        sp_ = Space(nc, ctx, name)
        cols = CHUNKS[s] * P
        w = width + HEADS
        pay = sp_.sb("pay", [P, cols], I32)
        node_i = sp_.sb("node_i", [1, cols + EXTRA], I32)
        nodes = sp_.sb("nodes", [P, NTP, 2 * HEADS])
        index = sp_.sb("index", [P, 2, GRP], I32)
        got = sp_.sb("got", [P, 2, GRP, w])
        local = sp_.sb("local", [P, 2, GRP * P])
        spread = sp_.sb("spread", [P, 2, GRP * P])
        mine = sp_.sb("mine", [P, 2, PAIRS, 2 * HEADS])
        p_ard = sp_.ps("p_ard", [P, 2, 512])
        s_load, s_zero, s_index, s_turn, s_kept, s_spread, s_sfree, s_ard, s_pfree, s_mine = (
            sp_.sem(n) for n in ("load", "zero", "index", "turn", "kept", "spread", "sfree", "ard", "pfree", "mine"))
        s_local, s_out = ([sp_.sem(f"{n}{h}") for h in range(2)] for n in ("local", "out"))
        s_got = [sp_.gathered(0), sp_.gathered(1)]
        block = sp_.block()

        @block.sync
        def _(sp):
            sp.dma_start(pay[:, :], tables[s][0, :, :]).then_inc(s_load, 16)
            sp.dma_start(node_i[:, :], node_rows[s]).then_inc(s_load, 16)
            sp.dma_start(nodes[:, :, :], nodes_in).then_inc(s_load, 16)
            for h in range(2):
                sp.sem_inc(s_out[h], 16)
            sp.wait_ge(s_load, 48)
            turns = turns_of(sp, node_i, s)
            with sp.Fori(0, turns) as t:
                for h in range(2):
                    sp.wait_ge(s_spread, 2 * t + (h + 1))
                    sp.dma_start(local[:, h, :], local_rows[s][bass.ds((2 * t + h) * GRP, GRP), :]
                                 .rearrange("i e -> (i e)").partition_broadcast(P)).then_inc(s_local[h], 16)
                    sp.wait_ge(s_got[h], 16 * GRP * t + 16 * GRP)
                    sp.dma_start(rows_out[bass.ds(2 * t + h, 1), :, :],
                                 got[:, h, :, :]).then_inc(s_out[h], 16)
            for h in range(2):
                sp.wait_ge(s_out[h], 16 * turns + 16)
                sp.sem_inc(s_turn)

        @block.gpsimd
        def _(pool):
            pool.wait_ge(s_load, 48)
            turns = turns_of(pool, node_i, s)
            with pool.Fori(0, turns) as t:
                for h in range(2):
                    pool.wait_ge(s_index, 2 * t + (h + 1))
                    pool.wait_ge(s_kept, 2 * t + (h + 1))
                    pool.wait_ge(s_out[h], 16 * t + 16)
                    pool.sem_inc(s_turn)
                    for i in range(GRP):
                        pool.indirect_dma_start(
                            out=got[:, h, i, :], out_offset=None, in_=table[:, :],
                            in_offset=bass.IndirectOffsetOnAxis(ap=index[:, h, i:i + 1], axis=0)).then_inc(s_got[h], 16)

        @block.scalar
        def _(act):
            act.wait_ge(s_load, 48)
            act.wait_ge(s_zero, 2)
            for h in range(2):
                nc.scalar.copy(index[:, h, :], pay[:, h * GRP:(h + 1) * GRP]).then_inc(s_index, 1)
            act.sem_inc(s_pfree, 2)
            turns = turns_of(act, node_i, s)
            with act.Fori(0, turns) as t:
                for h in range(2):
                    tiles = [act.value_load(node_i[0:1, bass.ds((2 * t + h) * GRP + 2 * j, 1)], min_val=0, max_val=NT - 1)
                             for j in range(PAIRS)]
                    act.wait_ge(s_sfree, 2 * t + (h + 1))
                    for j in range(PAIRS):
                        last = nc.scalar.copy(mine[:, h, j:j + 1, :], nodes[:, bass.ds(tiles[j], 1), :])
                    last.then_inc(s_mine, 1)
                    act.wait_ge(s_ard, 2 * t + (h + 1))
                    nc.scalar.copy(ard[:, bass.ds((2 * t + h) * GRP, GRP), :],
                                   p_ard[:, h, 0:GRP * 2 * HEADS].rearrange("p (i e) -> p i e", i=GRP)).then_inc(s_pfree, 1)
                    act.wait_ge(s_got[h], 16 * GRP * t + 16 * GRP)
                    nc.scalar.copy(index[:, h, :], pay[:, bass.ds((2 * t + h + 2) * GRP, GRP)]).then_inc(s_index, 1)

        @block.vector
        def _(dve):
            nc.vector.memset(al[:, :, :], 0.0).then_inc(s_zero, 1)
            nc.vector.memset(ard[:, :, :], 0.0).then_inc(s_zero, 1)
            dve.wait_ge(s_zero, 2)
            dve.sem_inc(s_spread, 2)
            dve.sem_inc(s_kept, 2)
            dve.wait_ge(s_load, 48)
            turns = turns_of(dve, node_i, s)
            with dve.Fori(0, turns) as t:
                for h in range(2):
                    dve.wait_ge(s_local[h], 16 * t + 16)
                    dve.wait_ge(s_sfree, 2 * t + (h + 1))
                    nc.vector.tensor_scalar(spread[:, h, :], local[:, h, :], c["part"][:, 0:1], None,
                                            ALU.is_equal).then_inc(s_spread, 1)
                    dve.wait_ge(s_got[h], 16 * GRP * t + 16 * GRP)
                    nc.vector.tensor_copy(al[:, bass.ds((2 * t + h) * GRP, GRP), :], got[:, h, :, width:]).then_inc(s_kept, 1)

        @block.tensor
        def _(pe):
            pe.sem_inc(s_sfree, 2)
            pe.wait_ge(s_load, 48)
            turns = turns_of(pe, node_i, s)
            with pe.Fori(0, turns) as t:
                for h in range(2):
                    pe.wait_ge(s_mine, 2 * t + (h + 1))
                    pe.wait_ge(s_pfree, 2 * t + (h + 1))
                    pe.wait_ge(s_spread, 2 * t + (h + 3))
                    for i in range(GRP):
                        last = nc.tensor.matmul(p_ard[:, h, i * 8:(i + 1) * 8], spread[:, h, i * P:(i + 1) * P],
                                                mine[:, h, i // 2, :], start=True, stop=True)
                    last.then_inc(s_ard, 1)
                    pe.wait_ge(s_ard, 2 * t + (h + 1))
                    pe.sem_inc(s_sfree)


def attend_weights(nc, c, name, s, tables, al, ard):
    ctx = ExitStack()
    with ctx:
        sp_ = Space(nc, ctx, name)
        ch = CHUNKS[s]
        cols = ch * P
        key = sp_.sb("key", [P, cols], I32)
        local = sp_.sb("local", [P, cols], I32)
        valid = sp_.sb("valid", [P, cols])
        gid = sp_.sb("gid", [P, cols])
        masked = sp_.sb("masked", [P, cols])
        line = [sp_.sb(f"line{i}", [P, cols]) for i in range(HEADS + 1)]
        begin, end = sp_.sb("begin", [P, cols]), sp_.sb("end", [P, cols])
        fwd, bwd = sp_.sb("fwd", [P, cols]), sp_.sb("bwd", [P, cols])
        ends = sp_.sb("ends", [P, 4, HEADS])
        row = sp_.sb("row", [HEADS, 4, P])
        same, whole, step = (sp_.sb(n, [HEADS, P + 1]) for n in ("same", "whole", "step"))
        chain = sp_.sb("chain", [HEADS, 2, P + 2])
        carry_row = sp_.sb("carry_row", [HEADS, 2, P])
        carry = sp_.sb("carry", [P, 2, HEADS])
        top = sp_.sb("top", [P, cols, HEADS])
        p_line = sp_.ps("p_line", [P, 3, 512])
        p_row = sp_.ps("p_row", [P, 512])
        s_load, s_dve, s_in, s_flip, s_copied, s_ends, s_row, s_carry, s_carried, s_exp = (
            sp_.sem(n) for n in ("load", "dve", "in", "flip", "copied", "ends", "row", "carry", "carried", "exp"))
        block = sp_.block()
        bank = lambda i: p_line[:, i // 3, i % 3 * P:(i % 3 + 1) * P]

        @block.sync
        def _(sp):
            sp.dma_start(key[:, :], tables[s][1, :, :]).then_inc(s_load, 16)
            sp.dma_start(local[:, :], tables[s][2, :, :]).then_inc(s_load, 16)

        @block.tensor
        def _(pe):
            for a in range(HEADS + 1):
                pe.wait_ge(s_in, a + 1)
                src = gid if a == 0 else masked
                for i in range(ch):
                    last = nc.tensor.transpose(bank(i), src[:, i::ch], c["ident"][:, :])
                last.then_inc(s_flip, 1)
            pe.wait_ge(s_ends, 1)
            for j in range(4):
                last = nc.tensor.transpose(p_row[0:HEADS, j * P:(j + 1) * P], ends[:, j, :], c["ident"][:, :])
            last.then_inc(s_row, 1)
            pe.wait_ge(s_carry, 1)
            for j in range(2):
                last = nc.tensor.transpose(p_row[:, j * HEADS:(j + 1) * HEADS], carry_row[:, j, :],
                                           c["ident"][0:HEADS, 0:HEADS])
            last.then_inc(s_carried, 1)
            for a in range(HEADS):
                pe.wait_ge(s_in, HEADS + 2 + a)
                for i in range(ch):
                    last = nc.tensor.transpose(bank(i), line[a + 1][:, i * P:(i + 1) * P], c["ident"][:, :])
                last.then_inc(s_flip, 1)

        @block.scalar
        def _(act):
            act.wait_ge(s_exp, 1)
            nc.scalar.activation(ard[:, :, :], ard[:, :, :], ACT.Exp).then_inc(s_exp, 1)

        @block.vector
        def _(dve):
            done = Chain(dve, s_dve)
            v = nc.vector
            dve.wait_ge(s_load, 32)
            loc, k = local[:, :].bitcast(F32), key[:, :].bitcast(F32)
            done(v.tensor_scalar(gid[:, :], loc, 0.0, None, ALU.is_ge))
            done(v.scalar_tensor_tensor(valid[:, :], loc, float(P), gid[:, :], ALU.is_lt, ALU.mult))
            done(v.scalar_tensor_tensor(gid[:, :], k, 1.0, valid[:, :], ALU.add, ALU.mult))
            dve.sem_inc(s_in)
            for a in range(HEADS + 1):
                if a:
                    done(v.tensor_tensor(masked[:, :], al[:, :, a - 1], valid[:, :], ALU.mult))
                    done(v.tensor_scalar(bwd[:, :], valid[:, :], BIG, -BIG, ALU.mult, ALU.add))
                    done(v.tensor_tensor(masked[:, :], masked[:, :], bwd[:, :], ALU.add))
                    dve.sem_inc(s_in)
                dve.wait_ge(s_flip, a + 1)
                full = ch // 3 * 3
                done.mark(v.tensor_copy(line[a][:, 0:full * P].rearrange("p (b e) -> p b e", b=ch // 3),
                                        p_line[:, 0:ch // 3, 0:3 * P]))
                if ch % 3:
                    done.mark(v.tensor_copy(line[a][:, full * P:], p_line[:, ch // 3, 0:ch % 3 * P]))
                done.wait()
            g = line[0]
            done(v.tensor_tensor(begin[:, 1:], g[:, 1:], g[:, 0:cols - 1], ALU.not_equal))
            done.mark(v.memset(end[:, cols - 1:], 0.0))
            done.mark(v.tensor_scalar(end[:, 0:cols - 1], begin[:, 1:], -BIG, None, ALU.mult))
            done.mark(v.memset(begin[:, 0:1], 0.0))
            done(v.tensor_scalar(begin[:, 1:], begin[:, 1:], -BIG, None, ALU.mult))
            for h in range(HEADS):
                done(v.tensor_tensor_scan(fwd[:, :], begin[:, :], line[h + 1][:, :], -BIG, ALU.add, ALU.max))
                done(v.tensor_tensor_scan(bwd[:, ::-1], end[:, ::-1], line[h + 1][:, ::-1], -BIG, ALU.add, ALU.max))
                done.mark(v.tensor_copy(ends[:, 0, h:h + 1], fwd[:, cols - 1:]))
                done.mark(v.tensor_copy(ends[:, 1, h:h + 1], bwd[:, 0:1]))
                done.mark(v.tensor_copy(ends[:, 2, h:h + 1], g[:, 0:1]))
                done(v.tensor_copy(ends[:, 3, h:h + 1], g[:, cols - 1:]))
            dve.sem_inc(s_ends)
            dve.wait_ge(s_row, 1)
            done.mark(v.tensor_copy(row[:, :, :], p_row[0:HEADS, :].rearrange("p (j q) -> p j q", j=4)))
            done.mark(v.memset(same[:, :], 0.0))
            done(v.memset(chain[:, :, :], -BIG))
            done.mark(v.tensor_tensor(same[:, 1:P], row[:, 2, 1:], row[:, 3, 0:P - 1], ALU.is_equal))
            done(v.tensor_tensor(whole[:, 0:P], row[:, 2, :], row[:, 3, :], ALU.is_equal))
            for j in range(2):
                nxt = same[:, 0:P] if j == 0 else same[:, 1:P + 1]
                done(v.tensor_tensor(step[:, 0:P], whole[:, 0:P], nxt, ALU.mult))
                done(v.tensor_scalar(step[:, 0:P], step[:, 0:P], BIG, -BIG, ALU.mult, ALU.add))
                if j == 0:
                    done(v.tensor_tensor_scan(chain[:, 0, 1:P + 1], step[:, 0:P], row[:, 0, :], -BIG, ALU.add, ALU.max))
                    prev = chain[:, 0, 0:P]
                else:
                    done(v.tensor_tensor_scan(chain[:, 1, 1:P + 1][:, ::-1], step[:, 0:P][:, ::-1], row[:, 1, ::-1], -BIG,
                                              ALU.add, ALU.max))
                    prev = chain[:, 1, 2:P + 2]
                done(v.tensor_scalar(step[:, 0:P], nxt, BIG, -BIG, ALU.mult, ALU.add))
                done(v.tensor_tensor(carry_row[:, j, :], prev, step[:, 0:P], ALU.add))
            dve.sem_inc(s_carry)
            dve.wait_ge(s_carried, 1)
            done(v.tensor_copy(carry[:, :, :], p_row[:, 0:2 * HEADS].rearrange("p (j h) -> p j h", j=2)))
            for h in range(HEADS):
                done.mark(v.tensor_tensor_scan(fwd[:, :], begin[:, :], line[h + 1][:, :], carry[:, 0, h:h + 1],
                                               ALU.add, ALU.max))
                done(v.tensor_tensor_scan(bwd[:, ::-1], end[:, ::-1], line[h + 1][:, ::-1], carry[:, 1, h:h + 1],
                                          ALU.add, ALU.max))
                done(v.tensor_tensor(line[h + 1][:, :], fwd[:, :], bwd[:, :], ALU.max))
                dve.sem_inc(s_in)
                dve.wait_ge(s_flip, HEADS + 2 + h)
                for i in range(ch):
                    done.mark(v.tensor_copy(top[:, i::ch, h], bank(i)))
                done.wait()
            d_score, s_score = ard[:, :, 0:HEADS], ard[:, :, HEADS:]
            done(v.tensor_tensor(top[:, :, :], top[:, :, :], s_score, ALU.max))
            done(v.tensor_tensor(top[:, :, :], top[:, :, :], d_score, ALU.add))
            done.mark(v.tensor_tensor(s_score, s_score, d_score, ALU.add))
            done(v.tensor_tensor(d_score, al[:, :, :], d_score, ALU.add))
            for x in (top[:, :, :], ard[:, :, :]):
                done.mark(v.scalar_tensor_tensor(x, x, 0.2, x, ALU.mult, ALU.max))
            done.wait()
            done.mark(v.tensor_tensor(d_score, d_score, top[:, :, :], ALU.subtract))
            done(v.tensor_tensor(s_score, s_score, top[:, :, :], ALU.subtract))
            done(v.tensor_tensor(ard[:, :, :], ard[:, :, :],
                                 valid[:, :, None].to_broadcast([P, cols, 2 * HEADS]), ALU.mult))
            dve.sem_inc(s_exp)
            dve.wait_ge(s_exp, 2)


def attend_sum(nc, c, name, s, width, table, bias, tables, node_rows, rows_in, weights, out, counts):
    ctx = ExitStack()
    with ctx:
        sp_ = Space(nc, ctx, name)
        cols = CHUNKS[s] * P
        w, m, ch = width + HEADS, width + 2 * HEADS + 1, width // HEADS
        local = sp_.sb("local", [P, cols], I32)
        node_i = sp_.sb("node_i", [1, cols + EXTRA], I32)
        got = sp_.sb("got", [P, 2, GRP, w])
        hot = sp_.sb("hot", [P, 2, GRP, P])
        msg = sp_.sb("msg", [P, 2, GRP, m])
        acc = sp_.sb("acc", [P, NTP, m])
        own = sp_.sb("own", [P, NTP, w])
        bias_b = sp_.sb("bias", [P, width])
        has, inv, cnt = (sp_.sb(n, [P, NTP]) for n in ("has", "inv", "cnt"))
        w_own, den = sp_.sb("w_own", [P, NTP, HEADS]), sp_.sb("den", [P, NTP, HEADS])
        p_sum = sp_.ps("p_sum", [P, 2 * PAIRS, 512])
        s_load, s_acc, s_mfree, s_hot, s_side, s_sum, s_fin, s_out, s_tail = (
            sp_.sem(n) for n in ("load", "acc", "mfree", "hot", "side", "sum", "fin", "out", "tail"))
        s_got = [sp_.sem("got0"), sp_.sem("got1")]
        block = sp_.block()

        @block.sync
        def _(sp):
            sp.dma_start(local[:, :], tables[s][2, :, :]).then_inc(s_load, 16)
            sp.dma_start(node_i[:, :], node_rows[s]).then_inc(s_load, 16)
            sp.dma_start(own[:, :, :], table.rearrange("(t p) c -> p t c", p=P)).then_inc(s_load, 16)
            sp.dma_start(bias_b[:, :], bias.partition_broadcast(P)).then_inc(s_load, 16)
            sp.wait_ge(s_load, 64)
            turns = turns_of(sp, node_i, s)
            with sp.Fori(0, turns) as t:
                for h in range(2):
                    sp.wait_ge(s_hot, 2 * t + (h + 1))
                    sp.dma_start(got[:, h, :, :], rows_in[bass.ds(2 * t + h, 1), :, :]).then_inc(s_got[h], 16)
            sp.wait_ge(s_out, 1)
            sp.dma_start(out.rearrange("(t p) c -> p t c", p=P), acc[:, :, 0:width]).then_inc(s_fin, 16)
            sp.dma_start(counts, cnt[:, :]).then_inc(s_fin, 16)
            sp.wait_ge(s_fin, 32)

        @block.scalar
        def _(act):
            act.wait_ge(s_load, 64)
            turns = turns_of(act, node_i, s)
            with act.Fori(0, turns) as t:
                for h in range(2):
                    act.wait_ge(s_mfree, 2 * t + (h + 1))
                    nc.scalar.copy(msg[:, h, :, width:width + 2 * HEADS],
                                   weights[:, bass.ds((2 * t + h) * GRP, GRP), :]).then_inc(s_side, 1)

        @block.vector
        def _(dve):
            v = nc.vector
            done = Chain(dve, s_acc)
            done.mark(v.memset(acc[:, :, :], 0.0))
            done(v.memset(msg[:, :, :, :], 1.0))
            dve.sem_inc(s_mfree, 2)
            dve.sem_inc(s_hot, 2)
            dve.wait_ge(s_load, 64)
            loc = local[:, :].bitcast(F32)

            def messages(t, h):
                at = bass.ds((2 * t + h) * GRP, GRP)
                dve.wait_ge(s_mfree, 2 * t + (h + 1))
                v.tensor_tensor(hot[:, h, :, :], c["ramp"][:, None, 0:P].to_broadcast([P, GRP, P]),
                                loc[:, at][:, :, None].to_broadcast([P, GRP, P]), ALU.is_equal)
                dve.wait_ge(s_got[h], 16 * t + 16)
                for e in range(HEADS):
                    last = v.tensor_tensor(msg[:, h, :, e * ch:(e + 1) * ch], got[:, h, :, e * ch:(e + 1) * ch],
                                           weights[:, at, e:e + 1].to_broadcast([P, GRP, ch]), ALU.mult)
                last.then_inc(s_hot, 1)

            def add(t, h):
                tiles = [dve.value_load(node_i[0:1, bass.ds((2 * t + h) * GRP + 2 * j, 1)], min_val=0, max_val=NT - 1)
                         for j in range(PAIRS)]
                for j in range(PAIRS):
                    dve.wait_ge(s_sum, (2 * t + h) * PAIRS + (j + 1))
                    to = acc[:, bass.ds(tiles[j], 1), :]
                    done(v.tensor_tensor(to, to, p_sum[:, h * PAIRS + j:h * PAIRS + j + 1, 0:m], ALU.add))
                dve.sem_inc(s_mfree)

            messages(0, 0)
            messages(0, 1)
            last_turn = turns_of(dve, node_i, s, LAST_TURN)
            with dve.Fori(0, last_turn) as t:
                done.enter(t, 2 * PAIRS)
                for h in range(2):
                    add(t, h)
                    messages(t + 1, h)
            done.enter_last(last_turn)
            for h in range(2):
                add(last_turn, h)
            done = Chain(dve, s_tail)
            done(v.tensor_copy(cnt[:, :], acc[:, :, m - 1]))
            done.mark(v.tensor_scalar(has[:, :], cnt[:, :], 1.0, None, ALU.min))
            done(v.tensor_scalar(inv[:, :], cnt[:, :], 1.0, None, ALU.max))
            done.mark(v.reciprocal(inv[:, :], inv[:, :]))
            done(v.tensor_scalar(has[:, :], has[:, :], -1.0, 1.0, ALU.mult, ALU.add))
            done(v.tensor_tensor(w_own[:, :, :], acc[:, :, width + HEADS:width + 2 * HEADS],
                                 inv[:, :, None].to_broadcast([P, NTP, HEADS]), ALU.mult))
            done(v.tensor_tensor(w_own[:, :, :], w_own[:, :, :], has[:, :, None].to_broadcast([P, NTP, HEADS]), ALU.add))
            done(v.scalar_tensor_tensor(den[:, :, :], w_own[:, :, :], 1e-16, acc[:, :, width:width + HEADS],
                                        ALU.add, ALU.add))
            done(v.reciprocal(den[:, :, :], den[:, :, :]))
            for e in range(HEADS):
                o, a = own[:, :, e * ch:(e + 1) * ch], acc[:, :, e * ch:(e + 1) * ch]
                done(v.tensor_tensor(o, o, w_own[:, :, e:e + 1].to_broadcast([P, NTP, ch]), ALU.mult))
                done(v.tensor_tensor(a, a, o, ALU.add))
                done(v.tensor_tensor(a, a, den[:, :, e:e + 1].to_broadcast([P, NTP, ch]), ALU.mult))
            done(v.tensor_tensor(acc[:, :, 0:width], acc[:, :, 0:width],
                                 bias_b[:, None, :].to_broadcast([P, NTP, width]), ALU.add))
            dve.sem_inc(s_out)

        @block.tensor
        def _(pe):
            pe.wait_ge(s_load, 64)
            turns = turns_of(pe, node_i, s)
            with pe.Fori(0, turns) as t:
                for h in range(2):
                    pe.wait_ge(s_hot, 2 * t + (h + 3))
                    pe.wait_ge(s_side, 2 * t + (h + 1))
                    for j in range(PAIRS):
                        for i in (2 * j, 2 * j + 1):
                            last = nc.tensor.matmul(p_sum[:, h * PAIRS + j, 0:m], hot[:, h, i, :], msg[:, h, i, :],
                                                    start=(i == 2 * j), stop=(i > 2 * j))
                        last.then_inc(s_sum, 1)


def attention(nc, c, name, s, width, table, nodes_in, bias, tables, local_rows, node_rows, kept, out, counts):
    ctx = ExitStack()
    with ctx:
        sp_ = Space(nc, ctx, name)
        ard = sp_.sb("ard", [P, CHUNKS[s] * P, 2 * HEADS])
        inner = ExitStack()
        with inner:
            al = Space(nc, inner, name).sb("al", [P, CHUNKS[s] * P, HEADS])
            attend_gather(nc, c, name + "g", s, width, table, nodes_in, tables, local_rows, node_rows, kept, al, ard)
            attend_weights(nc, c, name + "w", s, tables, al, ard)
        attend_sum(nc, c, name + "s", s, width, table, bias, tables, node_rows, kept, ard, out, counts)


def pad_rows(nc, x, x_out):
    ctx = ExitStack()
    with ctx:
        sp_ = Space(nc, ctx, "pad")
        rows = sp_.sb("rows", [P, NTP, D])
        s_zero, s_load, s_out = (sp_.sem(n) for n in ("zero", "load", "out"))
        whole = N // P
        block = sp_.block()

        @block.vector
        def _(dve):
            nc.vector.memset(rows[:, whole:, :], 0.0).then_inc(s_zero, 1)

        @block.sync
        def _(sp):
            sp.dma_start(rows[:, 0:whole, :], x[0:whole * P, :].rearrange("(t p) d -> p t d", p=P)).then_inc(s_load, 16)
            sp.wait_ge(s_zero, 1)
            sp.dma_start(rows[0:N - whole * P, whole, :], x[whole * P:N, :]).then_inc(s_load, 16)
            sp.wait_ge(s_load, 32)
            sp.dma_start(x_out.rearrange("(t p) d -> p t d", p=P), rows[:, :, :]).then_inc(s_out, 16)
            sp.wait_ge(s_out, 16)


def rows_product(nc, c, name, rows_in, w_in, out, tiles, bn=None, x_in=None):
    ctx = ExitStack()
    with ctx:
        sp_ = Space(nc, ctx, name)
        part = D // len(rows_in)
        w = sp_.sb("w", [P, 2, D])
        rows = sp_.sb("rows", [P, 2, D])
        x = sp_.sb("x", [P, 2, D])
        rows_t = sp_.sb("rows_t", [P, 2, 2, P])
        y = sp_.sb("y", [P, 2, D])
        par = sp_.sb("par", [P, 5, D])
        scale, shift = sp_.sb("scale", [P, D]), sp_.sb("shift", [P, D])
        p_t = sp_.ps("p_t", [P, 2, 512])
        p_y = sp_.ps("p_y", [P, 2, 512])
        s_w, s_dve, s_std, s_t, s_rt, s_m, s_y, s_x = (
            sp_.sem(n) for n in ("w", "dve", "std", "t", "rt", "m", "y", "x"))
        s_in, s_out = ([sp_.sem(f"{n}{h}") for h in range(2)] for n in ("in", "out"))
        n_in = 16 * (len(rows_in) + (bn is not None))
        n_w = 16 * (2 + 5 * (bn is not None))
        block = sp_.block()

        @block.sync
        def _(sp):
            for k in range(2):
                sp.dma_start(w[:, k, :], w_in[k * P:(k + 1) * P, :]).then_inc(s_w, 16)
            if bn is not None:
                for i, a in enumerate(bn):
                    sp.dma_start(par[:, i, :], a.partition_broadcast(P)).then_inc(s_w, 16)
            with sp.Fori(0, tiles // 2) as t:
                for h in range(2):
                    at = bass.ds((2 * t + h) * P, P)
                    sp.wait_ge(s_t, 2 * t + (h + 1))
                    if bn is not None:
                        sp.wait_ge(s_x, 2 * t + (h + 1))
                        sp.dma_start(x[:, h, :], x_in[at, :]).then_inc(s_in[h], 16)
                    for i, a in enumerate(rows_in):
                        sp.dma_start(rows[:, h, i * part:(i + 1) * part], a[at, :]).then_inc(s_in[h], 16)

        @block.tensor
        def _(pe):
            pe.sem_inc(s_t, 2)
            pe.wait_ge(s_w, n_w)
            with pe.Fori(0, tiles // 2) as t:
                for h in range(2):
                    pe.wait_ge(s_in[h], n_in * t + n_in)
                    for k in range(2):
                        last = nc.tensor.transpose(p_t[:, h, k * P:(k + 1) * P], rows[:, h, k * P:(k + 1) * P],
                                                   c["ident"][:, :])
                    last.then_inc(s_t, 1)
                    pe.wait_ge(s_rt, 2 * t + (h + 1))
                    pe.wait_ge(s_y, 2 * t + (h + 1))
                    for k in range(2):
                        last = nc.tensor.matmul(p_y[:, h, 0:D], rows_t[:, h, k, :], w[:, k, :],
                                                start=(k == 0), stop=(k == 1))
                    last.then_inc(s_m, 1)

        @block.scalar
        def _(act):
            if bn is not None:
                act.wait_ge(s_dve, 1)
                nc.scalar.activation(scale[:, :], shift[:, :], ACT.Sqrt).then_inc(s_std, 1)
            for h in range(2):
                act.sem_inc(s_out[h], 16)
            with act.Fori(0, tiles // 2) as t:
                for h in range(2):
                    act.wait_ge(s_t, 2 * t + (h + 3))
                    nc.scalar.copy(rows_t[:, h, :, :], p_t[:, h, 0:D].rearrange("p (k e) -> p k e", k=2)).then_inc(s_rt, 1)
                    act.wait_ge(s_y, 2 * t + (h + 3))
                    act.dma_start(out[bass.ds((2 * t + h) * P, P), :], y[:, h, :]).then_inc(s_out[h], 16)
            for h in range(2):
                act.wait_ge(s_out[h], 16 * (tiles // 2) + 16)

        @block.vector
        def _(dve):
            v = nc.vector
            done = Chain(dve, s_dve)
            dve.sem_inc(s_y, 2)
            dve.sem_inc(s_x, 2)
            if bn is not None:
                b_fuse, gamma, beta, mean, var = (par[:, i, :] for i in range(5))
                dve.wait_ge(s_w, n_w)
                done(v.tensor_scalar(shift[:, :], var, EPS, None, ALU.add))
                dve.wait_ge(s_std, 1)
                done(v.reciprocal(scale[:, :], scale[:, :]))
                done.mark(v.tensor_tensor(shift[:, :], b_fuse, mean, ALU.subtract))
                done(v.tensor_tensor(scale[:, :], scale[:, :], gamma, ALU.mult))
                done(v.tensor_tensor(shift[:, :], shift[:, :], scale[:, :], ALU.mult))
                done(v.tensor_tensor(shift[:, :], shift[:, :], beta, ALU.add))
            with dve.Fori(0, tiles // 2) as t:
                done.enter(t, 4 if bn is not None else 0)
                for h in range(2):
                    dve.wait_ge(s_m, 2 * t + (h + 1))
                    dve.wait_ge(s_out[h], 16 * t + 16)
                    if bn is None:
                        v.tensor_copy(y[:, h, :], p_y[:, h, 0:D]).then_inc(s_y, 1)
                        continue
                    done(v.tensor_tensor(y[:, h, :], p_y[:, h, 0:D], scale[:, :], ALU.mult))
                    done(v.tensor_tensor(y[:, h, :], y[:, h, :], shift[:, :], ALU.add))
                    v.scalar_tensor_tensor(y[:, h, :], y[:, h, :], 0.0, x[:, h, :], ALU.max, ALU.add).then_inc(s_y, 1)
                    dve.wait_ge(s_y, 2 * t + (h + 3))
                    dve.sem_inc(s_x)
            if bn is not None:
                done.leave(tiles // 2)


def choose_experts(nc, c, agg, gamma, beta, gates_out):
    ctx = ExitStack()
    with ctx:
        sp_ = Space(nc, ctx, "gates")
        w = HEADS * NEXP
        a = sp_.sb("a", [P, NTP, w])
        sq = sp_.sb("sq", [P, NTP, w])
        par = sp_.sb("par", [P, 2, w])
        mean, var = sp_.sb("mean", [P, NTP]), sp_.sb("var", [P, NTP])
        score, rank, gate = (sp_.sb(n, [P, NTP, NEXP]) for n in ("score", "rank", "gate"))
        cmp, top, total = (sp_.sb(n, [P, NTP]) for n in ("cmp", "top", "total"))
        s_load, s_dve, s_act, s_var, s_exp, s_out, s_done = (
            sp_.sem(n) for n in ("load", "dve", "act", "var", "exp", "out", "done"))
        block = sp_.block()

        @block.sync
        def _(sp):
            sp.dma_start(a[:, :, :], agg.rearrange("(t p) c -> p t c", p=P)).then_inc(s_load, 16)
            sp.dma_start(par[:, 0, :], gamma.partition_broadcast(P)).then_inc(s_load, 16)
            sp.dma_start(par[:, 1, :], beta.partition_broadcast(P)).then_inc(s_load, 16)
            sp.wait_ge(s_done, 1)
            sp.dma_start(gates_out, gate[:, :, :]).then_inc(s_out, 16)
            sp.wait_ge(s_out, 16)

        @block.scalar
        def _(act):
            act.wait_ge(s_var, 1)
            nc.scalar.activation(var[:, :], var[:, :], ACT.Sqrt).then_inc(s_act, 1)
            act.wait_ge(s_exp, 1)
            nc.scalar.activation(gate[:, :, :], score[:, :, :], ACT.Exp).then_inc(s_act, 1)

        @block.vector
        def _(dve):
            v = nc.vector
            done = Chain(dve, s_dve)
            wide = lambda m, n: m[:, :, None].to_broadcast([P, NTP, n])
            dve.wait_ge(s_load, 48)
            done(v.tensor_reduce(mean[:, :], a[:, :, :], axis=AX.X, op=ALU.add))
            done(v.tensor_scalar(mean[:, :], mean[:, :], 1.0 / w, None, ALU.mult))
            done(v.tensor_tensor(a[:, :, :], a[:, :, :], wide(mean, w), ALU.subtract))
            done(v.tensor_tensor(sq[:, :, :], a[:, :, :], a[:, :, :], ALU.mult))
            done(v.tensor_reduce(var[:, :], sq[:, :, :], axis=AX.X, op=ALU.add))
            done(v.tensor_scalar(var[:, :], var[:, :], 1.0 / w, EPS, ALU.mult, ALU.add))
            dve.sem_inc(s_var)
            dve.wait_ge(s_act, 1)
            done(v.reciprocal(var[:, :], var[:, :]))
            done(v.tensor_tensor(a[:, :, :], a[:, :, :], wide(var, w), ALU.mult))
            done(v.tensor_tensor(a[:, :, :], a[:, :, :], par[:, 0:1, :].to_broadcast([P, NTP, w]), ALU.mult))
            done(v.tensor_tensor(a[:, :, :], a[:, :, :], par[:, 1:2, :].to_broadcast([P, NTP, w]), ALU.add))
            done(v.tensor_tensor(score[:, :, :], a[:, :, 0:NEXP], a[:, :, NEXP:2 * NEXP], ALU.add))
            for h in range(2, HEADS):
                done(v.tensor_tensor(score[:, :, :], score[:, :, :], a[:, :, h * NEXP:(h + 1) * NEXP], ALU.add))
            done(v.tensor_scalar(score[:, :, :], score[:, :, :], 1.0 / HEADS, None, ALU.mult))
            done(v.memset(rank[:, :, :], 0.0))
            for e in range(NEXP):
                for j in range(NEXP):
                    if j != e:
                        done(v.tensor_tensor(cmp[:, :], score[:, :, j], score[:, :, e], ALU.is_ge if j < e else ALU.is_gt))
                        done(v.tensor_tensor(rank[:, :, e], rank[:, :, e], cmp[:, :], ALU.add))
            done(v.tensor_reduce(top[:, :], score[:, :, :], axis=AX.X, op=ALU.max))
            done(v.tensor_tensor(score[:, :, :], score[:, :, :], wide(top, NEXP), ALU.subtract))
            dve.sem_inc(s_exp)
            dve.wait_ge(s_act, 2)
            done(v.scalar_tensor_tensor(gate[:, :, :], rank[:, :, :], 2.0, gate[:, :, :], ALU.is_lt, ALU.mult))
            done(v.tensor_reduce(total[:, :], gate[:, :, :], axis=AX.X, op=ALU.add))
            done(v.reciprocal(total[:, :], total[:, :]))
            done(v.tensor_tensor(gate[:, :, :], gate[:, :, :], wide(total, NEXP), ALU.mult))
            dve.sem_inc(s_done)


def gated_experts(nc, c, xt, x_in, gates_in, w1_in, b1_in, w2_in, b2_in, out):
    ctx = ExitStack()
    with ctx:
        sp_ = Space(nc, ctx, "ffn")
        FB = FH // P
        w1 = sp_.sb("w1", [P, 2, NEXP, FH])
        w2 = sp_.sb("w2", [P, NEXP, FB, D])
        b1 = sp_.sb("b1", [P, NEXP, FB])
        b2 = sp_.sb("b2", [1, NEXP, D])
        gates = sp_.sb("gates", [P, NTP, NEXP])
        y = sp_.sb("y", [P, 2, 2, D])
        hid = sp_.sb("hid", [P, FB, 2 * P])
        p_h = sp_.ps("p_h", [P, FB, 512])
        p_y = sp_.ps("p_y", [P, 2, 512])
        s_w, s_h, s_a, s_y, s_acc = (sp_.sem(n) for n in ("w", "h", "a", "y", "acc"))
        s_in, s_out = ([sp_.sem(f"{n}{h}") for h in range(2)] for n in ("in", "out"))
        turns = NTP // 2
        n_w = 16 * (2 * NEXP + NEXP + 3)
        block = sp_.block()
        def each_turn(eng, body):
            with eng.Fori(0, turns // 2) as t:
                for h in range(2):
                    body(2 * t + h, t, h)
            body(turns - 1, turns // 2, 0)

        @block.sync
        def _(sp):
            with nc.allow_non_contiguous_dma(reason="a bias per partition"):
                for e in range(NEXP):
                    for k in range(2):
                        sp.dma_start(w1[:, k, e, :], w1_in[e, k * P:(k + 1) * P, :]).then_inc(s_w, 16)
                    sp.dma_start(w2[:, e, :, :], w2_in[e, :, :].rearrange("(f p) d -> p f d", p=P)).then_inc(s_w, 16)
                sp.dma_start(b1[:, :, :].rearrange("p e f -> p (e f)"),
                             b1_in.rearrange("e (f p) -> p (e f)", p=P)).then_inc(s_w, 16)
            sp.dma_start(b2[:, :, :], b2_in.rearrange("(a e) d -> a e d", a=1)).then_inc(s_w, 16)
            sp.dma_start(gates[:, :, :], gates_in).then_inc(s_w, 16)
            for h in range(2):
                sp.sem_inc(s_out[h], 16)

            def body(n, t, h):
                sp.wait_ge(s_out[h], 16 * t + 16)
                sp.dma_start(y[:, h, :, :], x_in[bass.ds(n * 2 * P, 2 * P), :].rearrange("(i p) d -> p i d", p=P)).then_inc(s_in[h], 16)
            each_turn(sp, body)

        @block.tensor
        def _(pe):
            pe.wait_ge(s_w, n_w)

            def body(n, t, h):
                for e in range(NEXP):
                    for f in range(FB):
                        pe.wait_ge(s_a, (NEXP * FB) * n + (e * FB + f + 1))
                        for k in range(2):
                            last = nc.tensor.matmul(p_h[:, f, 0:2 * P], w1[:, k, e, f * P:(f + 1) * P],
                                                    xt[:, k, bass.ds(n * 2 * P, 2 * P)], start=(k == 0), stop=(k == 1))
                        last.then_inc(s_h, 1)
                    for i in range(2):
                        pe.wait_ge(s_acc, (NEXP * 2) * n + (2 * e + i + 1))
                        nc.tensor.matmul(p_y[:, i, 0:D], c["ones"][0:1, :], b2[0:1, e, :], start=True, stop=False)
                        for f in range(FB):
                            if i == 0:
                                pe.wait_ge(s_a, (NEXP * FB) * n + (e * FB + f + 1 + FB))
                            last = nc.tensor.matmul(p_y[:, i, 0:D], hid[:, f, i * P:(i + 1) * P], w2[:, e, f, :],
                                                    start=False, stop=(f == FB - 1))
                        last.then_inc(s_y, 1)
            each_turn(pe, body)

        @block.scalar
        def _(act):
            act.sem_inc(s_a, FB)
            act.wait_ge(s_w, n_w)

            def body(n, t, h):
                for e in range(NEXP):
                    for f in range(FB):
                        act.wait_ge(s_h, (NEXP * FB) * n + (e * FB + f + 1))
                        nc.scalar.activation(hid[:, f, :], p_h[:, f, 0:2 * P], ACT.Gelu, bias=b1[:, e, f:f + 1]).then_inc(s_a, 1)
                act.wait_ge(s_acc, (NEXP * 2) * n + (NEXP * 2 + 2))
                act.dma_start(out[bass.ds(n * 2 * P, 2 * P), :].rearrange("(i p) d -> p i d", p=P),
                              y[:, h, :, :]).then_inc(s_out[h], 16)
            each_turn(act, body)
            act.wait_ge(s_out[0], 16 * (turns // 2 + 1) + 16)
            act.wait_ge(s_out[1], 16 * (turns // 2) + 16)

        @block.vector
        def _(dve):
            dve.sem_inc(s_acc, 2)
            dve.wait_ge(s_w, n_w)

            def body(n, t, h):
                dve.wait_ge(s_in[h], 16 * t + 16)
                for e in range(NEXP):
                    for i in range(2):
                        dve.wait_ge(s_y, (NEXP * 2) * n + (2 * e + i + 1))
                        if e:
                            dve.wait_ge(s_acc, (NEXP * 2) * n + (2 * e + i + 1))
                        nc.vector.scalar_tensor_tensor(y[:, h, i, :], p_y[:, i, 0:D], gates[:, bass.ds(2 * n + i, 1), e],
                                                       y[:, h, i, :], ALU.mult, ALU.add).then_inc(s_acc, 1)
            each_turn(dve, body)


def hyper_sum(nc, c, name, s, table, tables, node_rows, out, counts_in, relu, x_in=None):
    ctx = ExitStack()
    with ctx:
        sp_ = Space(nc, ctx, name)
        back = s == 3
        cols, which = CHUNKS[s] * P, TURNS_ALL if back else TURNS_HYPER
        tiles_out, m = (NTP, D + 1) if back else (NHT, D)
        pay = sp_.sb("pay", [P, cols], I32)
        local = sp_.sb("local", [P, cols], I32)
        node_i = sp_.sb("node_i", [1, cols + EXTRA], I32)
        cnt, rest = sp_.sb("cnt", [P, NTP]), sp_.sb("rest", [P, NTP])
        index = sp_.sb("index", [P, 2, GRP], I32)
        got = sp_.sb("got", [P, 2, GRP, D])
        hot = sp_.sb("hot", [P, 2, GRP, P])
        acc = sp_.sb("acc", [P, NTP, m])
        x = sp_.sb("x", [P, NTP, D]) if x_in is not None else None
        last_row = sp_.sb("last_row", [P, D])
        p_sum = sp_.ps("p_sum", [P, 2 * PAIRS, 512])
        s_load, s_clamp, s_index, s_turn, s_hot, s_sum, s_acc, s_tail, s_out, s_fin, s_x = (
            sp_.sem(n) for n in ("load", "clamp", "index", "turn", "hot", "sum", "acc", "tail", "out", "fin", "x"))
        s_got = [sp_.gathered(0), sp_.gathered(1)]
        LOADS = 16 * 5
        block = sp_.block()

        @block.sync
        def _(sp):
            sp.dma_start(pay[:, :], tables[s][0, :, :]).then_inc(s_load, 16)
            sp.dma_start(local[:, :], tables[s][2, :, :]).then_inc(s_load, 16)
            sp.dma_start(node_i[:, :], node_rows[s]).then_inc(s_load, 16)
            sp.dma_start(cnt[:, :], counts_in).then_inc(s_load, 16)
            sp.dma_start(last_row[:, :], table[NHYP - 1, :].partition_broadcast(P)).then_inc(s_load, 16)
            if x_in is not None:
                sp.dma_start(x[:, :, :], x_in.rearrange("(t p) d -> p t d", p=P)).then_inc(s_x, 16)
            sp.wait_ge(s_out, 1)
            sp.dma_start(out.rearrange("(t p) d -> p t d", p=P), acc[:, 0:tiles_out, 0:D]).then_inc(s_fin, 16)
            sp.wait_ge(s_fin, 16)

        @block.gpsimd
        def _(pool):
            pool.wait_ge(s_load, LOADS)
            turns = turns_of(pool, node_i, s, which)
            with pool.Fori(0, turns) as t:
                for h in range(2):
                    pool.wait_ge(s_index, 2 * t + (h + 1))
                    pool.wait_ge(s_sum, (2 * t + h) * PAIRS + PAIRS)
                    pool.sem_inc(s_turn)
                    for i in range(GRP):
                        pool.indirect_dma_start(
                            out=got[:, h, i, :], out_offset=None, in_=table[:, :],
                            in_offset=bass.IndirectOffsetOnAxis(ap=index[:, h, i:i + 1], axis=0)).then_inc(s_got[h], 16)

        @block.scalar
        def _(act):
            act.wait_ge(s_load, LOADS)
            act.wait_ge(s_clamp, 1)
            for h in range(2):
                nc.scalar.copy(index[:, h, :], pay[:, h * GRP:(h + 1) * GRP]).then_inc(s_index, 1)
            turns = turns_of(act, node_i, s, which)
            with act.Fori(0, turns) as t:
                for h in range(2):
                    act.wait_ge(s_got[h], 16 * GRP * t + 16 * GRP)
                    nc.scalar.copy(index[:, h, :], pay[:, bass.ds((2 * t + h + 2) * GRP, GRP)]).then_inc(s_index, 1)

        @block.tensor
        def _(pe):
            pe.sem_inc(s_sum, 2 * PAIRS)
            pe.wait_ge(s_load, LOADS)
            turns = turns_of(pe, node_i, s, which)
            with pe.Fori(0, turns) as t:
                for h in range(2):
                    pe.wait_ge(s_hot, 2 * t + (h + 1))
                    pe.wait_ge(s_got[h], 16 * GRP * t + 16 * GRP)
                    for j in range(PAIRS):
                        at = h * PAIRS + j
                        for i in (2 * j, 2 * j + 1):
                            last = nc.tensor.matmul(p_sum[:, at, 0:D], hot[:, h, i, :], got[:, h, i, :],
                                                    start=(i == 2 * j), stop=(i > 2 * j))
                        for i in (2 * j, 2 * j + 1) if back else ():
                            last = nc.tensor.matmul(p_sum[:, at, D:D + 1], hot[:, h, i, :], c["ones"][:, 0:1],
                                                    start=(i == 2 * j), stop=(i > 2 * j))
                        last.then_inc(s_sum, 1)

        @block.vector
        def _(dve):
            v = nc.vector
            done = Chain(dve, s_acc)
            done(v.memset(acc[:, :, :], 0.0))
            dve.wait_ge(s_load, LOADS)
            done(v.tensor_scalar_min(pay[:, :], pay[:, :], float(NHYP - 1 if back else N - 1)))
            dve.sem_inc(s_clamp)
            loc = local[:, :].bitcast(F32)
            turns = turns_of(dve, node_i, s, which)

            def one_hot(t, h):
                at = bass.ds((2 * t + h) * GRP, GRP)
                v.tensor_tensor(hot[:, h, :, :], c["ramp"][:, None, 0:P].to_broadcast([P, GRP, P]),
                                loc[:, at][:, :, None].to_broadcast([P, GRP, P]), ALU.is_equal).then_inc(s_hot, 1)

            one_hot(0, 0)
            one_hot(0, 1)
            with dve.Fori(0, turns) as t:
                done.enter(t, 2 * PAIRS)
                for h in range(2):
                    tiles = [dve.value_load(node_i[0:1, bass.ds((2 * t + h) * GRP + 2 * j, 1)], min_val=0, max_val=NT - 1)
                             for j in range(PAIRS)]
                    for j in range(PAIRS):
                        dve.wait_ge(s_sum, (2 * t + h) * PAIRS + (j + 1 + 2 * PAIRS))
                        to = acc[:, bass.ds(tiles[j], 1), :]
                        done(v.tensor_tensor(to, to, p_sum[:, h * PAIRS + j:h * PAIRS + j + 1, 0:m], ALU.add))
                    one_hot(t + 1, h)
            done = Chain(dve, s_tail)
            if back:
                done(v.tensor_tensor(rest[:, :], cnt[:, :], acc[:, :, D], ALU.subtract))
                for b in range(NTP):
                    done.mark(v.scalar_tensor_tensor(acc[:, b, 0:D], last_row[:, :], rest[:, b:b + 1], acc[:, b, 0:D],
                                                     ALU.mult, ALU.add))
                done.wait()
            done(v.tensor_scalar(cnt[:, :], cnt[:, :], 1.0, None, ALU.max))
            done(v.reciprocal(cnt[:, :], cnt[:, :]))
            a = acc[:, 0:tiles_out, 0:D]
            done(v.tensor_tensor(a, a, cnt[:, 0:tiles_out, None].to_broadcast([P, tiles_out, D]), ALU.mult))
            if relu:
                done(v.tensor_scalar(a, a, 0.0, None, ALU.max))
            if x_in is not None:
                dve.wait_ge(s_x, 16)
                done(v.tensor_tensor(a, a, x[:, :, :], ALU.add))
            dve.sem_inc(s_out)


def route(nc, c, xt, rows_in, gate_w, gate_b, slots, coef_out, index_out):
    ctx = ExitStack()
    with ctx:
        sp_ = Space(nc, ctx, "route")
        M = MEXP
        gw = sp_.sb("gw", [P, 2, M])
        gb = sp_.sb("gb", [M, 1])
        zero = sp_.sb("zero", [P, 4096])
        rows = sp_.sb("rows", [P, NTP, D])
        logit_t = sp_.sb("logit_t", [M, NPAD])
        prob, one, tmp, place = (sp_.sb(n, [P, NTP, M]) for n in ("prob", "one", "tmp", "place"))
        top, total, taken, pos, expert, token, kept, coef, slot = (
            sp_.sb(n, [P, NTP]) for n in ("top", "total", "taken", "pos", "expert", "token", "kept", "coef", "slot"))
        before = sp_.sb("before", [P, P])
        per_tile, ahead = sp_.sb("per_tile", [P, NTP, M]), sp_.sb("ahead", [P, M, NTP + 1])
        index = sp_.sb("index", [P, NTP], I32)
        back = sp_.sb("back", [P, NTP], I32)
        p_log = sp_.ps("p_log", [P, 2, 512])
        p_tok = sp_.ps("p_tok", [P, 512])
        p_pre = sp_.ps("p_pre", [P, 2, 512])
        s_load, s_zero, s_fill, s_dve, s_log, s_logged, s_tok, s_exp, s_one, s_pre, s_index, s_done, s_out, s_tri = (
            sp_.sem(n) for n in ("load", "zero", "fill", "dve", "log", "logged", "tok", "exp", "one", "pre", "index",
                                 "done", "out", "tri"))
        s_rows, s_sent = sp_.sem("rows_in"), sp_.gathered(0)
        pieces = [(a, min(a + 512, NPAD)) for a in range(0, NPAD, 512)]
        block = sp_.block()

        @block.sync
        def _(sp):
            for k in range(2):
                sp.dma_start(gw[:, k, :], gate_w[k * P:(k + 1) * P, :]).then_inc(s_load, 16)
            sp.dma_start(gb[:, :], gate_b.rearrange("(e a) -> e a", a=1)).then_inc(s_load, 16)
            sp.wait_ge(s_zero, 1)
            n = MEXP * CAPP * D // P // 4096
            flat = slots.rearrange("(n p r) d -> n p (r d)", n=n, p=P)
            for i in range(n):
                sp.dma_start(flat[i, :, :], zero[:, :]).then_inc(s_fill, 16)
            sp.dma_start(rows[:, :, :], rows_in.rearrange("(t p) d -> p t d", p=P)).then_inc(s_rows, 16)
            sp.wait_ge(s_done, 1)
            sp.dma_start(coef_out, coef[:, :]).then_inc(s_out, 16)
            sp.dma_start(index_out, back[:, :]).then_inc(s_out, 16)
            sp.wait_ge(s_out, 32)
            sp.wait_ge(s_fill, 16 * n)

        @block.gpsimd
        def _(pool):
            nc.gpsimd.memset(zero[:, :], 0.0).then_inc(s_zero, 1)
            pool.wait_ge(s_zero, 1)
            nc.gpsimd.affine_select(out=before[:, :], in_=c["ones"][:, :], compare_op=ALU.is_gt, fill=0.0, base=0,
                                    pattern=[[1, P]], channel_multiplier=-1).then_inc(s_tri, 1)
            pool.wait_ge(s_rows, 16)
            pool.wait_ge(s_fill, 16 * (MEXP * CAPP * D // P // 4096))
            pool.wait_ge(s_index, 1)
            for t in range(NTP):
                pool.indirect_dma_start(out=slots[:, :], out_offset=bass.IndirectOffsetOnAxis(ap=index[:, t:t + 1], axis=0),
                                        in_=rows[:, t, :], in_offset=None,
                                        bounds_check=MEXP * CAPP - 1, oob_is_err=False).then_inc(s_sent, 16)
            pool.wait_ge(s_sent, 16 * NTP)

        @block.tensor
        def _(pe):
            pe.wait_ge(s_load, 48)
            for n, (a, b) in enumerate(pieces):
                if n >= 2:
                    pe.wait_ge(s_logged, n - 1)
                for k in range(2):
                    last = nc.tensor.matmul(p_log[0:M, n % 2, 0:b - a], gw[:, k, :], xt[:, k, a:b],
                                            start=(k == 0), stop=(k == 1))
                last.then_inc(s_log, 1)
            pe.wait_ge(s_logged, len(pieces))
            for t in range(NTP):
                last = nc.tensor.transpose(p_tok[:, t * M:(t + 1) * M], logit_t[:, t * P:(t + 1) * P], c["ident"][0:M, 0:M])
            last.then_inc(s_tok, 1)
            pe.wait_ge(s_tri, 1)
            pe.wait_ge(s_one, 1)
            flat = one[:, :, :].rearrange("p t e -> p (t e)")
            nc.tensor.matmul(p_pre[:, 0, 0:NTP * M], before[:, :], flat, start=True, stop=True)
            nc.tensor.matmul(p_pre[:, 1, 0:NTP * M], c["ones"][:, :], flat, start=True, stop=True).then_inc(s_pre, 1)

        @block.scalar
        def _(act):
            for n, (a, b) in enumerate(pieces):
                act.wait_ge(s_log, n + 1)
                nc.scalar.activation(logit_t[:, a:b], p_log[0:M, n % 2, 0:b - a], ACT.Identity, bias=gb[:, 0:1]).then_inc(s_logged, 1)
            act.wait_ge(s_exp, 1)
            nc.scalar.activation(prob[:, :, :], prob[:, :, :], ACT.Exp).then_inc(s_exp, 1)

        @block.vector
        def _(dve):
            v = nc.vector
            done = Chain(dve, s_dve)
            wide = lambda m: m[:, :, None].to_broadcast([P, NTP, M])
            dve.wait_ge(s_tok, 1)
            done(v.tensor_copy(prob[:, :, :], p_tok[:, 0:NTP * M].rearrange("p (t e) -> p t e", e=M)))
            done(v.tensor_reduce(top[:, :], prob[:, :, :], axis=AX.X, op=ALU.max))
            done(v.tensor_tensor(prob[:, :, :], prob[:, :, :], wide(top), ALU.subtract))
            dve.sem_inc(s_exp)
            dve.wait_ge(s_exp, 2)
            done(v.tensor_reduce(total[:, :], prob[:, :, :], axis=AX.X, op=ALU.add))
            done(v.reciprocal(total[:, :], total[:, :]))
            done(v.tensor_tensor(prob[:, :, :], prob[:, :, :], wide(total), ALU.mult))
            done(v.tensor_reduce(top[:, :], prob[:, :, :], axis=AX.X, op=ALU.max))
            done(v.tensor_tensor(one[:, :, :], prob[:, :, :], wide(top), ALU.is_ge))
            done(v.tensor_scalar(token[:, :], c["ramp"][:, 0:NTP], float(P), c["part"][:, 0:1], ALU.mult, ALU.add))
            done(v.tensor_scalar(taken[:, :], token[:, :], float(N), None, ALU.is_ge))
            for e in range(M):
                done(v.scalar_tensor_tensor(one[:, :, e], taken[:, :], 0.5, one[:, :, e], ALU.is_lt, ALU.mult))
                done(v.tensor_tensor(taken[:, :], taken[:, :], one[:, :, e], ALU.add))
            dve.sem_inc(s_one)
            dve.wait_ge(s_pre, 1)
            done.mark(v.tensor_copy(place[:, :, :], p_pre[:, 0, 0:NTP * M].rearrange("p (t e) -> p t e", e=M)))
            done.mark(v.tensor_copy(per_tile[:, :, :], p_pre[:, 1, 0:NTP * M].rearrange("p (t e) -> p t e", e=M)))
            done(v.memset(ahead[:, :, :], 0.0))
            for e in range(M):
                done(v.tensor_tensor_scan(ahead[:, e, 1:], c["ones"][:, 0:NTP], per_tile[:, :, e], 0.0, ALU.mult, ALU.add))
            done(v.tensor_tensor(place[:, :, :], place[:, :, :], ahead[:, :, 0:NTP].rearrange("p e t -> p t e"), ALU.add))
            done(v.tensor_tensor(tmp[:, :, :], place[:, :, :], one[:, :, :], ALU.mult))
            done(v.tensor_reduce(pos[:, :], tmp[:, :, :], axis=AX.X, op=ALU.add))
            done(v.tensor_tensor(tmp[:, :, :], one[:, :, :], c["ramp"][:, None, 0:M].to_broadcast([P, NTP, M]), ALU.mult))
            done(v.tensor_reduce(expert[:, :], tmp[:, :, :], axis=AX.X, op=ALU.add))
            done(v.tensor_scalar(kept[:, :], pos[:, :], float(CAP), None, ALU.is_lt))
            done(v.tensor_scalar(token[:, :], token[:, :], float(N), None, ALU.is_lt))
            done(v.tensor_tensor(kept[:, :], kept[:, :], token[:, :], ALU.mult))
            done(v.tensor_tensor(coef[:, :], top[:, :], kept[:, :], ALU.mult))
            done(v.scalar_tensor_tensor(slot[:, :], expert[:, :], float(CAPP), pos[:, :], ALU.mult, ALU.add))
            done(v.tensor_scalar(kept[:, :], kept[:, :], -float(MEXP * CAPP), float(MEXP * CAPP), ALU.mult, ALU.add))
            done(v.tensor_tensor(slot[:, :], slot[:, :], kept[:, :], ALU.add))
            done(v.tensor_copy(index[:, :], slot[:, :]))
            dve.sem_inc(s_index)
            done(v.tensor_scalar(slot[:, :], slot[:, :], float(MEXP * CAPP - 1), None, ALU.min))
            done(v.tensor_copy(back[:, :], slot[:, :]))
            dve.sem_inc(s_done)


def routed_experts(nc, c, slots, w1_in, b1_in, w2_in, b2_in, out):
    ctx = ExitStack()
    with ctx:
        sp_ = Space(nc, ctx, "moe")
        FB, UNITS = MF // P, CAPP // (2 * P)
        w1 = sp_.sb("w1", [P, 2, 2, MF])
        w2 = sp_.sb("w2", [P, 2, FB, D])
        b1 = sp_.sb("b1", [P, 2, FB])
        b2 = sp_.sb("b2", [1, 2, D])
        x = sp_.sb("x", [P, 2, 2, D])
        xt = sp_.sb("xt", [P, 2, 2, 2 * P])
        hid = sp_.sb("hid", [P, FB, 2 * P])
        y = sp_.sb("y", [P, 2, 2, D])
        p_t = sp_.ps("p_t", [P, 2, 512])
        p_h = sp_.ps("p_h", [P, 4, 512])
        p_y = sp_.ps("p_y", [P, 2, 512])
        s_t, s_xt, s_h, s_a, s_y, s_copy = (sp_.sem(n) for n in ("t", "xt", "h", "a", "y", "copy"))
        s_in, s_out, s_w = ([sp_.sem(f"{n}{h}") for h in range(2)] for n in ("in", "out", "w"))
        NW = 16 * 5
        per_turn = 2 * UNITS
        block = sp_.block()

        def each_unit(eng, body, expert=None):
            with eng.Fori(0, MEXP // 2) as t:
                for o in range(2):
                    if expert:
                        expert(t, o)
                    for q in range(UNITS):
                        u = o * UNITS + q
                        body(t, o, u, u % 2)

        @block.sync
        def _(sp):
            for h in range(2):
                sp.sem_inc(s_out[h], 16)

            def expert(t, o):
                sp.wait_ge(s_y, per_turn * 2 * t + (2 * UNITS * o + 1))
                with nc.allow_non_contiguous_dma(reason="a bias per partition"):
                    for k in range(2):
                        sp.dma_start(w1[:, o, k, :], w1_in[bass.ds(2 * t + o, 1), k * P:(k + 1) * P, :]
                                     .rearrange("a p f -> p (a f)")).then_inc(s_w[o], 16)
                    sp.dma_start(w2[:, o, :, :], w2_in[bass.ds(2 * t + o, 1), :, :]
                                 .rearrange("a (f p) d -> p (a f) d", p=P)).then_inc(s_w[o], 16)
                    sp.dma_start(b1[:, o, :], b1_in[bass.ds(2 * t + o, 1), :].rearrange("a (f p) -> p (a f)", p=P)).then_inc(s_w[o], 16)
                    sp.dma_start(b2[:, o, :], b2_in[bass.ds(2 * t + o, 1), :]).then_inc(s_w[o], 16)

            def body(t, o, u, h):
                sp.wait_ge(s_t, per_turn * t + (u + 1))
                sp.dma_start(x[:, h, :, :], slots[bass.ds((per_turn * t + u) * 2 * P, 2 * P), :]
                             .rearrange("(i p) d -> p i d", p=P)).then_inc(s_in[h], 16)
            each_unit(sp, body, expert)

        @block.tensor
        def _(pe):
            pe.sem_inc(s_t, 2)
            pe.sem_inc(s_y, 2 * UNITS + 1)

            def body(t, o, u, h):
                if u % UNITS == 0:
                    pe.wait_ge(s_w[o], NW * t + NW)
                pe.wait_ge(s_in[h], 16 * (UNITS * t) + 16 * (u // 2 + 1))
                for k in range(2):
                    for i in range(2):
                        last = nc.tensor.transpose(p_t[:, k, i * P:(i + 1) * P], x[:, h, i, k * P:(k + 1) * P], c["ident"][:, :])
                last.then_inc(s_t, 1)
                pe.wait_ge(s_xt, per_turn * t + (u + 1))
                for f in range(FB):
                    pe.wait_ge(s_a, per_turn * FB * t + (u * FB + f + 1))
                    for k in range(2):
                        last = nc.tensor.matmul(p_h[:, f % 4, 0:2 * P], w1[:, o, k, f * P:(f + 1) * P], xt[:, h, k, :],
                                                start=(k == 0), stop=(k == 1))
                    last.then_inc(s_h, 1)
                for i in range(2):
                    pe.wait_ge(s_copy, per_turn * 2 * t + (2 * u + i + 1))
                    nc.tensor.matmul(p_y[:, i, 0:D], c["ones"][0:1, :], b2[0:1, o, :], start=True, stop=False)
                    for f in range(FB):
                        if i == 0:
                            pe.wait_ge(s_a, per_turn * FB * t + (u * FB + f + 1 + 4))
                        last = nc.tensor.matmul(p_y[:, i, 0:D], hid[:, f, i * P:(i + 1) * P], w2[:, o, f, :],
                                                start=False, stop=(f == FB - 1))
                    last.then_inc(s_y, 1)
            each_unit(pe, body)

        @block.scalar
        def _(act):
            act.sem_inc(s_a, 4)

            def body(t, o, u, h):
                for f in range(FB):
                    act.wait_ge(s_h, per_turn * FB * t + (u * FB + f + 1))
                    nc.scalar.activation(hid[:, f, :], p_h[:, f % 4, 0:2 * P], ACT.Relu, bias=b1[:, o, f:f + 1]).then_inc(s_a, 1)
                act.wait_ge(s_copy, per_turn * 2 * t + (2 * u + 4))
                act.dma_start(out[bass.ds((per_turn * t + u) * 2 * P, 2 * P), :].rearrange("(i p) d -> p i d", p=P),
                              y[:, h, :, :]).then_inc(s_out[h], 16)
            each_unit(act, body)
            for h in range(2):
                act.wait_ge(s_out[h], 16 * (MEXP * UNITS // 2) + 16)

        @block.vector
        def _(dve):
            dve.sem_inc(s_copy, 2)

            def body(t, o, u, h):
                dve.wait_ge(s_t, per_turn * t + (u + 3))
                nc.vector.tensor_copy(xt[:, h, :, :], p_t[:, :, 0:2 * P]).then_inc(s_xt, 1)
                dve.wait_ge(s_out[h], 16 * (UNITS * t) + 16 * (u // 2 + 1))
                for i in range(2):
                    dve.wait_ge(s_y, per_turn * 2 * t + (2 * u + i + 1 + 2 * UNITS + 1))
                    nc.vector.tensor_copy(y[:, h, i, :], p_y[:, i, 0:D]).then_inc(s_copy, 1)
            each_unit(dve, body)


def combine(nc, c, expert_out, coef_in, index_in, x_in, out):
    ctx = ExitStack()
    with ctx:
        sp_ = Space(nc, ctx, "combine")
        got = sp_.sb("got", [P, NTP, D])
        x = sp_.sb("x", [P, NTP, D])
        coef = sp_.sb("coef", [P, NTP])
        index = sp_.sb("index", [P, NTP], I32)
        mask = sp_.sb("mask", [P, 5, D], I32)
        fill = sp_.sb("fill", [P, 3, D])
        s_load, s_index, s_dve, s_done, s_out = (sp_.sem(n) for n in ("load", "index", "dve", "done", "out"))
        s_got = sp_.gathered(0)
        whole = N // P
        block = sp_.block()

        @block.sync
        def _(sp):
            sp.dma_start(index[:, :], index_in).then_inc(s_index, 16)
            sp.dma_start(coef[:, :], coef_in).then_inc(s_load, 16)
            sp.dma_start(x[:, :, :], x_in.rearrange("(t p) d -> p t d", p=P)).then_inc(s_load, 16)
            sp.wait_ge(s_done, 1)
            sp.dma_start(out[0:whole * P, :].rearrange("(t p) d -> p t d", p=P), x[:, 0:whole, :]).then_inc(s_out, 16)
            sp.dma_start(out[whole * P:N, :], x[0:N - whole * P, whole, :]).then_inc(s_out, 16)
            sp.wait_ge(s_out, 32)

        @block.gpsimd
        def _(pool):
            pool.wait_ge(s_index, 16)
            for t in range(NTP):
                pool.indirect_dma_start(out=got[:, t, :], out_offset=None, in_=expert_out[:, :],
                                        in_offset=bass.IndirectOffsetOnAxis(ap=index[:, t:t + 1], axis=0)).then_inc(s_got, 16)

        @block.vector
        def _(dve):
            v = nc.vector
            done = Chain(dve, s_dve)
            for i, a in enumerate((0.0, 1e4, -1e4)):
                done.mark(v.memset(fill[:, i, :], a))
            done.wait()
            dve.wait_ge(s_load, 32)
            dve.wait_ge(s_got, 16 * NTP)
            for a in range(0, NTP, 5):
                g = got[:, a:a + 5, :]
                done(v.tensor_tensor(g, g, coef[:, a:a + 5, None].to_broadcast([P, 5, D]), ALU.mult))
                for i, (value, op) in enumerate(((None, ALU.not_equal), (3.4028234e38, ALU.is_gt), (-3.4028234e38, ALU.is_lt))):
                    if value is None:
                        done(v.tensor_tensor(mask[:, :, :], g, g, op))
                    else:
                        done(v.tensor_scalar(mask[:, :, :], g, value, None, op))
                    for j in range(5):
                        done.mark(v.copy_predicated(got[:, a + j, :], mask[:, j, :], fill[:, i, :]))
                    done.wait()
                done(v.tensor_tensor(x[:, a:a + 5, :], x[:, a:a + 5, :], g, ALU.add))
            dve.sem_inc(s_done)


def build(nc, a, out):
    def dram(name, shape, dt=F32):
        return nc.dram_tensor(name, shape, dt).ap()

    rec = [dram(f"rec{s}", [ET2 + 1, P], I32) for s in range(LISTS)]
    local_rows = [dram(f"local_rows{s}", [CHUNKS[s] * P, P]) for s in range(LISTS)]
    tables = [dram(f"tables{s}", [3, P, CHUNKS[s] * P], I32) for s in range(LISTS)]
    node_rows = [dram(f"node_rows{s}", [1, CHUNKS[s] * P + EXTRA], I32) for s in range(LISTS)]
    lists = (tables, local_rows, node_rows)
    x0, x1, x2, x3 = (dram(f"x{i}", [NPAD, D]) for i in range(4))
    scores = [dram(f"scores{s}", [P, NTP, 2 * HEADS]) for s in range(3)]
    wide = [dram(f"wide{s}", [NPAD, HC + HEADS]) for s in range(2)]
    slim = dram("slim", [NPAD, HEADS * NEXP + HEADS])
    att = [dram(f"att{s}", [NPAD, HC]) for s in range(2)] + [dram("att2", [NPAD, HEADS * NEXP])]
    counts = [dram(f"counts{s}", [P, NTP]) for s in range(3)]
    kept = dram("kept", [ITEMS1 // GRP, P, GRP * (HC + HEADS)])
    kept2 = dram("kept2", [ITEMS2 // GRP, P, GRP * (HEADS * NEXP + HEADS)])
    gates = dram("gates", [P, NTP, NEXP])
    ctx = ExitStack()
    with ctx:
        sp_ = Space(nc, ctx, "main")
        c = {"ident": sp_.sb("ident", [P, P]), "ones": sp_.sb("ones", [P, P]), "ramp": sp_.sb("ramp", [P, CHM * P]),
             "part": sp_.sb("part", [P, 1]), "item_of": sp_.sb("item_of", [P, CHM]),
             "sign": sp_.sb("sign", [P, 8]), "turn": sp_.sb("turn", [P, 8])}
        GATHERED[:] = [sp_.sem("gathered0"), sp_.sem("gathered1")]
        constants(nc, c)
        sort_edges(nc, c, a["src"], a["dst"], a["L0_ffn_edge_index"], rec)
        for s in range(LISTS):
            make_items(nc, c, s, rec, local_rows, tables, node_rows)
        pad_rows(nc, a["x"], x0)

        inner = ExitStack()
        with inner:
            xt = Space(nc, inner, "l0g").sb("xt", [P, 2, NPAD + 2 * P])
            normalise(nc, c, "norm0", x0, xt)
            project(nc, c, "proj0", xt, [a["L0_gnn_W_f"], a["L0_gnn_W_b"]],
                    [dict(width=HC, a_src=a[f"L0_gnn_a_src_{x}"], a_dst=a[f"L0_gnn_a_dst_{x}"], table=wide[s],
                          nodes=scores[s]) for s, x in enumerate("fb")])
        for s, x in enumerate("fb"):
            attention(nc, c, f"att{s}", s, HC, wide[s], scores[s], a[f"L0_gnn_b_{x}"], *lists, kept, att[s], counts[s])
        rows_product(nc, c, "fuse", att[0:2], a["L0_gnn_W_fuse"], x1, NTP,
                     bn=[a[f"L0_gnn_{n}"] for n in ("b_fuse", "gamma", "beta", "run_mean", "run_var")], x_in=x0)

        inner = ExitStack()
        with inner:
            xt = Space(nc, inner, "l0f").sb("xt", [P, 2, NPAD + 2 * P])
            normalise(nc, c, "norm1", x1, xt)
            project(nc, c, "proj1", xt, [a["L0_ffn_W_gat"]],
                    [dict(width=HEADS * NEXP, a_src=a["L0_ffn_att_src"], a_dst=a["L0_ffn_att_dst"], table=slim,
                          nodes=scores[2])])
        attention(nc, c, "att2", 2, HEADS * NEXP, slim, scores[2], a["L0_ffn_b_gat"], *lists, kept2, att[2], counts[2])
        choose_experts(nc, c, att[2], a["L0_ffn_ln_gamma"], a["L0_ffn_ln_beta"], gates)
        inner = ExitStack()
        with inner:
            xt = Space(nc, inner, "l0e").sb("xt", [P, 2, NPAD + 2 * P])
            normalise(nc, c, "norm1b", x1, xt)
            gated_experts(nc, c, xt, x1, gates, a["L0_ffn_W1"], a["L0_ffn_b1"], a["L0_ffn_W2"], a["L0_ffn_b2"], x2)

        xn, h1, e1, h2, n1, h3, e2, h4 = (
            dram(n, [NPAD if n in ("xn", "h1", "n1", "h3") else NHT * P, D]) for n in ("xn", "h1", "e1", "h2", "n1", "h3", "e2", "h4"))
        inner = ExitStack()
        with inner:
            xt = Space(nc, inner, "l1g").sb("xt", [P, 2, NPAD + 2 * P])
            normalise(nc, c, "norm2", x2, xt, rows_out=xn)
        rows_product(nc, c, "n2e0", [xn], a["L1_gnn_W0_n2e"], h1, NTP)
        hyper_sum(nc, c, "hyp0", 0, h1, tables, node_rows, e1, counts[0], True)
        rows_product(nc, c, "e2n0", [e1], a["L1_gnn_W0_e2n"], h2, NHT)
        hyper_sum(nc, c, "hyp1", 3, h2, tables, node_rows, n1, counts[1], True)
        rows_product(nc, c, "n2e1", [n1], a["L1_gnn_W1_n2e"], h3, NTP)
        hyper_sum(nc, c, "hyp2", 0, h3, tables, node_rows, e2, counts[0], True)
        rows_product(nc, c, "e2n1", [e2], a["L1_gnn_W1_e2n"], h4, NHT)
        hyper_sum(nc, c, "hyp3", 3, h4, tables, node_rows, x3, counts[1], False, x_in=x2)

        slots, done = dram("slots", [MEXP * CAPP, D]), dram("done", [MEXP * CAPP, D])
        coef, back, xm = dram("coef", [P, NTP]), dram("back", [P, NTP], I32), dram("xm", [NPAD, D])
        inner = ExitStack()
        with inner:
            xt = Space(nc, inner, "l1f").sb("xt", [P, 2, NPAD + 2 * P])
            normalise(nc, c, "norm3", x3, xt, rows_out=xm)
            route(nc, c, xt, xm, a["L1_ffn_gate_w"], a["L1_ffn_gate_b"], slots, coef, back)
        routed_experts(nc, c, slots, a["L1_ffn_w1"], a["L1_ffn_b1"], a["L1_ffn_w2"], a["L1_ffn_b2"], done)
        combine(nc, c, done, coef, back, x3, out)


_INS = (["x", "src", "dst"]
        + ["L0_gnn_" + n for n in ("W_f", "a_src_f", "a_dst_f", "b_f", "W_b", "a_src_b", "a_dst_b", "b_b", "W_fuse",
                                   "b_fuse", "gamma", "beta", "run_mean", "run_var")]
        + ["L0_ffn_" + n for n in ("W_gat", "att_src", "att_dst", "b_gat", "ln_gamma", "ln_beta", "W1", "b1", "W2",
                                   "b2", "edge_index")]
        + ["L1_gnn_" + n for n in ("W0_n2e", "W0_e2n", "W1_n2e", "W1_e2n")]
        + ["L1_ffn_" + n for n in ("gate_w", "gate_b", "w1", "b1", "w2", "b2")])


def kernel(**inputs):
    import numpy as np
    import concourse.bacc as bacc
    from concourse.bass_utils import run_bass_kernel_spmd

    nc = bacc.Bacc("TRN2", target_bir_lowering=False, num_devices=1)
    arrays, args = {}, {}
    for name in _INS:
        arr = np.ascontiguousarray(inputs[name])
        arrays[f"in_{name}"] = arr
        args[name] = nc.dram_tensor(f"in_{name}", arr.shape, mybir.dt.from_np(arr.dtype), kind="ExternalInput").ap()
    out = nc.dram_tensor("out_x", (N, D), F32, kind="ExternalOutput").ap()
    build(nc, args, out)
    r = run_bass_kernel_spmd(nc, [arrays], core_ids=[0])
    return r.results[0]["out_x"]
```

```python
import concourse.bass as bass
from concourse import mybir
from contextlib import ExitStack

F32 = mybir.dt.float32
I32 = mybir.dt.int32
ALU = mybir.AluOpType
ACT = mybir.ActivationFunctionType
AX = mybir.AxisListType

P = 128
N = 6250
D = 256
NT = -(-N // P)
NTP = NT + 1
NPAD = NTP * P
E1 = 100000
E2 = 131072
SORT = 1 << 17
ROW = SORT // P
ET1 = -(-E1 // P)
ET2 = E2 // P
ROUND = 16
GRP = ROUND // 2
MOST = lambda edge_tiles: -(-(edge_tiles + 2 * NT) // ROUND) * ROUND
ITEMS1 = MOST(ET1)
ITEMS2 = MOST(ET2 + 1)
PAIRS = GRP // 2
CH1 = -(-ITEMS1 // P)
CH2 = -(-ITEMS2 // P)
CHUNKS = [CH1, CH1, CH2, CH1]
LISTS = len(CHUNKS)
ITEMS = [ITEMS1, ITEMS1, ITEMS2, ITEMS1]
CHM = max(CHUNKS)
BESIDE = NTP
LEAST_ITEMS = [1.0, 1.0, (BESIDE + 1.0) * ROUND, 1.0]
TURNS_ALL, TURNS_HYPER, LAST_TURN = 0, 1, 2
EXTRA = 3
KEY_SHIFT = 13
CODE_BASE = 1 << 28
FIELD = (1 << KEY_SHIFT) - 1
BIG = 1.0e30
HEADS = 4
CH = 32
HC = HEADS * CH
NEXP = 4
FH = 512
MEXP = 8
MF = 1024
NHYP = 2500
NHT = -(-NHYP // P)
CAP = -(-(5 * N) // (4 * MEXP))
CAPP = -(-CAP // P) * P
EPS = 1e-5


class Chain:

    def __init__(self, eng, sem):
        self.eng, self.sem, self.base, self.count = eng, sem, 0, 0

    def value(self):
        return self.base + self.count

    def mark(self, ins):
        ins.then_inc(self.sem, 1)
        self.count += 1

    def wait(self):
        self.eng.wait_ge(self.sem, self.value())

    def __call__(self, ins):
        self.mark(ins)
        self.wait()

    def enter(self, t, per_turn):
        self.outer = self.value()
        self.per_turn = per_turn
        self.base, self.count = t * per_turn + self.outer, 0

    def enter_last(self, t):
        self.leave(0)
        self.enter(t, self.per_turn)

    def leave(self, turns):
        assert self.count == self.per_turn, (self.count, self.per_turn)
        self.base, self.count = self.outer + turns * self.per_turn, 0


class Space:

    def __init__(self, nc, ctx, prefix):
        self.nc, self.ctx, self.prefix, self.sems = nc, ctx, prefix, []

    def sb(self, name, shape, dt=F32):
        return self.ctx.enter_context(self.nc.sbuf_tensor(f"{self.prefix}_{name}", shape, dt))

    def ps(self, name, shape, dt=F32):
        return self.ctx.enter_context(self.nc.psum_tensor(f"{self.prefix}_{name}", shape, dt))

    def sem(self, name):
        self.sems.append(self.ctx.enter_context(self.nc.semaphore(f"{self.prefix}_{name}")))
        return self.sems[-1]

    def gathered(self, i):
        self.sems.append(GATHERED[i])
        return self.sems[-1]

    def block(self):
        self.ctx.callback(self.clear)
        return self.ctx.enter_context(self.nc.Block())

    def clear(self):
        for s in self.sems:
            if s in GATHERED:
                self.nc.gpsimd.dma_reset(range(s.num, s.num + 1))
            self.nc.gpsimd.sem_clear(s)
        self.nc.all_engine_barrier(sem_only=True)


GATHERED = []


def constants(nc, c):
    ctx = ExitStack()
    with ctx:
        sp_ = Space(nc, ctx, "const")
        s_pool, s_dve = sp_.sem("pool"), sp_.sem("dve")
        ramp_i = sp_.sb("ramp_i", [P, CHM * P], I32)
        part_i = sp_.sb("part_i", [P, 1], I32)
        row_i = sp_.sb("row_i", [P, CHM], I32)
        bits = sp_.sb("bits", [P, 8], I32)
        block = sp_.block()

        @block.gpsimd
        def _(pool):
            nc.gpsimd.memset(c["ident"][:, :], 0.0).then_inc(s_pool, 1)
            nc.gpsimd.memset(c["ones"][:, :], 1.0).then_inc(s_pool, 1)
            nc.gpsimd.iota(ramp_i[:, :], pattern=[[1, CHM * P]], base=0, channel_multiplier=0).then_inc(s_pool, 1)
            nc.gpsimd.iota(part_i[:, :], pattern=[[1, 1]], base=0, channel_multiplier=1).then_inc(s_pool, 1)
            nc.gpsimd.iota(row_i[:, :], pattern=[[P, CHM]], base=0, channel_multiplier=1).then_inc(s_pool, 1)
            pool.wait_ge(s_pool, 5)
            nc.gpsimd.affine_select(out=c["ident"][:, :], in_=c["ident"][:, :], compare_op=ALU.not_equal, fill=1.0,
                                    base=0, pattern=[[-1, P]], channel_multiplier=1).then_inc(s_pool, 1)

        @block.vector
        def _(dve):
            done = Chain(dve, s_dve)
            dve.wait_ge(s_pool, 5)
            nc.vector.tensor_copy(c["ramp"][:, :], ramp_i[:, :])
            nc.vector.tensor_copy(c["part"][:, :], part_i[:, :])
            nc.vector.tensor_copy(c["item_of"][:, :], row_i[:, :])
            for b in range(7):
                done.mark(nc.vector.tensor_scalar(bits[:, b:b + 1], part_i[:, :], b, 1,
                                                  ALU.logical_shift_right, ALU.bitwise_and))
            done.wait()
            done(nc.vector.tensor_scalar(c["sign"][:, 0:7], bits[:, 0:7], -2.0, 1.0, ALU.mult, ALU.add))
            done.mark(nc.vector.tensor_tensor(c["turn"][:, 1:7], c["sign"][:, 0:6], c["sign"][:, 1:7], ALU.mult))
            done.mark(nc.vector.tensor_copy(c["turn"][:, 0:1], c["sign"][:, 0:1]))
            done(nc.vector.tensor_copy(c["turn"][:, 7:8], c["sign"][:, 6:7]))


def sort_edges(nc, c, src, dst, edges2, rec):
    ctx = ExitStack()
    with ctx:
        sp_ = Space(nc, ctx, "sort")
        ends = sp_.sb("ends", [P, 4, ROW], I32)
        pay = sp_.sb("pay", [P, LISTS, ROW], I32)
        beyond = sp_.sb("beyond", [P, ROW], I32)
        xy = [sp_.sb("x", [P, LISTS * ROW]), sp_.sb("y", [P, LISTS * ROW])]
        pad = sp_.sb("pad", [1, P], I32)
        flip = sp_.ps("flip", [P, LISTS * ROW])
        s_pad, s_load = sp_.sem("pad"), sp_.sem("load")
        s_dve, s_ready, s_flipped, s_half, s_out = (sp_.sem(x) for x in ("dve", "ready", "flipped", "half", "out"))
        HALF = LISTS * ROW // 2
        full = E1 // ROW * ROW // (16 * ROW) * 16
        rest = E1 - full * ROW
        block = sp_.block()

        @block.gpsimd
        def _(pool):
            nc.gpsimd.memset(ends[:, 0:2, :], N).then_inc(s_pad, 1)
            nc.gpsimd.memset(pad[:, :], CODE_BASE + (N << KEY_SHIFT)).then_inc(s_pad, 1)

        @block.sync
        def _(sp):
            for j in range(2):
                sp.dma_start(ends[:, 2 + j, :], edges2[1 - j, :].rearrange("(p c) -> p c", c=ROW)).then_inc(s_load, 16)
            sp.wait_ge(s_pad, 2)
            for j, a in ((0, dst), (1, src)):
                sp.dma_start(ends[0:full, j, :], a[0:full * ROW].rearrange("(p c) -> p c", c=ROW)).then_inc(s_load, 16)
                sp.dma_start(ends[full:full + rest // ROW, j, :],
                             a[full * ROW:full * ROW + rest // ROW * ROW].rearrange("(p c) -> p c", c=ROW)).then_inc(s_load, 16)
                sp.dma_start(ends[full + rest // ROW:full + rest // ROW + 1, j, 0:rest % ROW],
                             a[E1 - rest % ROW:E1].rearrange("(p c) -> p c", p=1)).then_inc(s_load, 16)
            for s in range(LISTS):
                sp.dma_start(rec[s][ET2:ET2 + 1, :], pad[:, :]).then_inc(s_out, 16)
            sp.wait_ge(s_ready, 15)
            for s in range(LISTS):
                sp.dma_start(rec[s][0:ET2, :].rearrange("(p a) b -> p (a b)", a=ROW // P),
                             xy[0][:, s * ROW:(s + 1) * ROW].bitcast(I32)).then_inc(s_out, 16)
            sp.wait_ge(s_out, 16 * 2 * LISTS)

        @block.vector
        def _(dve):
            done = Chain(dve, s_dve)
            at = [0]

            def swap():
                at[0] ^= 1
                return xy[at[0] ^ 1], xy[at[0]]

            dve.wait_ge(s_load, 16 * 8)
            for s, (k, v) in enumerate(((0, 1), (1, 0), (2, 3), (1, 0))):
                done.mark(nc.vector.tensor_scalar_min(pay[:, s, :], ends[:, v, :], float(N - 1)))
            done.wait()
            done(nc.vector.tensor_scalar_min(ends[:, :, :], ends[:, :, :], float(N)))
            done(nc.vector.tensor_scalar(beyond[:, :], ends[:, 0, :], float(NHYP), float(N), ALU.is_ge, ALU.mult))
            done(nc.vector.tensor_tensor(ends[:, 3, :], ends[:, 1, :], beyond[:, :], ALU.max))
            x = xy[0][:, :].bitcast(I32).rearrange("p (s c) -> p s c", s=LISTS)
            y = xy[1][:, :].bitcast(I32).rearrange("p (s c) -> p s c", s=LISTS)
            done(nc.vector.tensor_scalar(y, ends[:, :, :], KEY_SHIFT, CODE_BASE, ALU.logical_shift_left, ALU.bitwise_or))
            done(nc.vector.tensor_tensor(x, y, pay[:, :, :], ALU.bitwise_or))

            def exchange(gap):
                a, b = swap()
                a, b = (z[:, :].rearrange("p (m two j) -> p m two j", two=2, j=gap) for z in (a, b))
                done.mark(nc.vector.tensor_tensor(b[:, :, 0, :], a[:, :, 0, :], a[:, :, 1, :], ALU.min))
                done(nc.vector.tensor_tensor(b[:, :, 1, :], a[:, :, 0, :], a[:, :, 1, :], ALU.max))

            def exchange_both_ways(gap, run):
                a, b = swap()
                a, b = (z[:, :].rearrange("p (g d m two j) -> p g d m two j", d=2, m=run // (2 * gap), two=2, j=gap)
                        for z in (a, b))
                for d, lower, upper in ((0, ALU.min, ALU.max), (1, ALU.max, ALU.min)):
                    for half, op in ((0, lower), (1, upper)):
                        done.mark(nc.vector.tensor_tensor(b[:, :, d, :, half, :], a[:, :, d, :, 0, :],
                                                          a[:, :, d, :, 1, :], op))
                done.wait()

            def turn(b):
                a, z = swap()
                done(nc.vector.tensor_scalar(z[:, :], a[:, :], c["turn"][:, b:b + 1], None, ALU.mult))

            def change_layout(n):
                a, b = swap()
                dve.sem_inc(s_ready)
                dve.wait_ge(s_flipped, n)
                done(nc.vector.tensor_copy(b[:, 0:HALF], flip[:, 0:HALF]))
                dve.wait_ge(s_half, n)

            for k in range(1, 10):
                for j in range(k - 1, -1, -1):
                    exchange_both_ways(1 << j, 1 << k)
            turn(0)
            for j in range(9, -1, -1):
                exchange(1 << j)
            n = 0
            for k in range(11, 18):
                turn(k - 10)
                n += 1
                change_layout(n)
                for j in range(k - 1, 6, -1):
                    exchange(1 << (j - 10) if j >= 10 else P << (j - 7))
                n += 1
                change_layout(n)
                for j in range(6, -1, -1):
                    exchange(1 << j)
            if at[0]:
                a, b = swap()
                done(nc.vector.tensor_copy(b[:, :], a[:, :]))
            dve.sem_inc(s_ready)

        at = [0]

        @block.tensor
        def _(pe):
            for n, (x, _) in enumerate(layouts()):
                pe.wait_ge(s_ready, n + 1)
                for b in range(LISTS * ROW // P):
                    last = nc.tensor.transpose(flip[:, b * P:(b + 1) * P], xy[x][:, b * P:(b + 1) * P], c["ident"][:, :])
                last.then_inc(s_flipped, 1)

        @block.scalar
        def _(act):
            for n, (_, y) in enumerate(layouts()):
                act.wait_ge(s_flipped, n + 1)
                nc.scalar.copy(xy[y][:, HALF:], flip[:, HALF:]).then_inc(s_half, 1)


def layouts():
    at = sum(range(1, 10)) + 1 + 10
    for k in range(11, 18):
        at += 1
        yield at % 2, (at + 1) % 2
        at += 1 + (k - 7)
        yield at % 2, (at + 1) % 2
        at += 1 + 7


def make_items(nc, c, s, rec, local_rows, tables, node_rows):
    chunks, n_items = CHUNKS[s], CHUNKS[s] * P
    ctx = ExitStack()
    with ctx:
        sp_ = Space(nc, ctx, f"items{s}")
        last_code = sp_.sb("last_code", [P, ROW // P], I32)
        last_key_i = sp_.sb("last_key_i", [P, ROW // P], I32)
        last_key = sp_.sb("last_key", [P, ROW // P])
        bound = sp_.sb("bound", [P, NTP])
        below = sp_.sb("below", [P, NTP, ROW // P])
        count = sp_.sb("count", [P, NTP])
        first = sp_.sb("first", [1, NTP])
        items_i = sp_.sb("items_i", [1, NT], I32)
        items_f = sp_.sb("items_f", [1, NT])
        ones = sp_.sb("ones", [1, NT])
        start = sp_.sb("start", [1, NTP])
        ahead = sp_.sb("ahead", [1, NTP])
        step = sp_.sb("step", [1, NT])
        turns = sp_.sb("turns", [1, EXTRA])
        turns_i = sp_.sb("turns_i", [1, EXTRA], I32)
        start_c, step_c = sp_.sb("start_c", [NT, 1]), sp_.sb("step_c", [NT, 1])
        began = sp_.sb("began", [NT, n_items])
        node_of, off_of = sp_.sb("node_of", [P, chunks]), sp_.sb("off_of", [P, chunks])
        tile_f = sp_.sb("tile_f", [P, chunks])
        tile_i = sp_.sb("tile_i", [P, chunks], I32)
        rows = sp_.sb("rows", [P, chunks, P], I32)
        keys_r = sp_.sb("keys_r", [P, chunks, P], I32)
        local_r = sp_.sb("local_r", [P, chunks, P])
        code_t = sp_.sb("code_t", [P, n_items])
        keys_t = sp_.sb("keys_t", [P, n_items], I32)
        p_first = sp_.ps("p_first", [P, 512])
        p_node = sp_.ps("p_node", [P, 3, 512])
        p_flip = sp_.ps("p_flip", [P, 3, 512])
        s_load, s_dve, s_first, s_began, s_node, s_tile, s_out = (
            sp_.sem(x) for x in ("load", "dve", "first", "began", "node", "tile", "out"))
        s_flip, s_table, s_count, s_start, s_column = (sp_.sem(x) for x in ("flip", "table", "count", "start", "column"))
        s_rows = sp_.gathered(0)
        g = {"pay": sp_.sb("pay", [P, n_items], I32), "key": sp_.sb("key", [P, n_items]),
             "local": sp_.sb("local", [P, n_items]), "node_f": sp_.sb("node_f", [P, n_items]),
             "node_i": sp_.sb("node_i", [1, n_items + EXTRA], I32)}
        parts = [(a, min(a + 384, n_items)) for a in range(0, n_items, 384)]
        block = sp_.block()

        @block.sync
        def _(sp):
            with nc.allow_non_contiguous_dma(reason="the last code of every edge tile"):
                sp.dma_start(last_code[:, :], rec[s][0:ET2, P - 1].rearrange("(p a) -> p a", a=ROW // P)).then_inc(s_load, 16)
            sp.wait_ge(s_table, 1)
            for q in range(chunks):
                sp.dma_start(local_rows[s][q * P:(q + 1) * P, :], local_r[:, q, :]).then_inc(s_out, 16)
            sp.wait_ge(s_table, 2)
            sp.dma_start(tables[s][0, :, :], g["pay"][:, :]).then_inc(s_out, 16)
            sp.dma_start(tables[s][1, :, :], g["key"][:, :].bitcast(I32)).then_inc(s_out, 16)
            sp.dma_start(tables[s][2, :, :], g["local"][:, :].bitcast(I32)).then_inc(s_out, 16)
            sp.dma_start(tables[s][3, :, :], g["node_f"][:, :].bitcast(I32)).then_inc(s_out, 16)
            sp.dma_start(node_rows[s], g["node_i"][:, :]).then_inc(s_out, 16)
            sp.wait_ge(s_out, 16 * (chunks + 5))

        @block.vector
        def _(dve):
            done = Chain(dve, s_dve)
            dve.wait_ge(s_load, 16)
            done(nc.vector.tensor_scalar(last_key_i[:, :], last_code[:, :], KEY_SHIFT, FIELD,
                                         ALU.logical_shift_right, ALU.bitwise_and))
            done.mark(nc.vector.tensor_copy(last_key[:, :], last_key_i[:, :]))
            done(nc.vector.tensor_scalar(bound[:, :], c["ramp"][:, 0:NTP], float(P), float(N), ALU.mult, ALU.min))
            done(nc.vector.tensor_tensor(below[:, :, :], last_key[:, None, :].to_broadcast([P, NTP, ROW // P]),
                                         bound[:, :, None].to_broadcast([P, NTP, ROW // P]), ALU.is_lt))
            done(nc.vector.tensor_reduce(count[:, :], below[:, :, :], axis=AX.X, op=ALU.add))
            dve.sem_inc(s_count)
            dve.wait_ge(s_first, 1)
            done(nc.vector.tensor_copy(first[:, :], p_first[0:1, 0:NTP]))
            done(nc.vector.tensor_tensor(items_f[:, :], first[:, 1:], first[:, 0:NT], ALU.subtract))
            done(nc.vector.tensor_scalar(items_i[:, :], items_f[:, :], 2.0, None, ALU.add))
            done(nc.vector.tensor_scalar(items_i[:, :], items_i[:, :], 1, 1, ALU.logical_shift_right, ALU.logical_shift_left))
            done.mark(nc.vector.tensor_copy(items_f[:, :], items_i[:, :]))
            done.mark(nc.vector.memset(ones[:, :], 1.0))
            done(nc.vector.memset(start[:, 0:1], 0.0))
            done(nc.vector.tensor_tensor_scan(start[:, 1:], ones[:, :], items_f[:, :], 0.0, ALU.mult, ALU.add))
            done(nc.vector.tensor_tensor(ahead[:, :], start[:, :], first[:, :], ALU.subtract))
            done.mark(nc.vector.memset(step[:, 0:1], 0.0))
            done.mark(nc.vector.tensor_tensor(step[:, 1:], ahead[:, 1:NT], ahead[:, 0:NT - 1], ALU.subtract))
            done(nc.vector.tensor_scalar(start[:, NT:], start[:, NT:], LEAST_ITEMS[s], None, ALU.max))
            for at, b, more in ((TURNS_ALL, NT, ROUND - 1.0), (TURNS_HYPER, NHT, ROUND - 1.0), (LAST_TURN, NT, -1.0)):
                done.mark(nc.vector.tensor_scalar(turns[:, at:at + 1], start[:, b:b + 1], more, None, ALU.add))
            done.wait()
            done(nc.vector.tensor_copy(turns_i[:, :], turns[:, :]))
            done(nc.vector.tensor_scalar(g["node_i"][:, n_items:], turns_i[:, :], ROUND.bit_length() - 1, None,
                                         ALU.logical_shift_right))
            dve.sem_inc(s_start)
            dve.wait_ge(s_column, 1)
            done.mark(nc.vector.tensor_copy(start_c[:, :], p_first[0:NT, 64:65]))
            done(nc.vector.tensor_copy(step_c[:, :], p_first[0:NT, 65:66]))
            done(nc.vector.tensor_scalar(began[:, :], c["ramp"][0:NT, 0:n_items], start_c[:, 0:1], None, ALU.is_ge))
            done(nc.vector.memset(began[0:1, :], 0.0))
            dve.sem_inc(s_began)
            dve.wait_ge(s_node, 1)
            done.mark(nc.vector.tensor_copy(node_of[:, :], p_first[:, 128:128 + chunks]))
            done(nc.vector.tensor_copy(off_of[:, :], p_first[:, 192:192 + chunks]))
            done(nc.vector.tensor_tensor(tile_f[:, :], c["item_of"][:, 0:chunks], off_of[:, :], ALU.subtract))
            done(nc.vector.tensor_scalar_min(tile_f[:, :], tile_f[:, :], float(ET2)))
            done(nc.vector.tensor_copy(tile_i[:, :], tile_f[:, :]))
            dve.sem_inc(s_tile)
            for n, (a, b) in enumerate(parts):
                done.mark(nc.vector.tensor_copy(g["node_f"][:, a:b], p_node[:, n, 0:b - a]))
            done.wait()
            done(nc.vector.tensor_copy(g["node_i"][:, 0:n_items], g["node_f"][0:1, :]))
            dve.wait_ge(s_rows, 16 * chunks)
            done(nc.vector.tensor_scalar(keys_r[:, :, :], rows[:, :, :], KEY_SHIFT, FIELD,
                                         ALU.logical_shift_right, ALU.bitwise_and))
            done(nc.vector.tensor_copy(local_r[:, :, :], keys_r[:, :, :]))
            for q in range(chunks):
                done(nc.vector.scalar_tensor_tensor(local_r[:, q, :], node_of[:, q:q + 1].to_broadcast([P, P]), -float(P),
                                                    local_r[:, q, :], ALU.mult, ALU.add))
            dve.sem_inc(s_table)
            dve.wait_ge(s_flip, 1)
            for n, (a, b) in enumerate(parts):
                done.mark(nc.vector.tensor_copy(code_t[:, a:b], p_flip[:, n, 0:b - a]))
            done.wait()
            code = code_t[:, :].bitcast(I32)
            done.mark(nc.vector.tensor_scalar(g["pay"][:, :], code, FIELD, None, ALU.bitwise_and))
            done(nc.vector.tensor_scalar(keys_t[:, :], code, KEY_SHIFT, FIELD, ALU.logical_shift_right, ALU.bitwise_and))
            done(nc.vector.tensor_copy(g["key"][:, :], keys_t[:, :]))
            done(nc.vector.scalar_tensor_tensor(g["local"][:, :], g["node_f"][:, :], -float(P), g["key"][:, :],
                                                ALU.mult, ALU.add))
            dve.sem_inc(s_table)

        @block.tensor
        def _(pe):
            pe.wait_ge(s_count, 1)
            nc.tensor.matmul(p_first[:, 0:NTP], c["ones"][:, :], count[:, :], start=True, stop=True).then_inc(s_first, 1)
            pe.wait_ge(s_start, 1)
            nc.tensor.matmul(p_first[0:NT, 64:65], start[:, 0:NT], c["ones"][0:1, 0:1], start=True, stop=True)
            nc.tensor.matmul(p_first[0:NT, 65:66], step[:, :], c["ones"][0:1, 0:1], start=True, stop=True).then_inc(s_column, 1)
            pe.wait_ge(s_began, 1)
            for n, (a, b) in enumerate(parts):
                nc.tensor.matmul(p_node[:, n, 0:b - a], c["ones"][0:NT, :], began[:, a:b], start=True, stop=True)
            for q in range(chunks):
                nc.tensor.matmul(p_first[:, 128 + q:129 + q], began[:, q * P:(q + 1) * P], c["ones"][0:NT, 0:1],
                                 start=True, stop=True)
                last = nc.tensor.matmul(p_first[:, 192 + q:193 + q], began[:, q * P:(q + 1) * P], step_c[:, :],
                                        start=True, stop=True)
            last.then_inc(s_node, 1)
            pe.wait_ge(s_rows, 16 * chunks)
            for q in range(chunks):
                last = nc.tensor.transpose(p_flip[:, q // 3, q % 3 * P:(q % 3 + 1) * P],
                                           rows[:, q, :].bitcast(F32), c["ident"][:, :])
            last.then_inc(s_flip, 1)

        @block.gpsimd
        def _(pool):
            pool.wait_ge(s_tile, 1)
            for q in range(chunks):
                pool.indirect_dma_start(out=rows[:, q, :], out_offset=None, in_=rec[s][:, :],
                                        in_offset=bass.IndirectOffsetOnAxis(ap=tile_i[:, q:q + 1], axis=0)).then_inc(s_rows, 16)



def normalise(nc, c, name, x_in, xt, rows_out=None):
    ctx = ExitStack()
    with ctx:
        sp_ = Space(nc, ctx, name)
        x = sp_.sb("x", [P, NTP, D])
        stats = sp_.sb("stats", [P, NTP, 6])
        mean, dev, var, rstd = (sp_.sb(n, [P, NTP]) for n in ("mean", "dev", "var", "rstd"))
        y = sp_.sb("y", [P, 2, D])
        p_t = sp_.ps("p_t", [P, 2, 2, 256])
        s_load, s_dve, s_stats, s_var, s_std = (sp_.sem(n) for n in ("load", "dve", "stats", "var", "std"))
        s_y, s_t, s_xt = sp_.sem("y_ready"), sp_.sem("t_ready"), sp_.sem("t_free")
        s_out = [sp_.sem("out0"), sp_.sem("out1")]
        block = sp_.block()

        @block.sync
        def _(sp):
            sp.dma_start(x[:, :, :], x_in.rearrange("(t p) d -> p t d", p=P)).then_inc(s_load, 16)
            if rows_out is not None:
                for h in range(2):
                    sp.sem_inc(s_out[h], 16)
                with sp.Fori(0, NTP // 2) as t:
                    for h in range(2):
                        sp.wait_ge(s_y, 2 * t + (h + 1))
                        sp.dma_start(rows_out[bass.ds((2 * t + h) * P, P), :], y[:, h, :]).then_inc(s_out[h], 16)
                for h in range(2):
                    sp.wait_ge(s_out[h], 16 * (NTP // 2 + 1))

        @block.vector
        def _(dve):
            dve.wait_ge(s_load, 16)
            with dve.Fori(0, NTP // 2) as t:
                for h in range(2):
                    nc.vector.bn_stats(stats[:, bass.ds(2 * t + h, 1), :],
                                       x[:, bass.ds(2 * t + h, 1), :]).then_inc(s_stats, 1)
            done = Chain(dve, s_dve)
            dve.wait_ge(s_stats, NTP)
            even, odd = stats[:, :, 1], stats[:, :, 4]
            done.mark(nc.vector.tensor_tensor(mean[:, :], even, odd, ALU.add))
            done.mark(nc.vector.tensor_tensor(dev[:, :], even, odd, ALU.subtract))
            done(nc.vector.tensor_tensor(var[:, :], stats[:, :, 2], stats[:, :, 5], ALU.add))
            done.mark(nc.vector.tensor_scalar(mean[:, :], mean[:, :], 0.5, None, ALU.mult))
            done.mark(nc.vector.tensor_scalar(var[:, :], var[:, :], 1.0 / D, EPS, ALU.mult, ALU.add))
            done(nc.vector.tensor_tensor(dev[:, :], dev[:, :], dev[:, :], ALU.mult))
            done(nc.vector.scalar_tensor_tensor(var[:, :], dev[:, :], 0.25, var[:, :], ALU.mult, ALU.add))
            dve.sem_inc(s_var)
            dve.wait_ge(s_std, 1)
            done(nc.vector.reciprocal(rstd[:, :], rstd[:, :]))
            with dve.Fori(0, NTP // 2) as t:
                for h in range(2):
                    if rows_out is not None:
                        dve.wait_ge(s_out[h], 16 * t + 16)
                    dve.wait_ge(s_t, 2 * t + (h + 1))
                    nc.vector.tensor_scalar(y[:, h, :], x[:, bass.ds(2 * t + h, 1), :], mean[:, bass.ds(2 * t + h, 1)],
                                            rstd[:, bass.ds(2 * t + h, 1)], ALU.subtract, ALU.mult).then_inc(s_y, 1)

        @block.tensor
        def _(pe):
            pe.sem_inc(s_t, 2)
            with pe.Fori(0, NTP // 2) as t:
                for h in range(2):
                    pe.wait_ge(s_xt, 2 * t + (h + 1))
                    pe.wait_ge(s_y, 2 * t + (h + 1))
                    for k in range(2):
                        last = nc.tensor.transpose(p_t[:, h, k, 0:P], y[:, h, k * P:(k + 1) * P], c["ident"][:, :])
                    last.then_inc(s_t, 1)

        @block.scalar
        def _(act):
            act.wait_ge(s_var, 1)
            nc.scalar.activation(rstd[:, :], var[:, :], ACT.Sqrt).then_inc(s_std, 1)
            act.sem_inc(s_xt, 2)
            nc.scalar.mul(xt[:, :, NPAD:], c["ramp"][:, None, 0:2 * P].to_broadcast([P, 2, 2 * P]), 0.0)
            with act.Fori(0, NTP // 2) as t:
                for h in range(2):
                    act.wait_ge(s_t, 2 * t + (h + 3))
                    nc.scalar.copy(xt[:, :, bass.ds((2 * t + h) * P, P)], p_t[:, h, :, 0:P]).then_inc(s_xt, 1)


def project(nc, c, name, xt, weights, graphs):
    ctx = ExitStack()
    with ctx:
        sp_ = Space(nc, ctx, name)
        width = graphs[0]["width"]
        n_g = len(graphs)
        w = sp_.sb("w", [P, 2, n_g * width])
        att = sp_.sb("att", [P, 2, n_g * width])
        prod = sp_.sb("prod", [P, 2, n_g * width])
        rows = sp_.sb("rows", [P, 2, n_g, width + HEADS])
        scores = sp_.sb("scores", [P, 2, 2, n_g * HEADS])
        nodes = [sp_.sb(f"nodes{i}", [P, NTP, 2 * HEADS]) for i in range(n_g)]
        slot = sp_.sb("slot", [P, 2, 2, P])
        p_x = sp_.ps("p_x", [P, 2, 512])
        s_load, s_dve, s_x, s_scores, s_rows, s_fin, s_slot = (
            sp_.sem(n) for n in ("load", "dve", "x_ready", "scores", "rows", "fin", "slot"))
        s_out = [sp_.sem("out0"), sp_.sem("out1")]
        block = sp_.block()

        @block.sync
        def _(sp):
            for i, g in enumerate(graphs):
                for k in range(2):
                    sp.dma_start(w[:, k, i * width:(i + 1) * width], weights[i][k * P:(k + 1) * P, :]).then_inc(s_load, 16)
                for j, a in enumerate((g["a_dst"], g["a_src"])):
                    sp.dma_start(att[:, j, i * width:(i + 1) * width],
                                 a.rearrange("h c -> (h c)").partition_broadcast(P)).then_inc(s_load, 16)
            for h in range(2):
                sp.sem_inc(s_out[h], 16 * n_g)
            with sp.Fori(0, NTP // 2) as t:
                for h in range(2):
                    sp.wait_ge(s_scores, 2 * t + (h + 1))
                    for i, g in enumerate(graphs):
                        sp.dma_start(g["table"][bass.ds((2 * t + h) * P, P), :], rows[:, h, i, :]).then_inc(s_out[h], 16)
            for h in range(2):
                sp.wait_ge(s_out[h], 16 * n_g * (NTP // 2 + 1))
            for i, g in enumerate(graphs):
                sp.dma_start(g["nodes"], nodes[i][:, :, :]).then_inc(s_fin, 16)
            sp.wait_ge(s_fin, 16 * n_g)

        @block.tensor
        def _(pe):
            pe.wait_ge(s_load, 16 * 4 * n_g)
            with pe.Fori(0, NTP // 2) as t:
                for h in range(2):
                    pe.wait_ge(s_rows, 2 * t + (h + 1))
                    pe.wait_ge(s_slot, 2 * t + (h + 1))
                    for k in range(2):
                        last = nc.tensor.matmul(p_x[:, h, 0:n_g * width], slot[:, h, k, :],
                                                w[:, k, :], start=(k == 0), stop=(k == 1))
                    last.then_inc(s_x, 1)

        @block.scalar
        def _(act):
            act.sem_inc(s_rows, 2)
            for h in range(2):
                nc.scalar.copy(slot[:, h, :, :], xt[:, :, h * P:(h + 1) * P]).then_inc(s_slot, 1)
            with act.Fori(0, NTP // 2) as t:
                for h in range(2):
                    act.wait_ge(s_out[h], 16 * n_g * t + 16 * n_g)
                    act.wait_ge(s_x, 2 * t + (h + 1))
                    last = nc.scalar.copy(rows[:, h, :, 0:width],
                                          p_x[:, h, 0:n_g * width].rearrange("p (g c) -> p g c", g=n_g))
                    last.then_inc(s_rows, 1)
                    nc.scalar.copy(slot[:, h, :, :],
                                   xt[:, :, bass.ds((2 * t + (h + 2)) * P, P)]).then_inc(s_slot, 1)

        @block.vector
        def _(dve):
            done = Chain(dve, s_dve)
            dve.wait_ge(s_load, 16 * 4 * n_g)
            with dve.Fori(0, NTP // 2) as t:
                done.enter(t, 2 * 4)
                for h in range(2):
                    dve.wait_ge(s_rows, 2 * t + (h + 3))
                    for j in range(2):
                        done.mark(nc.vector.tensor_tensor(
                            prod[:, j, :].rearrange("p (g c) -> p g c", g=n_g), rows[:, h, :, 0:width],
                            att[:, j, :].rearrange("p (g c) -> p g c", g=n_g), ALU.mult))
                    done.wait()
                    for j in range(2):
                        done.mark(nc.vector.tensor_reduce(
                            scores[:, h, j, :], prod[:, j, :].rearrange("p (g c) -> p g c", g=n_g * HEADS),
                            axis=AX.X, op=ALU.add))
                    done.wait()
                    dve.wait_ge(s_out[h], 16 * n_g * t + 16 * n_g)
                    for i in range(n_g):
                        nc.vector.tensor_copy(
                            nodes[i][:, bass.ds(2 * t + h, 1), :].rearrange("p a (j e) -> p (a j) e", j=2),
                            scores[:, h, :, i * HEADS:(i + 1) * HEADS])
                        last = nc.vector.tensor_copy(rows[:, h, i, width:], scores[:, h, 1, i * HEADS:(i + 1) * HEADS])
                    last.then_inc(s_scores, 1)
                done.leave(NTP // 2)


def turns_of(eng, node_i, s, which=TURNS_ALL):
    at = CHUNKS[s] * P + which
    least = (BESIDE + 1 if s == 2 else 1) - (which == LAST_TURN)
    return eng.value_load(node_i[0:1, at:at + 1], min_val=least, max_val=ITEMS[s] // ROUND)


def attend_pass(nc, c, name, width, tables, local_rows, node_rows, gather=None, add=None, experts=None):
    ctx = ExitStack()
    with ctx:
        sp_ = Space(nc, ctx, name)
        w, m, ch = width + HEADS, width + 2 * HEADS + 1, width // HEADS
        if gather:
            s, table, nodes_in, rows_out, al, ard = gather
            cols = CHUNKS[s] * P
            pay = sp_.sb("pay", [P, cols], I32)
            node_g = sp_.sb("node_g", [1, cols + EXTRA], I32)
            nodes = sp_.sb("nodes", [P, NTP, 2 * HEADS])
            index = sp_.sb("index", [P, 2, GRP], I32)
            got = sp_.sb("got", [P, 2, GRP, w])
            local_r = sp_.sb("local_r", [P, 2, GRP * P])
            spread = sp_.sb("spread", [P, 2, GRP * P])
            mine = sp_.sb("mine", [P, 2, PAIRS, 2 * HEADS])
            p_ard = sp_.ps("p_ard", [P, 2, 512])
        if add:
            s_a, rows_in, weights, acc = add
            s, cols = (s, cols) if gather else (s_a, CHUNKS[s_a] * P)
            local_c = sp_.sb("local_c", [P, cols], I32)
            node_a = sp_.sb("node_a", [1, cols + EXTRA], I32)
            kept = sp_.sb("kept", [P, 2, GRP, w])
            hot = sp_.sb("hot", [P, 2, GRP, P])
            msg = sp_.sb("msg", [P, 2, GRP, m])
            p_sum = sp_.ps("p_sum", [P, PAIRS, 512])
        ring = add and not gather
        if ring:
            running = sp_.sb("running", [P, 2, PAIRS, m])
            tile_f = sp_.sb("tile_f", [P, cols], I32)
            same = sp_.sb("same", [P, cols // 2])
        ffn = GatedExperts(nc, c, sp_, *experts) if experts else None

        def each_turn(eng, turns, body):
            if not ffn:
                with eng.Fori(0, turns) as t:
                    for h in range(2):
                        body(t, h, None)
                return
            with eng.Fori(0, BESIDE // 2) as n:
                for e in range(NEXP):
                    body(2 * n + e // 2, e % 2, (n, e))
            with eng.Fori(BESIDE, turns) as t:
                for h in range(2):
                    body(t, h, None)
        bank = lambda h, j: p_sum[:, h * PAIRS // 2 + j // 2:h * PAIRS // 2 + j // 2 + 1, j % 2 * 256:j % 2 * 256 + m]
        s_load, s_zero, s_index, s_turn, s_kept, s_spread, s_sfree, s_ard, s_pfree, s_mine = (
            sp_.sem(n) for n in ("load", "zero", "index", "turn", "kept", "spread", "sfree", "ard", "pfree", "mine"))
        s_acc, s_mfree, s_hot, s_side, s_sum, s_ran, s_stored = (
            sp_.sem(n) for n in ("acc", "mfree", "hot", "side", "sum", "ran", "stored"))
        s_local, s_out, s_rows = ([sp_.sem(f"{n}{h}") for h in range(2)] for n in ("local", "out", "rows"))
        s_got = [sp_.gathered(0), sp_.gathered(1)] if gather else None
        LOADS = 16 * (3 * bool(gather) + 2 * bool(add) + bool(ring))
        MOST_TURNS = ITEMS[s] // ROUND

        def turns_for(eng, which=TURNS_ALL):
            eng.wait_ge(s_load, LOADS)
            if s < 2:
                return MOST_TURNS - (which == LAST_TURN)
            return turns_of(eng, node_g if gather else node_a, s, which)

        def node_tiles(eng, node_i, t, h):
            return [eng.value_load(node_i[0:1, bass.ds((2 * t + h) * GRP + 2 * j, 1)], min_val=0, max_val=NT - 1)
                    for j in range(PAIRS)]
        block = sp_.block()

        @block.sync
        def _(sp):
            if gather:
                sp.dma_start(pay[:, :], tables[s][0, :, :]).then_inc(s_load, 16)
                sp.dma_start(node_g[:, :], node_rows[s]).then_inc(s_load, 16)
                sp.dma_start(nodes[:, :, :], nodes_in).then_inc(s_load, 16)
            if add:
                sp.dma_start(local_c[:, :], tables[s_a][2, :, :]).then_inc(s_load, 16)
                sp.dma_start(node_a[:, :], node_rows[s_a]).then_inc(s_load, 16)
            if ring:
                sp.dma_start(tile_f[:, :], tables[s_a][3, :, :]).then_inc(s_load, 16)
            turns = turns_for(sp)
            if ffn:
                ffn.load(sp)

            def body(t, h, beside):
                if add:
                    sp.wait_ge(s_hot, 2 * t + (h + 1))
                    sp.dma_start(kept[:, h, :, :], rows_in[bass.ds(2 * t + h, 1), :, :]).then_inc(s_rows[h], 16)
                if gather:
                    sp.wait_ge(s_spread, 2 * t + (h + 1))
                    sp.dma_start(local_r[:, h, :], local_rows[s][bass.ds((2 * t + h) * GRP, GRP), :]
                                 .rearrange("i e -> (i e)").partition_broadcast(P)).then_inc(s_local[h], 16)
                if beside:
                    ffn.store(sp, *beside)
            each_turn(sp, turns, body)
            if ffn:
                ffn.stored(sp)

        @block.gpsimd
        def _(pool):
            if not gather:
                return
            turns = turns_for(pool)

            def body(t, h, beside):
                pool.wait_ge(s_index, 2 * t + (h + 1))
                pool.wait_ge(s_kept, 2 * t + (h + 1))
                pool.wait_ge(s_out[h], 16 * t + 16)
                pool.sem_inc(s_turn)
                for i in range(GRP):
                    pool.indirect_dma_start(
                        out=got[:, h, i, :], out_offset=None, in_=table[:, :],
                        in_offset=bass.IndirectOffsetOnAxis(ap=index[:, h, i:i + 1], axis=0)).then_inc(s_got[h], 16)
            each_turn(pool, turns, body)

        @block.scalar
        def _(act):
            turns = turns_for(act)
            if gather:
                act.wait_ge(s_zero, 2)
                for h in range(2):
                    act.sem_inc(s_out[h], 16)
                    nc.scalar.copy(index[:, h, :], pay[:, h * GRP:(h + 1) * GRP]).then_inc(s_index, 1)
                act.sem_inc(s_pfree, 2)
                act.sem_inc(s_kept, 2)

            def side(t, h):
                act.wait_ge(s_mfree, 2 * t + (h + 1))
                nc.scalar.copy(msg[:, h, :, width:width + 2 * HEADS],
                               weights[:, bass.ds((2 * t + h) * GRP, GRP), :]).then_inc(s_side, 1)

            if ring:
                side(0, 0)
                side(0, 1)
            if ffn:
                ffn.start(act)

            def body(t, h, beside):
                if ring:
                    tiles = node_tiles(act, node_a, t, h)
                    for j in range(PAIRS):
                        act.wait_ge(s_ran, (2 * t + h) * PAIRS + (j + 1))
                        act.wait_ge(s_stored, (2 * t + h) * PAIRS + (j + 2 * PAIRS))
                        nc.scalar.copy(acc[:, bass.ds(tiles[j], 1), :], running[:, h, j:j + 1, :]).then_inc(s_stored, 1)
                    side(t + 1, h)
                    return
                if add:
                    side(t, h)
                if beside:
                    ffn.gelu(act, *beside)
                tiles = node_tiles(act, node_g, t, h)
                act.wait_ge(s_sfree, 2 * t + (h + 1))
                for j in range(PAIRS):
                    last = nc.scalar.copy(mine[:, h, j:j + 1, :], nodes[:, bass.ds(tiles[j], 1), :])
                last.then_inc(s_mine, 1)
                act.wait_ge(s_got[h], 16 * GRP * t + 16 * GRP)
                nc.scalar.copy(index[:, h, :], pay[:, bass.ds((2 * t + h + 2) * GRP, GRP)]).then_inc(s_index, 1)
                act.dma_start(rows_out[bass.ds(2 * t + h, 1), :, :], got[:, h, :, :]).then_inc(s_out[h], 16)
                nc.scalar.copy(al[:, bass.ds((2 * t + h) * GRP, GRP), :], got[:, h, :, width:]).then_inc(s_kept, 1)
                act.wait_ge(s_ard, 2 * t + (h + 1))
                nc.scalar.copy(ard[:, bass.ds((2 * t + h) * GRP, GRP), :],
                               p_ard[:, h, 0:GRP * 2 * HEADS].rearrange("p (i e) -> p i e", i=GRP)).then_inc(s_pfree, 1)
            each_turn(act, turns, body)
            for h in range(2) if gather else ():
                act.wait_ge(s_out[h], 16 * turns + 16)
                act.sem_inc(s_turn)

        @block.tensor
        def _(pe):
            turns = turns_for(pe)
            if gather:
                pe.sem_inc(s_sfree, 2)
            if ffn:
                ffn.ready(pe)

            def body(t, h, beside):
                if add:
                    pe.wait_ge(s_hot, 2 * t + (h + 3))
                    pe.wait_ge(s_side, 2 * t + (h + 1))
                    for j in range(PAIRS):
                        for i in (2 * j, 2 * j + 1):
                            last = nc.tensor.matmul(bank(h, j), hot[:, h, i, :], msg[:, h, i, :],
                                                    start=(i == 2 * j), stop=(i > 2 * j))
                        last.then_inc(s_sum, 1)
                if beside:
                    ffn.products(pe, *beside)
                if gather:
                    pe.wait_ge(s_mine, 2 * t + (h + 1))
                    pe.wait_ge(s_pfree, 2 * t + (h + 1))
                    pe.wait_ge(s_spread, 2 * t + (h + 3))
                    for i in range(GRP):
                        last = nc.tensor.matmul(p_ard[:, h, i * 8:(i + 1) * 8], spread[:, h, i * P:(i + 1) * P],
                                                mine[:, h, i // 2, :], start=True, stop=True)
                    last.then_inc(s_ard, 1)
                    pe.wait_ge(s_ard, 2 * t + (h + 1))
                    pe.sem_inc(s_sfree)
            each_turn(pe, turns, body)

        @block.vector
        def _(dve):
            v = nc.vector
            done = Chain(dve, s_acc)
            if gather:
                v.memset(al[:, :, :], 0.0).then_inc(s_zero, 1)
                v.memset(ard[:, :, :], 0.0).then_inc(s_zero, 1)
                dve.wait_ge(s_zero, 2)
                dve.sem_inc(s_spread, 2)
            if add:
                done.mark(v.memset(acc[:, :, :], 0.0))
                if ring:
                    done.mark(v.memset(running[:, :, :, :], 0.0))
                    done.mark(v.memset(same[:, 0:1], 0.0))
                done(v.memset(msg[:, :, :, :], 1.0))
                dve.sem_inc(s_mfree, 2)
                dve.sem_inc(s_hot, 2)
            turns = turns_for(dve)
            if ring:
                f = tile_f[:, :].bitcast(F32)
                done(v.tensor_tensor(same[:, 1:], f[:, 2::2], f[:, 0:cols - 2:2], ALU.is_equal))
                dve.sem_inc(s_stored, 2 * PAIRS)

            def spread_out(t, h):
                dve.wait_ge(s_local[h], 16 * t + 16)
                dve.wait_ge(s_sfree, 2 * t + (h + 1))
                v.tensor_scalar(spread[:, h, :], local_r[:, h, :], c["part"][:, 0:1], None, ALU.is_equal).then_inc(s_spread, 1)

            def messages(t, h):
                at = bass.ds((2 * t + h) * GRP, GRP)
                dve.wait_ge(s_mfree, 2 * t + (h + 1))
                v.tensor_tensor(hot[:, h, :, :], c["ramp"][:, None, 0:P].to_broadcast([P, GRP, P]),
                                local_c[:, at].bitcast(F32)[:, :, None].to_broadcast([P, GRP, P]), ALU.is_equal)
                dve.wait_ge(s_rows[h], 16 * t + 16)
                for e in range(HEADS):
                    last = v.tensor_tensor(msg[:, h, :, e * ch:(e + 1) * ch], kept[:, h, :, e * ch:(e + 1) * ch],
                                           weights[:, at, e:e + 1].to_broadcast([P, GRP, ch]), ALU.mult)
                last.then_inc(s_hot, 1)

            def add_half(t, h):
                if ring:
                    dve.wait_ge(s_stored, (2 * t + h) * PAIRS + PAIRS)
                    for j in range(PAIRS):
                        if j % 2 == 0:
                            dve.wait_ge(s_sum, (2 * t + h) * PAIRS + (j + 2))
                        before = running[:, h, j - 1:j, :] if j else running[:, 1 - h, PAIRS - 1:, :]
                        ran(v.scalar_tensor_tensor(running[:, h, j:j + 1, :], before,
                                                   same[:, bass.ds((2 * t + h) * PAIRS + j, 1)], bank(h, j),
                                                   ALU.mult, ALU.add))
                    dve.sem_inc(s_mfree)
                    return
                tiles = node_tiles(dve, node_a, t, h)
                for j in range(PAIRS):
                    if j % 2 == 0:
                        dve.wait_ge(s_sum, (2 * t + h) * PAIRS + (j + 2))
                    to = acc[:, bass.ds(tiles[j], 1), :]
                    done(v.tensor_tensor(to, to, bank(h, j), ALU.add))
                dve.sem_inc(s_mfree)

            if not add:
                def body(t, h, beside):
                    spread_out(t, h)
                    if beside:
                        ffn.take(dve, *beside)
                if ffn:
                    ffn.free(dve)
                each_turn(dve, turns, body)
                return
            messages(0, 0)
            messages(0, 1)
            last_turn = turns_for(dve, LAST_TURN)
            ran = Chain(dve, s_ran)
            if ring:
                done = ran
            with dve.Fori(0, last_turn) as t:
                done.enter(t, 2 * PAIRS)
                for h in range(2):
                    if gather:
                        spread_out(t, h)
                    add_half(t, h)
                    messages(t + 1, h)
            done.enter_last(last_turn)
            for h in range(2):
                if gather:
                    spread_out(last_turn, h)
                add_half(last_turn, h)


def attend_weights(nc, c, name, s, tables, al, ard):
    ctx = ExitStack()
    with ctx:
        sp_ = Space(nc, ctx, name)
        ch = CHUNKS[s]
        cols = ch * P
        key = sp_.sb("key", [P, cols], I32)
        local = sp_.sb("local", [P, cols], I32)
        valid = sp_.sb("valid", [P, cols])
        gid = sp_.sb("gid", [P, cols])
        masked = sp_.sb("masked", [P, cols])
        line = [sp_.sb(f"line{i}", [P, cols]) for i in range(HEADS + 1)]
        begin, end = sp_.sb("begin", [P, cols]), sp_.sb("end", [P, cols])
        fwd, bwd = sp_.sb("fwd", [P, cols]), sp_.sb("bwd", [P, cols])
        ends = sp_.sb("ends", [P, 4, HEADS])
        row = sp_.sb("row", [HEADS, 4, P])
        same, whole, step = (sp_.sb(n, [HEADS, P + 1]) for n in ("same", "whole", "step"))
        chain = sp_.sb("chain", [HEADS, 2, P + 2])
        carry_row = sp_.sb("carry_row", [HEADS, 2, P])
        carry = sp_.sb("carry", [P, 2, HEADS])
        top = sp_.sb("top", [P, cols, HEADS])
        p_line = sp_.ps("p_line", [P, 3, 512])
        p_row = sp_.ps("p_row", [P, 512])
        s_load, s_dve, s_in, s_flip, s_copied, s_ends, s_row, s_carry, s_carried, s_exp = (
            sp_.sem(n) for n in ("load", "dve", "in", "flip", "copied", "ends", "row", "carry", "carried", "exp"))
        block = sp_.block()
        bank = lambda i: p_line[:, i // 3, i % 3 * P:(i % 3 + 1) * P]

        @block.sync
        def _(sp):
            sp.dma_start(key[:, :], tables[s][1, :, :]).then_inc(s_load, 16)
            sp.dma_start(local[:, :], tables[s][2, :, :]).then_inc(s_load, 16)

        @block.tensor
        def _(pe):
            for a in range(HEADS + 1):
                pe.wait_ge(s_in, a + 1)
                src = gid if a == 0 else masked
                for i in range(ch):
                    last = nc.tensor.transpose(bank(i), src[:, i::ch], c["ident"][:, :])
                last.then_inc(s_flip, 1)
            pe.wait_ge(s_ends, 1)
            for j in range(4):
                last = nc.tensor.transpose(p_row[0:HEADS, j * P:(j + 1) * P], ends[:, j, :], c["ident"][:, :])
            last.then_inc(s_row, 1)
            pe.wait_ge(s_carry, 1)
            for j in range(2):
                last = nc.tensor.transpose(p_row[:, j * HEADS:(j + 1) * HEADS], carry_row[:, j, :],
                                           c["ident"][0:HEADS, 0:HEADS])
            last.then_inc(s_carried, 1)
            for a in range(HEADS):
                pe.wait_ge(s_in, HEADS + 2 + a)
                for i in range(ch):
                    last = nc.tensor.transpose(bank(i), line[a + 1][:, i * P:(i + 1) * P], c["ident"][:, :])
                last.then_inc(s_flip, 1)

        @block.scalar
        def _(act):
            act.wait_ge(s_exp, 1)
            nc.scalar.activation(ard[:, :, :], ard[:, :, :], ACT.Exp).then_inc(s_exp, 1)

        @block.vector
        def _(dve):
            done = Chain(dve, s_dve)
            v = nc.vector
            dve.wait_ge(s_load, 32)
            loc, k = local[:, :].bitcast(F32), key[:, :].bitcast(F32)
            done(v.tensor_scalar(gid[:, :], loc, 0.0, None, ALU.is_ge))
            done(v.scalar_tensor_tensor(valid[:, :], loc, float(P), gid[:, :], ALU.is_lt, ALU.mult))
            done(v.scalar_tensor_tensor(gid[:, :], k, 1.0, valid[:, :], ALU.add, ALU.mult))
            dve.sem_inc(s_in)
            for a in range(HEADS + 1):
                if a:
                    done(v.tensor_tensor(masked[:, :], al[:, :, a - 1], valid[:, :], ALU.mult))
                    done(v.tensor_scalar(bwd[:, :], valid[:, :], BIG, -BIG, ALU.mult, ALU.add))
                    done(v.tensor_tensor(masked[:, :], masked[:, :], bwd[:, :], ALU.add))
                    dve.sem_inc(s_in)
                dve.wait_ge(s_flip, a + 1)
                full = ch // 3 * 3
                done.mark(v.tensor_copy(line[a][:, 0:full * P].rearrange("p (b e) -> p b e", b=ch // 3),
                                        p_line[:, 0:ch // 3, 0:3 * P]))
                if ch % 3:
                    done.mark(v.tensor_copy(line[a][:, full * P:], p_line[:, ch // 3, 0:ch % 3 * P]))
                done.wait()
            g = line[0]
            done(v.tensor_tensor(begin[:, 1:], g[:, 1:], g[:, 0:cols - 1], ALU.not_equal))
            done.mark(v.memset(end[:, cols - 1:], 0.0))
            done.mark(v.tensor_scalar(end[:, 0:cols - 1], begin[:, 1:], -BIG, None, ALU.mult))
            done.mark(v.memset(begin[:, 0:1], 0.0))
            done(v.tensor_scalar(begin[:, 1:], begin[:, 1:], -BIG, None, ALU.mult))
            for h in range(HEADS):
                done(v.tensor_tensor_scan(fwd[:, :], begin[:, :], line[h + 1][:, :], -BIG, ALU.add, ALU.max))
                done(v.tensor_tensor_scan(bwd[:, ::-1], end[:, ::-1], line[h + 1][:, ::-1], -BIG, ALU.add, ALU.max))
                done.mark(v.tensor_copy(ends[:, 0, h:h + 1], fwd[:, cols - 1:]))
                done.mark(v.tensor_copy(ends[:, 1, h:h + 1], bwd[:, 0:1]))
                done.mark(v.tensor_copy(ends[:, 2, h:h + 1], g[:, 0:1]))
                done(v.tensor_copy(ends[:, 3, h:h + 1], g[:, cols - 1:]))
            dve.sem_inc(s_ends)
            dve.wait_ge(s_row, 1)
            done.mark(v.tensor_copy(row[:, :, :], p_row[0:HEADS, :].rearrange("p (j q) -> p j q", j=4)))
            done.mark(v.memset(same[:, :], 0.0))
            done(v.memset(chain[:, :, :], -BIG))
            done.mark(v.tensor_tensor(same[:, 1:P], row[:, 2, 1:], row[:, 3, 0:P - 1], ALU.is_equal))
            done(v.tensor_tensor(whole[:, 0:P], row[:, 2, :], row[:, 3, :], ALU.is_equal))
            for j in range(2):
                nxt = same[:, 0:P] if j == 0 else same[:, 1:P + 1]
                done(v.tensor_tensor(step[:, 0:P], whole[:, 0:P], nxt, ALU.mult))
                done(v.tensor_scalar(step[:, 0:P], step[:, 0:P], BIG, -BIG, ALU.mult, ALU.add))
                if j == 0:
                    done(v.tensor_tensor_scan(chain[:, 0, 1:P + 1], step[:, 0:P], row[:, 0, :], -BIG, ALU.add, ALU.max))
                    prev = chain[:, 0, 0:P]
                else:
                    done(v.tensor_tensor_scan(chain[:, 1, 1:P + 1][:, ::-1], step[:, 0:P][:, ::-1], row[:, 1, ::-1], -BIG,
                                              ALU.add, ALU.max))
                    prev = chain[:, 1, 2:P + 2]
                done(v.tensor_scalar(step[:, 0:P], nxt, BIG, -BIG, ALU.mult, ALU.add))
                done(v.tensor_tensor(carry_row[:, j, :], prev, step[:, 0:P], ALU.add))
            dve.sem_inc(s_carry)
            dve.wait_ge(s_carried, 1)
            done(v.tensor_copy(carry[:, :, :], p_row[:, 0:2 * HEADS].rearrange("p (j h) -> p j h", j=2)))
            for h in range(HEADS):
                done.mark(v.tensor_tensor_scan(fwd[:, :], begin[:, :], line[h + 1][:, :], carry[:, 0, h:h + 1],
                                               ALU.add, ALU.max))
                done(v.tensor_tensor_scan(bwd[:, ::-1], end[:, ::-1], line[h + 1][:, ::-1], carry[:, 1, h:h + 1],
                                          ALU.add, ALU.max))
                done(v.tensor_tensor(line[h + 1][:, :], fwd[:, :], bwd[:, :], ALU.max))
                dve.sem_inc(s_in)
                dve.wait_ge(s_flip, HEADS + 2 + h)
                for i in range(ch):
                    done.mark(v.tensor_copy(top[:, i::ch, h], bank(i)))
                done.wait()
            d_score, s_score = ard[:, :, 0:HEADS], ard[:, :, HEADS:]
            done(v.tensor_tensor(top[:, :, :], top[:, :, :], s_score, ALU.max))
            done(v.tensor_tensor(top[:, :, :], top[:, :, :], d_score, ALU.add))
            done.mark(v.tensor_tensor(s_score, s_score, d_score, ALU.add))
            done(v.tensor_tensor(d_score, al[:, :, :], d_score, ALU.add))
            for x in (top[:, :, :], ard[:, :, :]):
                done.mark(v.scalar_tensor_tensor(x, x, 0.2, x, ALU.mult, ALU.max))
            done.wait()
            done.mark(v.tensor_tensor(d_score, d_score, top[:, :, :], ALU.subtract))
            done(v.tensor_tensor(s_score, s_score, top[:, :, :], ALU.subtract))
            done(v.tensor_tensor(ard[:, :, :], ard[:, :, :],
                                 valid[:, :, None].to_broadcast([P, cols, 2 * HEADS]), ALU.mult))
            dve.sem_inc(s_exp)
            dve.wait_ge(s_exp, 2)


def attend_finish(nc, c, name, width, table, bias, acc, out, counts):
    ctx = ExitStack()
    with ctx:
        sp_ = Space(nc, ctx, name)
        w, m, ch = width + HEADS, width + 2 * HEADS + 1, width // HEADS
        own = sp_.sb("own", [P, NTP, w])
        bias_b = sp_.sb("bias", [P, width])
        has, inv, cnt = (sp_.sb(n, [P, NTP]) for n in ("has", "inv", "cnt"))
        w_own, den = sp_.sb("w_own", [P, NTP, HEADS]), sp_.sb("den", [P, NTP, HEADS])
        s_load, s_dve, s_out, s_fin = (sp_.sem(n) for n in ("load", "dve", "out", "fin"))
        block = sp_.block()

        @block.sync
        def _(sp):
            sp.dma_start(own[:, :, :], table.rearrange("(t p) c -> p t c", p=P)).then_inc(s_load, 16)
            sp.dma_start(bias_b[:, :], bias.partition_broadcast(P)).then_inc(s_load, 16)
            sp.wait_ge(s_out, 1)
            sp.dma_start(out.rearrange("(t p) c -> p t c", p=P), acc[:, :, 0:width]).then_inc(s_fin, 16)
            sp.dma_start(counts, cnt[:, :]).then_inc(s_fin, 16)
            sp.wait_ge(s_fin, 32)

        @block.vector
        def _(dve):
            v = nc.vector
            done = Chain(dve, s_dve)
            done(v.tensor_copy(cnt[:, :], acc[:, :, m - 1]))
            done.mark(v.tensor_scalar(has[:, :], cnt[:, :], 1.0, None, ALU.min))
            done(v.tensor_scalar(inv[:, :], cnt[:, :], 1.0, None, ALU.max))
            done.mark(v.reciprocal(inv[:, :], inv[:, :]))
            done(v.tensor_scalar(has[:, :], has[:, :], -1.0, 1.0, ALU.mult, ALU.add))
            done(v.tensor_tensor(w_own[:, :, :], acc[:, :, width + HEADS:width + 2 * HEADS],
                                 inv[:, :, None].to_broadcast([P, NTP, HEADS]), ALU.mult))
            done(v.tensor_tensor(w_own[:, :, :], w_own[:, :, :], has[:, :, None].to_broadcast([P, NTP, HEADS]), ALU.add))
            done(v.scalar_tensor_tensor(den[:, :, :], w_own[:, :, :], 1e-16, acc[:, :, width:width + HEADS],
                                        ALU.add, ALU.add))
            done(v.reciprocal(den[:, :, :], den[:, :, :]))
            dve.wait_ge(s_load, 32)
            for e in range(HEADS):
                o, a = own[:, :, e * ch:(e + 1) * ch], acc[:, :, e * ch:(e + 1) * ch]
                done(v.tensor_tensor(o, o, w_own[:, :, e:e + 1].to_broadcast([P, NTP, ch]), ALU.mult))
                done(v.tensor_tensor(a, a, o, ALU.add))
                done(v.tensor_tensor(a, a, den[:, :, e:e + 1].to_broadcast([P, NTP, ch]), ALU.mult))
            done(v.tensor_tensor(acc[:, :, 0:width], acc[:, :, 0:width],
                                 bias_b[:, None, :].to_broadcast([P, NTP, width]), ALU.add))
            dve.sem_inc(s_out)


def both_attentions(nc, c, lists, wide, scores, biases, kept, att, counts):
    tables, local_rows, node_rows = lists
    cols, m = CHUNKS[0] * P, HC + 2 * HEADS + 1
    gather = lambda s, al, ard: (s, wide[s], scores[s], kept[s], al, ard)
    ctx = ExitStack()
    with ctx:
        ard1 = Space(nc, ctx, "att1").sb("ard", [P, cols, 2 * HEADS])
        inner = ExitStack()
        with inner:
            al1 = Space(nc, inner, "att1").sb("al", [P, cols, HEADS])
            first = ExitStack()
            with first:
                ard0 = Space(nc, first, "att0").sb("ard", [P, cols, 2 * HEADS])
                scores0 = ExitStack()
                with scores0:
                    al0 = Space(nc, scores0, "att0").sb("al", [P, cols, HEADS])
                    attend_pass(nc, c, "att0g", HC, *lists, gather=gather(0, al0, ard0))
                    attend_weights(nc, c, "att0w", 0, tables, al0, ard0)
                acc0 = Space(nc, first, "att0").sb("acc", [P, NTP, m])
                attend_pass(nc, c, "att01", HC, *lists, gather=gather(1, al1, ard1), add=(0, kept[0], ard0, acc0))
                attend_finish(nc, c, "att0f", HC, wide[0], biases[0], acc0, att[0], counts[0])
            attend_weights(nc, c, "att1w", 1, tables, al1, ard1)
        acc1 = Space(nc, ctx, "att1").sb("acc", [P, NTP, m])
        attend_pass(nc, c, "att1s", HC, *lists, add=(1, kept[1], ard1, acc1))
        attend_finish(nc, c, "att1f", HC, wide[1], biases[1], acc1, att[1], counts[1])


def pad_rows(nc, x, x_out):
    ctx = ExitStack()
    with ctx:
        sp_ = Space(nc, ctx, "pad")
        rows = sp_.sb("rows", [P, NTP, D])
        s_zero, s_load, s_out = (sp_.sem(n) for n in ("zero", "load", "out"))
        whole = N // P
        block = sp_.block()

        @block.vector
        def _(dve):
            nc.vector.memset(rows[:, whole:, :], 0.0).then_inc(s_zero, 1)

        @block.sync
        def _(sp):
            sp.dma_start(rows[:, 0:whole, :], x[0:whole * P, :].rearrange("(t p) d -> p t d", p=P)).then_inc(s_load, 16)
            sp.wait_ge(s_zero, 1)
            sp.dma_start(rows[0:N - whole * P, whole, :], x[whole * P:N, :]).then_inc(s_load, 16)
            sp.wait_ge(s_load, 32)
            sp.dma_start(x_out.rearrange("(t p) d -> p t d", p=P), rows[:, :, :]).then_inc(s_out, 16)
            sp.wait_ge(s_out, 16)


def rows_product(nc, c, name, rows_in, w_in, out, tiles, bn=None, x_in=None):
    ctx = ExitStack()
    with ctx:
        sp_ = Space(nc, ctx, name)
        part = D // len(rows_in)
        G = 5
        turns = tiles // (2 * G)
        w = sp_.sb("w", [P, 2, D])
        rows = sp_.sb("rows", [P, 2, G, D])
        x = sp_.sb("x", [P, 2, G, D])
        rows_t = sp_.sb("rows_t", [P, 2, 2, P])
        y = sp_.sb("y", [P, 2, G, D])
        par = sp_.sb("par", [P, 5, D])
        scale, shift = sp_.sb("scale", [P, D]), sp_.sb("shift", [P, D])
        p_t = sp_.ps("p_t", [P, 2, 512])
        p_y = sp_.ps("p_y", [P, G, 512])
        s_w, s_dve, s_std, s_t, s_rt, s_m, s_y, s_done = (
            sp_.sem(n) for n in ("w", "dve", "std", "t", "rt", "m", "y", "done"))
        s_in, s_out = ([sp_.sem(f"{n}{h}") for h in range(2)] for n in ("in", "out"))
        n_in = 16 * (len(rows_in) + (bn is not None))
        n_w = 16 * (2 + 5 * (bn is not None))
        block = sp_.block()

        @block.sync
        def _(sp):
            for k in range(2):
                sp.dma_start(w[:, k, :], w_in[k * P:(k + 1) * P, :]).then_inc(s_w, 16)
            if bn is not None:
                for i, a in enumerate(bn):
                    sp.dma_start(par[:, i, :], a.partition_broadcast(P)).then_inc(s_w, 16)

            def load(t, h):
                at = bass.ds((2 * t + h) * G * P, G * P)
                for i, a in enumerate(rows_in):
                    sp.dma_start(rows[:, h, :, i * part:(i + 1) * part],
                                 a[at, :].rearrange("(g p) d -> p g d", p=P)).then_inc(s_in[h], 16)
                if bn is not None:
                    sp.dma_start(x[:, h, :, :], x_in[at, :].rearrange("(g p) d -> p g d", p=P)).then_inc(s_in[h], 16)

            def store(t, h):
                sp.wait_ge(s_done, 2 * t + (h + 1))
                sp.dma_start(out[bass.ds((2 * t + h) * G * P, G * P), :].rearrange("(g p) d -> p g d", p=P),
                             y[:, h, :, :]).then_inc(s_out[h], 16)
            for h in range(2):
                sp.sem_inc(s_out[h], 16)
                load(0, h)
            with sp.Fori(0, turns - 1) as t:
                for h in range(2):
                    store(t, h)
                    load(t + 1, h)
            for h in range(2):
                store(turns - 1, h)
            for h in range(2):
                sp.wait_ge(s_out[h], 16 * turns + 16)

        @block.tensor
        def _(pe):
            pe.wait_ge(s_w, n_w)
            with pe.Fori(0, turns) as t:
                for q in range(2 * G + 1):
                    if q < 2 * G:
                        h, i = q // G, q % G
                        if i == 0:
                            pe.wait_ge(s_in[h], n_in * t + n_in)
                        pe.wait_ge(s_rt, 2 * G * t + (q + 1))
                        for k in range(2):
                            last = nc.tensor.transpose(p_t[:, q % 2, k * P:(k + 1) * P], rows[:, h, i, k * P:(k + 1) * P],
                                                       c["ident"][:, :])
                        last.then_inc(s_t, 1)
                    if q:
                        n = q - 1
                        pe.wait_ge(s_rt, 2 * G * t + (n + 3))
                        pe.wait_ge(s_y, 2 * G * t + (n + 1))
                        for k in range(2):
                            last = nc.tensor.matmul(p_y[:, n % G, 0:D], rows_t[:, n % 2, k, :], w[:, k, :],
                                                    start=(k == 0), stop=(k == 1))
                        last.then_inc(s_m, 1)

        @block.scalar
        def _(act):
            if bn is not None:
                act.wait_ge(s_dve, 1)
                nc.scalar.activation(scale[:, :], shift[:, :], ACT.Sqrt).then_inc(s_std, 1)
            act.sem_inc(s_rt, 2)
            with act.Fori(0, turns) as t:
                for q in range(2 * G):
                    act.wait_ge(s_t, 2 * G * t + (q + 1))
                    nc.scalar.copy(rows_t[:, q % 2, :, :], p_t[:, q % 2, 0:D].rearrange("p (k e) -> p k e", k=2)).then_inc(s_rt, 1)

        @block.vector
        def _(dve):
            v = nc.vector
            done = Chain(dve, s_dve)
            dve.sem_inc(s_y, G)
            if bn is not None:
                b_fuse, gamma, beta, mean, var = (par[:, i, :] for i in range(5))
                dve.wait_ge(s_w, n_w)
                done(v.tensor_scalar(shift[:, :], var, EPS, None, ALU.add))
                dve.wait_ge(s_std, 1)
                done(v.reciprocal(scale[:, :], scale[:, :]))
                done.mark(v.tensor_tensor(shift[:, :], b_fuse, mean, ALU.subtract))
                done(v.tensor_tensor(scale[:, :], scale[:, :], gamma, ALU.mult))
                done(v.tensor_tensor(shift[:, :], shift[:, :], scale[:, :], ALU.mult))
                done(v.tensor_tensor(shift[:, :], shift[:, :], beta, ALU.add))
            with dve.Fori(0, turns) as t:
                done.enter(t, 2 if bn is not None else 0)
                for h in range(2):
                    dve.wait_ge(s_out[h], 16 * t + 16)
                    for i in range(G):
                        dve.wait_ge(s_m, 2 * G * t + (G * h + i + 1))
                        if bn is None:
                            v.tensor_copy(y[:, h, i, :], p_y[:, i, 0:D]).then_inc(s_y, 1)
                        else:
                            v.tensor_tensor(y[:, h, i, :], p_y[:, i, 0:D], scale[:, :], ALU.mult).then_inc(s_y, 1)
                    dve.wait_ge(s_y, 2 * G * t + (G * h + 2 * G))
                    if bn is not None:
                        a = y[:, h, :, :]
                        done(v.tensor_tensor(a, a, shift[:, None, :].to_broadcast([P, G, D]), ALU.add))
                        dve.wait_ge(s_in[h], n_in * t + n_in)
                        v.scalar_tensor_tensor(a, a, 0.0, x[:, h, :, :], ALU.max, ALU.add).then_inc(s_done, 1)
                    else:
                        dve.sem_inc(s_done)
            if bn is not None:
                done.leave(turns)


def choose_experts(nc, c, agg, gamma, beta, gates_out):
    ctx = ExitStack()
    with ctx:
        sp_ = Space(nc, ctx, "gates")
        w = HEADS * NEXP
        a = sp_.sb("a", [P, NTP, w])
        sq = sp_.sb("sq", [P, NTP, w])
        par = sp_.sb("par", [P, 2, w])
        mean, var = sp_.sb("mean", [P, NTP]), sp_.sb("var", [P, NTP])
        score, rank, gate = (sp_.sb(n, [P, NTP, NEXP]) for n in ("score", "rank", "gate"))
        cmp, top, total = (sp_.sb(n, [P, NTP]) for n in ("cmp", "top", "total"))
        s_load, s_dve, s_act, s_var, s_exp, s_out, s_done = (
            sp_.sem(n) for n in ("load", "dve", "act", "var", "exp", "out", "done"))
        block = sp_.block()

        @block.sync
        def _(sp):
            sp.dma_start(a[:, :, :], agg.rearrange("(t p) c -> p t c", p=P)).then_inc(s_load, 16)
            sp.dma_start(par[:, 0, :], gamma.partition_broadcast(P)).then_inc(s_load, 16)
            sp.dma_start(par[:, 1, :], beta.partition_broadcast(P)).then_inc(s_load, 16)
            sp.wait_ge(s_done, 1)
            sp.dma_start(gates_out, gate[:, :, :]).then_inc(s_out, 16)
            sp.wait_ge(s_out, 16)

        @block.scalar
        def _(act):
            act.wait_ge(s_var, 1)
            nc.scalar.activation(var[:, :], var[:, :], ACT.Sqrt).then_inc(s_act, 1)
            act.wait_ge(s_exp, 1)
            nc.scalar.activation(gate[:, :, :], score[:, :, :], ACT.Exp).then_inc(s_act, 1)

        @block.vector
        def _(dve):
            v = nc.vector
            done = Chain(dve, s_dve)
            wide = lambda m, n: m[:, :, None].to_broadcast([P, NTP, n])
            dve.wait_ge(s_load, 48)
            done(v.tensor_reduce(mean[:, :], a[:, :, :], axis=AX.X, op=ALU.add))
            done(v.tensor_scalar(mean[:, :], mean[:, :], 1.0 / w, None, ALU.mult))
            done(v.tensor_tensor(a[:, :, :], a[:, :, :], wide(mean, w), ALU.subtract))
            done(v.tensor_tensor(sq[:, :, :], a[:, :, :], a[:, :, :], ALU.mult))
            done(v.tensor_reduce(var[:, :], sq[:, :, :], axis=AX.X, op=ALU.add))
            done(v.tensor_scalar(var[:, :], var[:, :], 1.0 / w, EPS, ALU.mult, ALU.add))
            dve.sem_inc(s_var)
            dve.wait_ge(s_act, 1)
            done(v.reciprocal(var[:, :], var[:, :]))
            done(v.tensor_tensor(a[:, :, :], a[:, :, :], wide(var, w), ALU.mult))
            done(v.tensor_tensor(a[:, :, :], a[:, :, :], par[:, 0:1, :].to_broadcast([P, NTP, w]), ALU.mult))
            done(v.tensor_tensor(a[:, :, :], a[:, :, :], par[:, 1:2, :].to_broadcast([P, NTP, w]), ALU.add))
            done(v.tensor_tensor(score[:, :, :], a[:, :, 0:NEXP], a[:, :, NEXP:2 * NEXP], ALU.add))
            for h in range(2, HEADS):
                done(v.tensor_tensor(score[:, :, :], score[:, :, :], a[:, :, h * NEXP:(h + 1) * NEXP], ALU.add))
            done(v.tensor_scalar(score[:, :, :], score[:, :, :], 1.0 / HEADS, None, ALU.mult))
            done(v.memset(rank[:, :, :], 0.0))
            for e in range(NEXP):
                for j in range(NEXP):
                    if j != e:
                        done(v.tensor_tensor(cmp[:, :], score[:, :, j], score[:, :, e], ALU.is_ge if j < e else ALU.is_gt))
                        done(v.tensor_tensor(rank[:, :, e], rank[:, :, e], cmp[:, :], ALU.add))
            done(v.tensor_reduce(top[:, :], score[:, :, :], axis=AX.X, op=ALU.max))
            done(v.tensor_tensor(score[:, :, :], score[:, :, :], wide(top, NEXP), ALU.subtract))
            dve.sem_inc(s_exp)
            dve.wait_ge(s_act, 2)
            done(v.scalar_tensor_tensor(gate[:, :, :], rank[:, :, :], 2.0, gate[:, :, :], ALU.is_lt, ALU.mult))
            done(v.tensor_reduce(total[:, :], gate[:, :, :], axis=AX.X, op=ALU.add))
            done(v.reciprocal(total[:, :], total[:, :]))
            done(v.tensor_tensor(gate[:, :, :], gate[:, :, :], wide(total, NEXP), ALU.mult))
            dve.sem_inc(s_done)


def apply_gates(nc, c, x_in, gates_in, done_in, out):
    ctx = ExitStack()
    with ctx:
        sp_ = Space(nc, ctx, "apply")
        G = 5
        turns = NTP // (2 * G)
        gates = sp_.sb("gates", [P, NTP, NEXP])
        gate = sp_.sb("gate", [P, 2, G, NEXP])
        y = sp_.sb("y", [P, 2, NEXP, G, D])
        x = sp_.sb("x", [P, 2, G, D])
        s_gates, s_gate, s_gfree, s_dve, s_done = (sp_.sem(n) for n in ("gates", "gate", "gfree", "dve", "done"))
        s_in, s_out = ([sp_.sem(f"{n}{h}") for h in range(2)] for n in ("in", "out"))
        block = sp_.block()

        @block.sync
        def _(sp):
            sp.dma_start(gates[:, :, :], gates_in).then_inc(s_gates, 16)

            def load(t, h):
                at = bass.ds((2 * t + h) * G * P, G * P)
                for e in range(NEXP):
                    sp.dma_start(y[:, h, e, :, :], done_in[e][at, :].rearrange("(g p) d -> p g d", p=P)).then_inc(s_in[h], 16)
                sp.dma_start(x[:, h, :, :], x_in[at, :].rearrange("(g p) d -> p g d", p=P)).then_inc(s_in[h], 16)

            def store(t, h):
                sp.wait_ge(s_done, 2 * t + (h + 1))
                sp.dma_start(out[bass.ds((2 * t + h) * G * P, G * P), :].rearrange("(g p) d -> p g d", p=P),
                             x[:, h, :, :]).then_inc(s_out[h], 16)
            load(0, 0)
            load(0, 1)
            with sp.Fori(0, turns - 1) as t:
                for h in range(2):
                    store(t, h)
                    sp.wait_ge(s_out[h], 16 * t + 16)
                    load(t + 1, h)
            for h in range(2):
                store(turns - 1, h)
            for h in range(2):
                sp.wait_ge(s_out[h], 16 * turns)

        @block.scalar
        def _(act):
            act.wait_ge(s_gates, 16)
            act.sem_inc(s_gfree, 2)
            with act.Fori(0, turns) as t:
                for h in range(2):
                    act.wait_ge(s_gfree, 2 * t + (h + 1))
                    nc.scalar.copy(gate[:, h, :, :], gates[:, bass.ds((2 * t + h) * G, G), :]).then_inc(s_gate, 1)

        @block.vector
        def _(dve):
            v = nc.vector
            done = Chain(dve, s_dve)
            with dve.Fori(0, turns) as t:
                done.enter(t, 2 * (NEXP - 1) * G)
                for h in range(2):
                    dve.wait_ge(s_in[h], 16 * (NEXP + 1) * t + 16 * (NEXP + 1))
                    dve.wait_ge(s_gate, 2 * t + (h + 1))
                    for e in range(NEXP):
                        for g in range(G):
                            ins = v.scalar_tensor_tensor(x[:, h, g, :], y[:, h, e, g, :], gate[:, h, g, e:e + 1], x[:, h, g, :],
                                                         ALU.mult, ALU.add)
                            if e < NEXP - 1:
                                done.mark(ins)
                        if e < NEXP - 1:
                            done.wait()
                    ins.then_inc(s_done, 1)
                    dve.wait_ge(s_done, 2 * t + (h + 1))
                    dve.sem_inc(s_gfree)
            done.leave(turns)


class GatedExperts:

    FB = FH // P
    N_W = 16 * (3 * NEXP + 2)

    def __init__(self, nc, c, sp_, xt, w1_in, b1_in, w2_in, b2_in, out):
        self.nc, self.c, self.xt, self.ins, self.out = nc, c, xt, (w1_in, b1_in, w2_in, b2_in), out
        self.w1 = sp_.sb("w1", [P, 2, NEXP, FH])
        self.w2 = sp_.sb("w2", [P, NEXP, self.FB, D])
        self.b1 = sp_.sb("b1", [P, NEXP, self.FB])
        self.b2 = sp_.sb("b2", [1, NEXP, D])
        self.y = sp_.sb("y", [P, 2, 2, D])
        self.hid = sp_.sb("hid", [P, self.FB, 2 * P])
        self.p_h = sp_.ps("p_h", [P, self.FB, 512])
        self.p_y = sp_.ps("p_y", [P, 2, 512])
        self.s_w, self.s_h, self.s_a, self.s_y, self.s_copy = (sp_.sem(n) for n in ("w", "h", "a", "y_made", "copy"))
        self.s_y_out = [sp_.sem(f"y_out{h}") for h in range(2)]

    def load(self, sp):
        w1_in, b1_in, w2_in, b2_in = self.ins
        with self.nc.allow_non_contiguous_dma(reason="a bias per partition"):
            for e in range(NEXP):
                for k in range(2):
                    sp.dma_start(self.w1[:, k, e, :], w1_in[e, k * P:(k + 1) * P, :]).then_inc(self.s_w, 16)
                sp.dma_start(self.w2[:, e, :, :], w2_in[e, :, :].rearrange("(f p) d -> p f d", p=P)).then_inc(self.s_w, 16)
            sp.dma_start(self.b1[:, :, :].rearrange("p e f -> p (e f)"),
                         b1_in.rearrange("e (f p) -> p (e f)", p=P)).then_inc(self.s_w, 16)
        sp.dma_start(self.b2[:, :, :], b2_in.rearrange("(a e) d -> a e d", a=1)).then_inc(self.s_w, 16)
        for h in range(2):
            sp.sem_inc(self.s_y_out[h], 16)

    def store(self, sp, n, e):
        sp.wait_ge(self.s_copy, (NEXP * 2) * n + (2 * e + 4))
        sp.dma_start(self.out[e][bass.ds(n * 2 * P, 2 * P), :].rearrange("(i p) d -> p i d", p=P),
                     self.y[:, e % 2, :, :]).then_inc(self.s_y_out[e % 2], 16)

    def stored(self, sp):
        for h in range(2):
            sp.wait_ge(self.s_y_out[h], 16 * (NTP // 2 * NEXP // 2) + 16)

    def ready(self, pe):
        pe.wait_ge(self.s_w, self.N_W)

    def products(self, pe, n, e):
        nc, c, FB = self.nc, self.c, self.FB
        for f in range(FB):
            pe.wait_ge(self.s_a, (NEXP * FB) * n + (e * FB + f + 1))
            for k in range(2):
                last = nc.tensor.matmul(self.p_h[:, f, 0:2 * P], self.w1[:, k, e, f * P:(f + 1) * P],
                                        self.xt[:, k, bass.ds(n * 2 * P, 2 * P)], start=(k == 0), stop=(k == 1))
            last.then_inc(self.s_h, 1)
        for i in range(2):
            pe.wait_ge(self.s_copy, (NEXP * 2) * n + (2 * e + i + 1))
            nc.tensor.matmul(self.p_y[:, i, 0:D], c["ones"][0:1, :], self.b2[0:1, e, :], start=True, stop=False)
            for f in range(FB):
                if i == 0:
                    pe.wait_ge(self.s_a, (NEXP * FB) * n + (e * FB + f + 1 + FB))
                last = nc.tensor.matmul(self.p_y[:, i, 0:D], self.hid[:, f, i * P:(i + 1) * P], self.w2[:, e, f, :],
                                        start=False, stop=(f == FB - 1))
            last.then_inc(self.s_y, 1)

    def start(self, act):
        act.sem_inc(self.s_a, self.FB)
        act.wait_ge(self.s_w, self.N_W)

    def gelu(self, act, n, e):
        for f in range(self.FB):
            act.wait_ge(self.s_h, (NEXP * self.FB) * n + (e * self.FB + f + 1))
            self.nc.scalar.activation(self.hid[:, f, :], self.p_h[:, f, 0:2 * P], ACT.Gelu,
                                      bias=self.b1[:, e, f:f + 1]).then_inc(self.s_a, 1)

    def free(self, dve):
        dve.sem_inc(self.s_copy, 2)

    def take(self, dve, n, e):
        dve.wait_ge(self.s_y_out[e % 2], 32 * n + (16 * (e // 2) + 16))
        for i in range(2):
            dve.wait_ge(self.s_y, (NEXP * 2) * n + (2 * e + i + 1))
            self.nc.vector.tensor_copy(self.y[:, e % 2, i, :], self.p_y[:, i, 0:D]).then_inc(self.s_copy, 1)


def hyper_sum(nc, c, name, s, table, tables, node_rows, out, counts_in, relu, x_in=None):
    ctx = ExitStack()
    with ctx:
        sp_ = Space(nc, ctx, name)
        back = s == 3
        cols, which = CHUNKS[s] * P, TURNS_ALL if back else TURNS_HYPER
        tiles_out, m = (NTP, D + 1) if back else (NHT, D)
        pay = sp_.sb("pay", [P, cols], I32)
        local = sp_.sb("local", [P, cols], I32)
        node_i = sp_.sb("node_i", [1, cols + EXTRA], I32)
        cnt, rest = sp_.sb("cnt", [P, NTP]), sp_.sb("rest", [P, NTP])
        index = sp_.sb("index", [P, 2, GRP], I32)
        got = sp_.sb("got", [P, 2, GRP, D])
        hot = sp_.sb("hot", [P, 2, GRP, P])
        acc = sp_.sb("acc", [P, NTP, m])
        x = sp_.sb("x", [P, NTP, D]) if x_in is not None else None
        last_row = sp_.sb("last_row", [P, D])
        p_sum = sp_.ps("p_sum", [P, 2 * PAIRS, 512])
        s_load, s_clamp, s_index, s_turn, s_hot, s_sum, s_acc, s_tail, s_out, s_fin, s_x = (
            sp_.sem(n) for n in ("load", "clamp", "index", "turn", "hot", "sum", "acc", "tail", "out", "fin", "x"))
        s_got = [sp_.gathered(0), sp_.gathered(1)]
        LOADS = 16 * 5
        block = sp_.block()

        @block.sync
        def _(sp):
            sp.dma_start(pay[:, :], tables[s][0, :, :]).then_inc(s_load, 16)
            sp.dma_start(local[:, :], tables[s][2, :, :]).then_inc(s_load, 16)
            sp.dma_start(node_i[:, :], node_rows[s]).then_inc(s_load, 16)
            sp.dma_start(cnt[:, :], counts_in).then_inc(s_load, 16)
            sp.dma_start(last_row[:, :], table[NHYP - 1, :].partition_broadcast(P)).then_inc(s_load, 16)
            if x_in is not None:
                sp.dma_start(x[:, :, :], x_in.rearrange("(t p) d -> p t d", p=P)).then_inc(s_x, 16)
            sp.wait_ge(s_out, 1)
            sp.dma_start(out.rearrange("(t p) d -> p t d", p=P), acc[:, 0:tiles_out, 0:D]).then_inc(s_fin, 16)
            sp.wait_ge(s_fin, 16)

        @block.gpsimd
        def _(pool):
            pool.wait_ge(s_load, LOADS)
            turns = turns_of(pool, node_i, s, which)
            with pool.Fori(0, turns) as t:
                for h in range(2):
                    pool.wait_ge(s_index, 2 * t + (h + 1))
                    pool.wait_ge(s_sum, (2 * t + h) * PAIRS + PAIRS)
                    pool.sem_inc(s_turn)
                    for i in range(GRP):
                        pool.indirect_dma_start(
                            out=got[:, h, i, :], out_offset=None, in_=table[:, :],
                            in_offset=bass.IndirectOffsetOnAxis(ap=index[:, h, i:i + 1], axis=0)).then_inc(s_got[h], 16)

        @block.scalar
        def _(act):
            act.wait_ge(s_load, LOADS)
            act.wait_ge(s_clamp, 1)
            for h in range(2):
                nc.scalar.copy(index[:, h, :], pay[:, h * GRP:(h + 1) * GRP]).then_inc(s_index, 1)
            turns = turns_of(act, node_i, s, which)
            with act.Fori(0, turns) as t:
                for h in range(2):
                    act.wait_ge(s_got[h], 16 * GRP * t + 16 * GRP)
                    nc.scalar.copy(index[:, h, :], pay[:, bass.ds((2 * t + h + 2) * GRP, GRP)]).then_inc(s_index, 1)

        @block.tensor
        def _(pe):
            pe.sem_inc(s_sum, 2 * PAIRS)
            pe.wait_ge(s_load, LOADS)
            turns = turns_of(pe, node_i, s, which)
            with pe.Fori(0, turns) as t:
                for h in range(2):
                    pe.wait_ge(s_hot, 2 * t + (h + 1))
                    pe.wait_ge(s_got[h], 16 * GRP * t + 16 * GRP)
                    for j in range(PAIRS):
                        at = h * PAIRS + j
                        for i in (2 * j, 2 * j + 1):
                            last = nc.tensor.matmul(p_sum[:, at, 0:D], hot[:, h, i, :], got[:, h, i, :],
                                                    start=(i == 2 * j), stop=(i > 2 * j))
                        for i in (2 * j, 2 * j + 1) if back else ():
                            last = nc.tensor.matmul(p_sum[:, at, D:D + 1], hot[:, h, i, :], c["ones"][:, 0:1],
                                                    start=(i == 2 * j), stop=(i > 2 * j))
                        last.then_inc(s_sum, 1)

        @block.vector
        def _(dve):
            v = nc.vector
            done = Chain(dve, s_acc)
            done(v.memset(acc[:, :, :], 0.0))
            dve.wait_ge(s_load, LOADS)
            done(v.tensor_scalar_min(pay[:, :], pay[:, :], float(NHYP - 1 if back else N - 1)))
            dve.sem_inc(s_clamp)
            loc = local[:, :].bitcast(F32)
            turns = turns_of(dve, node_i, s, which)

            def one_hot(t, h):
                at = bass.ds((2 * t + h) * GRP, GRP)
                v.tensor_tensor(hot[:, h, :, :], c["ramp"][:, None, 0:P].to_broadcast([P, GRP, P]),
                                loc[:, at][:, :, None].to_broadcast([P, GRP, P]), ALU.is_equal).then_inc(s_hot, 1)

            one_hot(0, 0)
            one_hot(0, 1)
            with dve.Fori(0, turns) as t:
                done.enter(t, 2 * PAIRS)
                for h in range(2):
                    tiles = [dve.value_load(node_i[0:1, bass.ds((2 * t + h) * GRP + 2 * j, 1)], min_val=0, max_val=NT - 1)
                             for j in range(PAIRS)]
                    for j in range(PAIRS):
                        dve.wait_ge(s_sum, (2 * t + h) * PAIRS + (j + 1 + 2 * PAIRS))
                        to = acc[:, bass.ds(tiles[j], 1), :]
                        done(v.tensor_tensor(to, to, p_sum[:, h * PAIRS + j:h * PAIRS + j + 1, 0:m], ALU.add))
                    one_hot(t + 1, h)
            done = Chain(dve, s_tail)
            if back:
                done(v.tensor_tensor(rest[:, :], cnt[:, :], acc[:, :, D], ALU.subtract))
                for b in range(NTP):
                    done.mark(v.scalar_tensor_tensor(acc[:, b, 0:D], last_row[:, :], rest[:, b:b + 1], acc[:, b, 0:D],
                                                     ALU.mult, ALU.add))
                done.wait()
            done(v.tensor_scalar(cnt[:, :], cnt[:, :], 1.0, None, ALU.max))
            done(v.reciprocal(cnt[:, :], cnt[:, :]))
            a = acc[:, 0:tiles_out, 0:D]
            done(v.tensor_tensor(a, a, cnt[:, 0:tiles_out, None].to_broadcast([P, tiles_out, D]), ALU.mult))
            if relu:
                done(v.tensor_scalar(a, a, 0.0, None, ALU.max))
            if x_in is not None:
                dve.wait_ge(s_x, 16)
                done(v.tensor_tensor(a, a, x[:, :, :], ALU.add))
            dve.sem_inc(s_out)


def route(nc, c, xt, rows_in, gate_w, gate_b, slots, coef_out, index_out):
    ctx = ExitStack()
    with ctx:
        sp_ = Space(nc, ctx, "route")
        M = MEXP
        gw = sp_.sb("gw", [P, 2, M])
        gb = sp_.sb("gb", [M, 1])
        zero = sp_.sb("zero", [P, 4096])
        rows = sp_.sb("rows", [P, NTP, D])
        logit_t = sp_.sb("logit_t", [M, NPAD])
        prob, one, tmp, place = (sp_.sb(n, [P, NTP, M]) for n in ("prob", "one", "tmp", "place"))
        top, total, taken, pos, expert, token, kept, coef, slot = (
            sp_.sb(n, [P, NTP]) for n in ("top", "total", "taken", "pos", "expert", "token", "kept", "coef", "slot"))
        before = sp_.sb("before", [P, P])
        per_tile, ahead = sp_.sb("per_tile", [P, NTP, M]), sp_.sb("ahead", [P, M, NTP + 1])
        index = sp_.sb("index", [P, NTP], I32)
        back = sp_.sb("back", [P, NTP], I32)
        p_log = sp_.ps("p_log", [P, 2, 512])
        p_tok = sp_.ps("p_tok", [P, 512])
        p_pre = sp_.ps("p_pre", [P, 2, 512])
        s_load, s_zero, s_fill, s_dve, s_log, s_logged, s_tok, s_exp, s_one, s_pre, s_index, s_done, s_out, s_tri = (
            sp_.sem(n) for n in ("load", "zero", "fill", "dve", "log", "logged", "tok", "exp", "one", "pre", "index",
                                 "done", "out", "tri"))
        s_rows, s_sent = sp_.sem("rows_in"), sp_.gathered(0)
        pieces = [(a, min(a + 512, NPAD)) for a in range(0, NPAD, 512)]
        block = sp_.block()

        @block.sync
        def _(sp):
            for k in range(2):
                sp.dma_start(gw[:, k, :], gate_w[k * P:(k + 1) * P, :]).then_inc(s_load, 16)
            sp.dma_start(gb[:, :], gate_b.rearrange("(e a) -> e a", a=1)).then_inc(s_load, 16)
            sp.wait_ge(s_zero, 1)
            n = MEXP * CAPP * D // P // 4096
            flat = slots.rearrange("(n p r) d -> n p (r d)", n=n, p=P)
            for i in range(n):
                sp.dma_start(flat[i, :, :], zero[:, :]).then_inc(s_fill, 16)
            sp.dma_start(rows[:, :, :], rows_in.rearrange("(t p) d -> p t d", p=P)).then_inc(s_rows, 16)
            sp.wait_ge(s_done, 1)
            sp.dma_start(coef_out, coef[:, :]).then_inc(s_out, 16)
            sp.dma_start(index_out, back[:, :]).then_inc(s_out, 16)
            sp.wait_ge(s_out, 32)
            sp.wait_ge(s_fill, 16 * n)

        @block.gpsimd
        def _(pool):
            nc.gpsimd.memset(zero[:, :], 0.0).then_inc(s_zero, 1)
            pool.wait_ge(s_zero, 1)
            nc.gpsimd.affine_select(out=before[:, :], in_=c["ones"][:, :], compare_op=ALU.is_gt, fill=0.0, base=0,
                                    pattern=[[1, P]], channel_multiplier=-1).then_inc(s_tri, 1)
            pool.wait_ge(s_rows, 16)
            pool.wait_ge(s_fill, 16 * (MEXP * CAPP * D // P // 4096))
            pool.wait_ge(s_index, 1)
            for t in range(NTP):
                pool.indirect_dma_start(out=slots[:, :], out_offset=bass.IndirectOffsetOnAxis(ap=index[:, t:t + 1], axis=0),
                                        in_=rows[:, t, :], in_offset=None,
                                        bounds_check=MEXP * CAPP - 1, oob_is_err=False).then_inc(s_sent, 16)
            pool.wait_ge(s_sent, 16 * NTP)

        @block.tensor
        def _(pe):
            pe.wait_ge(s_load, 48)
            for n, (a, b) in enumerate(pieces):
                if n >= 2:
                    pe.wait_ge(s_logged, n - 1)
                for k in range(2):
                    last = nc.tensor.matmul(p_log[0:M, n % 2, 0:b - a], gw[:, k, :], xt[:, k, a:b],
                                            start=(k == 0), stop=(k == 1))
                last.then_inc(s_log, 1)
            pe.wait_ge(s_logged, len(pieces))
            for t in range(NTP):
                last = nc.tensor.transpose(p_tok[:, t * M:(t + 1) * M], logit_t[:, t * P:(t + 1) * P], c["ident"][0:M, 0:M])
            last.then_inc(s_tok, 1)
            pe.wait_ge(s_tri, 1)
            pe.wait_ge(s_one, 1)
            flat = one[:, :, :].rearrange("p t e -> p (t e)")
            nc.tensor.matmul(p_pre[:, 0, 0:NTP * M], before[:, :], flat, start=True, stop=True)
            nc.tensor.matmul(p_pre[:, 1, 0:NTP * M], c["ones"][:, :], flat, start=True, stop=True).then_inc(s_pre, 1)

        @block.scalar
        def _(act):
            for n, (a, b) in enumerate(pieces):
                act.wait_ge(s_log, n + 1)
                nc.scalar.activation(logit_t[:, a:b], p_log[0:M, n % 2, 0:b - a], ACT.Identity, bias=gb[:, 0:1]).then_inc(s_logged, 1)
            act.wait_ge(s_exp, 1)
            nc.scalar.activation(prob[:, :, :], prob[:, :, :], ACT.Exp).then_inc(s_exp, 1)

        @block.vector
        def _(dve):
            v = nc.vector
            done = Chain(dve, s_dve)
            wide = lambda m: m[:, :, None].to_broadcast([P, NTP, M])
            dve.wait_ge(s_tok, 1)
            done(v.tensor_copy(prob[:, :, :], p_tok[:, 0:NTP * M].rearrange("p (t e) -> p t e", e=M)))
            done(v.tensor_reduce(top[:, :], prob[:, :, :], axis=AX.X, op=ALU.max))
            done(v.tensor_tensor(prob[:, :, :], prob[:, :, :], wide(top), ALU.subtract))
            dve.sem_inc(s_exp)
            dve.wait_ge(s_exp, 2)
            done(v.tensor_reduce(total[:, :], prob[:, :, :], axis=AX.X, op=ALU.add))
            done(v.reciprocal(total[:, :], total[:, :]))
            done(v.tensor_tensor(prob[:, :, :], prob[:, :, :], wide(total), ALU.mult))
            done(v.tensor_reduce(top[:, :], prob[:, :, :], axis=AX.X, op=ALU.max))
            done(v.tensor_tensor(one[:, :, :], prob[:, :, :], wide(top), ALU.is_ge))
            done(v.tensor_scalar(token[:, :], c["ramp"][:, 0:NTP], float(P), c["part"][:, 0:1], ALU.mult, ALU.add))
            done(v.tensor_scalar(taken[:, :], token[:, :], float(N), None, ALU.is_ge))
            for e in range(M):
                done(v.scalar_tensor_tensor(one[:, :, e], taken[:, :], 0.5, one[:, :, e], ALU.is_lt, ALU.mult))
                done(v.tensor_tensor(taken[:, :], taken[:, :], one[:, :, e], ALU.add))
            dve.sem_inc(s_one)
            dve.wait_ge(s_pre, 1)
            done.mark(v.tensor_copy(place[:, :, :], p_pre[:, 0, 0:NTP * M].rearrange("p (t e) -> p t e", e=M)))
            done.mark(v.tensor_copy(per_tile[:, :, :], p_pre[:, 1, 0:NTP * M].rearrange("p (t e) -> p t e", e=M)))
            done(v.memset(ahead[:, :, :], 0.0))
            for e in range(M):
                done(v.tensor_tensor_scan(ahead[:, e, 1:], c["ones"][:, 0:NTP], per_tile[:, :, e], 0.0, ALU.mult, ALU.add))
            done(v.tensor_tensor(place[:, :, :], place[:, :, :], ahead[:, :, 0:NTP].rearrange("p e t -> p t e"), ALU.add))
            done(v.tensor_tensor(tmp[:, :, :], place[:, :, :], one[:, :, :], ALU.mult))
            done(v.tensor_reduce(pos[:, :], tmp[:, :, :], axis=AX.X, op=ALU.add))
            done(v.tensor_tensor(tmp[:, :, :], one[:, :, :], c["ramp"][:, None, 0:M].to_broadcast([P, NTP, M]), ALU.mult))
            done(v.tensor_reduce(expert[:, :], tmp[:, :, :], axis=AX.X, op=ALU.add))
            done(v.tensor_scalar(kept[:, :], pos[:, :], float(CAP), None, ALU.is_lt))
            done(v.tensor_scalar(token[:, :], token[:, :], float(N), None, ALU.is_lt))
            done(v.tensor_tensor(kept[:, :], kept[:, :], token[:, :], ALU.mult))
            done(v.tensor_tensor(coef[:, :], top[:, :], kept[:, :], ALU.mult))
            done(v.scalar_tensor_tensor(slot[:, :], expert[:, :], float(CAPP), pos[:, :], ALU.mult, ALU.add))
            done(v.tensor_scalar(kept[:, :], kept[:, :], -float(MEXP * CAPP), float(MEXP * CAPP), ALU.mult, ALU.add))
            done(v.tensor_tensor(slot[:, :], slot[:, :], kept[:, :], ALU.add))
            done(v.tensor_copy(index[:, :], slot[:, :]))
            dve.sem_inc(s_index)
            done(v.tensor_scalar(slot[:, :], slot[:, :], float(MEXP * CAPP - 1), None, ALU.min))
            done(v.tensor_copy(back[:, :], slot[:, :]))
            dve.sem_inc(s_done)


def routed_experts(nc, c, slots, w1_in, b1_in, w2_in, b2_in, out):
    ctx = ExitStack()
    with ctx:
        sp_ = Space(nc, ctx, "moe")
        FB, UNITS = MF // P, CAPP // (2 * P)
        w1 = sp_.sb("w1", [P, 2, 2, MF])
        w2 = sp_.sb("w2", [P, 2, FB, D])
        b1 = sp_.sb("b1", [P, 2, FB])
        b2 = sp_.sb("b2", [1, 2, D])
        x = sp_.sb("x", [P, 2, 2, D])
        xt = sp_.sb("xt", [P, 2, 2, 2 * P])
        hid = sp_.sb("hid", [P, FB, 2 * P])
        y = sp_.sb("y", [P, 2, 2, D])
        p_t = sp_.ps("p_t", [P, 2, 512])
        p_h = sp_.ps("p_h", [P, 4, 512])
        p_y = sp_.ps("p_y", [P, 2, 512])
        s_t, s_xt, s_h, s_a, s_y, s_copy = (sp_.sem(n) for n in ("t", "xt", "h", "a", "y", "copy"))
        s_in, s_out, s_w = ([sp_.sem(f"{n}{h}") for h in range(2)] for n in ("in", "out", "w"))
        NW = 16 * 5
        per_turn = 2 * UNITS
        block = sp_.block()

        def each_unit(eng, body, expert=None):
            with eng.Fori(0, MEXP // 2) as t:
                for o in range(2):
                    if expert:
                        expert(t, o)
                    for q in range(UNITS):
                        u = o * UNITS + q
                        body(t, o, u, u % 2)

        @block.sync
        def _(sp):
            for h in range(2):
                sp.sem_inc(s_out[h], 16)

            def expert(t, o):
                sp.wait_ge(s_y, per_turn * 2 * t + (2 * UNITS * o + 1))
                with nc.allow_non_contiguous_dma(reason="a bias per partition"):
                    for k in range(2):
                        sp.dma_start(w1[:, o, k, :], w1_in[bass.ds(2 * t + o, 1), k * P:(k + 1) * P, :]
                                     .rearrange("a p f -> p (a f)")).then_inc(s_w[o], 16)
                    sp.dma_start(w2[:, o, :, :], w2_in[bass.ds(2 * t + o, 1), :, :]
                                 .rearrange("a (f p) d -> p (a f) d", p=P)).then_inc(s_w[o], 16)
                    sp.dma_start(b1[:, o, :], b1_in[bass.ds(2 * t + o, 1), :].rearrange("a (f p) -> p (a f)", p=P)).then_inc(s_w[o], 16)
                    sp.dma_start(b2[:, o, :], b2_in[bass.ds(2 * t + o, 1), :]).then_inc(s_w[o], 16)

            def body(t, o, u, h):
                sp.wait_ge(s_t, per_turn * t + (u + 1))
                sp.dma_start(x[:, h, :, :], slots[bass.ds((per_turn * t + u) * 2 * P, 2 * P), :]
                             .rearrange("(i p) d -> p i d", p=P)).then_inc(s_in[h], 16)
            each_unit(sp, body, expert)

        @block.tensor
        def _(pe):
            pe.sem_inc(s_t, 2)
            pe.sem_inc(s_y, 2 * UNITS + 1)

            def body(t, o, u, h):
                if u % UNITS == 0:
                    pe.wait_ge(s_w[o], NW * t + NW)
                pe.wait_ge(s_in[h], 16 * (UNITS * t) + 16 * (u // 2 + 1))
                for k in range(2):
                    for i in range(2):
                        last = nc.tensor.transpose(p_t[:, k, i * P:(i + 1) * P], x[:, h, i, k * P:(k + 1) * P], c["ident"][:, :])
                last.then_inc(s_t, 1)
                pe.wait_ge(s_xt, per_turn * t + (u + 1))
                for f in range(FB):
                    pe.wait_ge(s_a, per_turn * FB * t + (u * FB + f + 1))
                    for k in range(2):
                        last = nc.tensor.matmul(p_h[:, f % 4, 0:2 * P], w1[:, o, k, f * P:(f + 1) * P], xt[:, h, k, :],
                                                start=(k == 0), stop=(k == 1))
                    last.then_inc(s_h, 1)
                for i in range(2):
                    pe.wait_ge(s_copy, per_turn * 2 * t + (2 * u + i + 1))
                    nc.tensor.matmul(p_y[:, i, 0:D], c["ones"][0:1, :], b2[0:1, o, :], start=True, stop=False)
                    for f in range(FB):
                        if i == 0:
                            pe.wait_ge(s_a, per_turn * FB * t + (u * FB + f + 1 + 4))
                        last = nc.tensor.matmul(p_y[:, i, 0:D], hid[:, f, i * P:(i + 1) * P], w2[:, o, f, :],
                                                start=False, stop=(f == FB - 1))
                    last.then_inc(s_y, 1)
            each_unit(pe, body)

        @block.scalar
        def _(act):
            act.sem_inc(s_a, 4)

            def body(t, o, u, h):
                for f in range(FB):
                    act.wait_ge(s_h, per_turn * FB * t + (u * FB + f + 1))
                    nc.scalar.activation(hid[:, f, :], p_h[:, f % 4, 0:2 * P], ACT.Relu, bias=b1[:, o, f:f + 1]).then_inc(s_a, 1)
                act.wait_ge(s_copy, per_turn * 2 * t + (2 * u + 4))
                act.dma_start(out[bass.ds((per_turn * t + u) * 2 * P, 2 * P), :].rearrange("(i p) d -> p i d", p=P),
                              y[:, h, :, :]).then_inc(s_out[h], 16)
            each_unit(act, body)
            for h in range(2):
                act.wait_ge(s_out[h], 16 * (MEXP * UNITS // 2) + 16)

        @block.vector
        def _(dve):
            dve.sem_inc(s_copy, 2)

            def body(t, o, u, h):
                dve.wait_ge(s_t, per_turn * t + (u + 3))
                nc.vector.tensor_copy(xt[:, h, :, :], p_t[:, :, 0:2 * P]).then_inc(s_xt, 1)
                dve.wait_ge(s_out[h], 16 * (UNITS * t) + 16 * (u // 2 + 1))
                for i in range(2):
                    dve.wait_ge(s_y, per_turn * 2 * t + (2 * u + i + 1 + 2 * UNITS + 1))
                    nc.vector.tensor_copy(y[:, h, i, :], p_y[:, i, 0:D]).then_inc(s_copy, 1)
            each_unit(dve, body)


def combine(nc, c, expert_out, coef_in, index_in, x_in, out):
    ctx = ExitStack()
    with ctx:
        sp_ = Space(nc, ctx, "combine")
        got = sp_.sb("got", [P, NTP, D])
        x = sp_.sb("x", [P, NTP, D])
        coef = sp_.sb("coef", [P, NTP])
        index = sp_.sb("index", [P, NTP], I32)
        mask = sp_.sb("mask", [P, 5, D], I32)
        fill = sp_.sb("fill", [P, 3, D])
        s_load, s_index, s_dve, s_done, s_out = (sp_.sem(n) for n in ("load", "index", "dve", "done", "out"))
        s_got = sp_.gathered(0)
        whole = N // P
        block = sp_.block()

        @block.sync
        def _(sp):
            sp.dma_start(index[:, :], index_in).then_inc(s_index, 16)
            sp.dma_start(coef[:, :], coef_in).then_inc(s_load, 16)
            sp.dma_start(x[:, :, :], x_in.rearrange("(t p) d -> p t d", p=P)).then_inc(s_load, 16)
            sp.wait_ge(s_done, 1)
            sp.dma_start(out[0:whole * P, :].rearrange("(t p) d -> p t d", p=P), x[:, 0:whole, :]).then_inc(s_out, 16)
            sp.dma_start(out[whole * P:N, :], x[0:N - whole * P, whole, :]).then_inc(s_out, 16)
            sp.wait_ge(s_out, 32)

        @block.gpsimd
        def _(pool):
            pool.wait_ge(s_index, 16)
            for t in range(NTP):
                pool.indirect_dma_start(out=got[:, t, :], out_offset=None, in_=expert_out[:, :],
                                        in_offset=bass.IndirectOffsetOnAxis(ap=index[:, t:t + 1], axis=0)).then_inc(s_got, 16)

        @block.vector
        def _(dve):
            v = nc.vector
            done = Chain(dve, s_dve)
            for i, a in enumerate((0.0, 1e4, -1e4)):
                done.mark(v.memset(fill[:, i, :], a))
            done.wait()
            dve.wait_ge(s_load, 32)
            dve.wait_ge(s_got, 16 * NTP)
            for a in range(0, NTP, 5):
                g = got[:, a:a + 5, :]
                done(v.tensor_tensor(g, g, coef[:, a:a + 5, None].to_broadcast([P, 5, D]), ALU.mult))
                for i, (value, op) in enumerate(((None, ALU.not_equal), (3.4028234e38, ALU.is_gt), (-3.4028234e38, ALU.is_lt))):
                    if value is None:
                        done(v.tensor_tensor(mask[:, :, :], g, g, op))
                    else:
                        done(v.tensor_scalar(mask[:, :, :], g, value, None, op))
                    for j in range(5):
                        done.mark(v.copy_predicated(got[:, a + j, :], mask[:, j, :], fill[:, i, :]))
                    done.wait()
                done(v.tensor_tensor(x[:, a:a + 5, :], x[:, a:a + 5, :], g, ALU.add))
            dve.sem_inc(s_done)


def build(nc, a, out):
    def dram(name, shape, dt=F32):
        return nc.dram_tensor(name, shape, dt).ap()

    rec = [dram(f"rec{s}", [ET2 + 1, P], I32) for s in range(LISTS)]
    local_rows = [dram(f"local_rows{s}", [CHUNKS[s] * P, P]) for s in range(LISTS)]
    tables = [dram(f"tables{s}", [4, P, CHUNKS[s] * P], I32) for s in range(LISTS)]
    node_rows = [dram(f"node_rows{s}", [1, CHUNKS[s] * P + EXTRA], I32) for s in range(LISTS)]
    lists = (tables, local_rows, node_rows)
    x0, x1, x2, x3 = (dram(f"x{i}", [NPAD, D]) for i in range(4))
    scores = [dram(f"scores{s}", [P, NTP, 2 * HEADS]) for s in range(3)]
    wide = [dram(f"wide{s}", [NPAD, HC + HEADS]) for s in range(2)]
    slim = dram("slim", [NPAD, HEADS * NEXP + HEADS])
    att = [dram(f"att{s}", [NPAD, HC]) for s in range(2)] + [dram("att2", [NPAD, HEADS * NEXP])]
    counts = [dram(f"counts{s}", [P, NTP]) for s in range(3)]
    kept = [dram(f"kept{s}", [ITEMS1 // GRP, P, GRP * (HC + HEADS)]) for s in range(2)]
    kept2 = dram("kept_slim", [ITEMS2 // GRP, P, GRP * (HEADS * NEXP + HEADS)])
    gates = dram("gates", [P, NTP, NEXP])
    ctx = ExitStack()
    with ctx:
        sp_ = Space(nc, ctx, "main")
        c = {"ident": sp_.sb("ident", [P, P]), "ones": sp_.sb("ones", [P, P]), "ramp": sp_.sb("ramp", [P, CHM * P]),
             "part": sp_.sb("part", [P, 1]), "item_of": sp_.sb("item_of", [P, CHM]),
             "sign": sp_.sb("sign", [P, 8]), "turn": sp_.sb("turn", [P, 8])}
        GATHERED[:] = [sp_.sem("gathered0"), sp_.sem("gathered1")]
        constants(nc, c)
        sort_edges(nc, c, a["src"], a["dst"], a["L0_ffn_edge_index"], rec)
        for s in range(LISTS):
            make_items(nc, c, s, rec, local_rows, tables, node_rows)
        pad_rows(nc, a["x"], x0)

        inner = ExitStack()
        with inner:
            xt = Space(nc, inner, "l0g").sb("xt", [P, 2, NPAD + 2 * P])
            normalise(nc, c, "norm0", x0, xt)
            project(nc, c, "proj0", xt, [a["L0_gnn_W_f"], a["L0_gnn_W_b"]],
                    [dict(width=HC, a_src=a[f"L0_gnn_a_src_{x}"], a_dst=a[f"L0_gnn_a_dst_{x}"], table=wide[s],
                          nodes=scores[s]) for s, x in enumerate("fb")])
        both_attentions(nc, c, lists, wide, scores, [a["L0_gnn_b_f"], a["L0_gnn_b_b"]], kept, att, counts)
        rows_product(nc, c, "fuse", att[0:2], a["L0_gnn_W_fuse"], x1, NTP,
                     bn=[a[f"L0_gnn_{n}"] for n in ("b_fuse", "gamma", "beta", "run_mean", "run_var")], x_in=x0)

        expert_out = [dram(f"expert_out{e}", [NPAD, D]) for e in range(NEXP)]
        outer = ExitStack()
        with outer:
            sp2 = Space(nc, outer, "att2")
            ard = sp2.sb("ard", [P, CHUNKS[2] * P, 2 * HEADS])
            inner = ExitStack()
            with inner:
                al = Space(nc, inner, "att2").sb("al", [P, CHUNKS[2] * P, HEADS])
                rows = ExitStack()
                with rows:
                    xt = Space(nc, rows, "l0f").sb("xt", [P, 2, NPAD + 2 * P])
                    normalise(nc, c, "norm1", x1, xt)
                    project(nc, c, "proj1", xt, [a["L0_ffn_W_gat"]],
                            [dict(width=HEADS * NEXP, a_src=a["L0_ffn_att_src"], a_dst=a["L0_ffn_att_dst"], table=slim,
                                  nodes=scores[2])])
                    attend_pass(nc, c, "att2g", HEADS * NEXP, *lists, gather=(2, slim, scores[2], kept2, al, ard),
                                experts=(xt, a["L0_ffn_W1"], a["L0_ffn_b1"], a["L0_ffn_W2"], a["L0_ffn_b2"], expert_out))
                attend_weights(nc, c, "att2w", 2, tables, al, ard)
            acc = sp2.sb("acc", [P, NTP, HEADS * NEXP + 2 * HEADS + 1])
            attend_pass(nc, c, "att2s", HEADS * NEXP, *lists, add=(2, kept2, ard, acc))
            attend_finish(nc, c, "att2f", HEADS * NEXP, slim, a["L0_ffn_b_gat"], acc, att[2], counts[2])
        choose_experts(nc, c, att[2], a["L0_ffn_ln_gamma"], a["L0_ffn_ln_beta"], gates)
        apply_gates(nc, c, x1, gates, expert_out, x2)

        xn, h1, e1, h2, n1, h3, e2, h4 = (
            dram(n, [NPAD if n in ("xn", "h1", "n1", "h3") else NHT * P, D]) for n in ("xn", "h1", "e1", "h2", "n1", "h3", "e2", "h4"))
        inner = ExitStack()
        with inner:
            xt = Space(nc, inner, "l1g").sb("xt", [P, 2, NPAD + 2 * P])
            normalise(nc, c, "norm2", x2, xt, rows_out=xn)
        rows_product(nc, c, "n2e0", [xn], a["L1_gnn_W0_n2e"], h1, NTP)
        hyper_sum(nc, c, "hyp0", 0, h1, tables, node_rows, e1, counts[0], True)
        rows_product(nc, c, "e2n0", [e1], a["L1_gnn_W0_e2n"], h2, NHT)
        hyper_sum(nc, c, "hyp1", 3, h2, tables, node_rows, n1, counts[1], True)
        rows_product(nc, c, "n2e1", [n1], a["L1_gnn_W1_n2e"], h3, NTP)
        hyper_sum(nc, c, "hyp2", 0, h3, tables, node_rows, e2, counts[0], True)
        rows_product(nc, c, "e2n1", [e2], a["L1_gnn_W1_e2n"], h4, NHT)
        hyper_sum(nc, c, "hyp3", 3, h4, tables, node_rows, x3, counts[1], False, x_in=x2)

        slots, done = dram("slots", [MEXP * CAPP, D]), dram("done", [MEXP * CAPP, D])
        coef, back, xm = dram("coef", [P, NTP]), dram("back", [P, NTP], I32), dram("xm", [NPAD, D])
        inner = ExitStack()
        with inner:
            xt = Space(nc, inner, "l1f").sb("xt", [P, 2, NPAD + 2 * P])
            normalise(nc, c, "norm3", x3, xt, rows_out=xm)
            route(nc, c, xt, xm, a["L1_ffn_gate_w"], a["L1_ffn_gate_b"], slots, coef, back)
        routed_experts(nc, c, slots, a["L1_ffn_w1"], a["L1_ffn_b1"], a["L1_ffn_w2"], a["L1_ffn_b2"], done)
        combine(nc, c, done, coef, back, x3, out)


_INS = (["x", "src", "dst"]
        + ["L0_gnn_" + n for n in ("W_f", "a_src_f", "a_dst_f", "b_f", "W_b", "a_src_b", "a_dst_b", "b_b", "W_fuse",
                                   "b_fuse", "gamma", "beta", "run_mean", "run_var")]
        + ["L0_ffn_" + n for n in ("W_gat", "att_src", "att_dst", "b_gat", "ln_gamma", "ln_beta", "W1", "b1", "W2",
                                   "b2", "edge_index")]
        + ["L1_gnn_" + n for n in ("W0_n2e", "W0_e2n", "W1_n2e", "W1_e2n")]
        + ["L1_ffn_" + n for n in ("gate_w", "gate_b", "w1", "b1", "w2", "b2")])


def kernel(**inputs):
    import numpy as np
    import concourse.bacc as bacc
    from concourse.bass_utils import run_bass_kernel_spmd

    nc = bacc.Bacc("TRN2", target_bir_lowering=False, num_devices=1)
    arrays, args = {}, {}
    for name in _INS:
        arr = np.ascontiguousarray(inputs[name])
        arrays[f"in_{name}"] = arr
        args[name] = nc.dram_tensor(f"in_{name}", arr.shape, mybir.dt.from_np(arr.dtype), kind="ExternalInput").ap()
    out = nc.dram_tensor("out_x", (N, D), F32, kind="ExternalOutput").ap()
    build(nc, args, out)
    r = run_bass_kernel_spmd(nc, [arrays], core_ids=[0])
    return r.results[0]["out_x"]
```

```python
import concourse.bass as bass
from concourse import mybir
from contextlib import ExitStack

F32 = mybir.dt.float32
I32 = mybir.dt.int32
ALU = mybir.AluOpType
ACT = mybir.ActivationFunctionType
AX = mybir.AxisListType

P = 128
N = 6250
D = 256
NT = -(-N // P)
NTP = NT + 1
NPAD = NTP * P
E1 = 100000
E2 = 131072
SORT = 1 << 17
ROW = SORT // P
ET1 = -(-E1 // P)
ET2 = E2 // P
ROUND = 16
GRP = ROUND // 2
MOST = lambda edge_tiles: -(-(edge_tiles + 2 * NT) // ROUND) * ROUND
ITEMS1 = MOST(ET1)
ITEMS2 = MOST(ET2 + 1)
PAIRS = GRP // 2
CH1 = -(-ITEMS1 // P)
CH2 = -(-ITEMS2 // P)
CHUNKS = [CH1, CH1, CH2, CH1]
LISTS = len(CHUNKS)
ITEMS = [ITEMS1, ITEMS1, ITEMS2, ITEMS1]
CHM = max(CHUNKS)
BESIDE = NTP
LEAST_ITEMS = [1.0, 1.0, (BESIDE + 1.0) * ROUND, 1.0]
TURNS_ALL, TURNS_HYPER, LAST_TURN = 0, 1, 2
EXTRA = 3
PACKED = 6
NODE_COLS = [n * P + EXTRA + n * P // GRP for n in CHUNKS]
KEY_SHIFT = 13
CODE_BASE = 1 << 28
FIELD = (1 << KEY_SHIFT) - 1
BIG = 1.0e30
HEADS = 4
CH = 32
HC = HEADS * CH
NEXP = 4
FH = 512
MEXP = 8
MF = 1024
NHYP = 2500
NHT = -(-NHYP // P)
CAP = -(-(5 * N) // (4 * MEXP))
CAPP = -(-CAP // P) * P
UNIT = 2 * P
EXPERT_UNITS = CAPP // UNIT
SPARE = 2
MOST_UNITS = MEXP * EXPERT_UNITS + SPARE
SLOTS = MOST_UNITS * UNIT
EPS = 1e-5


class Chain:

    def __init__(self, eng, sem):
        self.eng, self.sem, self.base, self.count = eng, sem, 0, 0

    def value(self):
        return self.base + self.count

    def mark(self, ins):
        ins.then_inc(self.sem, 1)
        self.count += 1

    def wait(self):
        self.eng.wait_ge(self.sem, self.value())

    def __call__(self, ins):
        self.mark(ins)
        self.wait()

    def enter(self, t, per_turn):
        self.outer = self.value()
        self.per_turn = per_turn
        self.base, self.count = t * per_turn + self.outer, 0

    def enter_last(self, t):
        self.leave(0)
        self.enter(t, self.per_turn)

    def leave(self, turns):
        assert self.count == self.per_turn, (self.count, self.per_turn)
        self.base, self.count = self.outer + turns * self.per_turn, 0


class Space:

    def __init__(self, nc, ctx, prefix):
        self.nc, self.ctx, self.prefix, self.sems = nc, ctx, prefix, []

    def sb(self, name, shape, dt=F32):
        return self.ctx.enter_context(self.nc.sbuf_tensor(f"{self.prefix}_{name}", shape, dt))

    def ps(self, name, shape, dt=F32):
        return self.ctx.enter_context(self.nc.psum_tensor(f"{self.prefix}_{name}", shape, dt))

    def sem(self, name):
        self.sems.append(self.ctx.enter_context(self.nc.semaphore(f"{self.prefix}_{name}")))
        return self.sems[-1]

    def gathered(self, i):
        self.sems.append(GATHERED[i])
        return self.sems[-1]

    def block(self):
        self.ctx.callback(self.clear)
        return self.ctx.enter_context(self.nc.Block())

    def clear(self):
        for s in self.sems:
            if s in GATHERED:
                self.nc.gpsimd.dma_reset(range(s.num, s.num + 1))
            self.nc.gpsimd.sem_clear(s)
        self.nc.all_engine_barrier(sem_only=True)


GATHERED = []


def constants(nc, c):
    ctx = ExitStack()
    with ctx:
        sp_ = Space(nc, ctx, "const")
        s_pool, s_dve = sp_.sem("pool"), sp_.sem("dve")
        ramp_i = sp_.sb("ramp_i", [P, CHM * P], I32)
        part_i = sp_.sb("part_i", [P, 1], I32)
        row_i = sp_.sb("row_i", [P, CHM], I32)
        bits = sp_.sb("bits", [P, 8], I32)
        block = sp_.block()

        @block.gpsimd
        def _(pool):
            nc.gpsimd.memset(c["ident"][:, :], 0.0).then_inc(s_pool, 1)
            nc.gpsimd.memset(c["ones"][:, :], 1.0).then_inc(s_pool, 1)
            nc.gpsimd.iota(ramp_i[:, :], pattern=[[1, CHM * P]], base=0, channel_multiplier=0).then_inc(s_pool, 1)
            nc.gpsimd.iota(part_i[:, :], pattern=[[1, 1]], base=0, channel_multiplier=1).then_inc(s_pool, 1)
            nc.gpsimd.iota(row_i[:, :], pattern=[[P, CHM]], base=0, channel_multiplier=1).then_inc(s_pool, 1)
            pool.wait_ge(s_pool, 5)
            nc.gpsimd.affine_select(out=c["ident"][:, :], in_=c["ident"][:, :], compare_op=ALU.not_equal, fill=1.0,
                                    base=0, pattern=[[-1, P]], channel_multiplier=1).then_inc(s_pool, 1)

        @block.vector
        def _(dve):
            done = Chain(dve, s_dve)
            dve.wait_ge(s_pool, 5)
            nc.vector.tensor_copy(c["ramp"][:, :], ramp_i[:, :])
            nc.vector.tensor_copy(c["part"][:, :], part_i[:, :])
            nc.vector.tensor_copy(c["item_of"][:, :], row_i[:, :])
            for b in range(7):
                done.mark(nc.vector.tensor_scalar(bits[:, b:b + 1], part_i[:, :], b, 1,
                                                  ALU.logical_shift_right, ALU.bitwise_and))
            done.wait()
            done(nc.vector.tensor_scalar(c["sign"][:, 0:7], bits[:, 0:7], -2.0, 1.0, ALU.mult, ALU.add))
            done.mark(nc.vector.tensor_tensor(c["turn"][:, 1:7], c["sign"][:, 0:6], c["sign"][:, 1:7], ALU.mult))
            done.mark(nc.vector.tensor_copy(c["turn"][:, 0:1], c["sign"][:, 0:1]))
            done(nc.vector.tensor_copy(c["turn"][:, 7:8], c["sign"][:, 6:7]))


def sort_edges(nc, c, src, dst, edges2, rec, x_in, x_out):
    ctx = ExitStack()
    with ctx:
        sp_ = Space(nc, ctx, "sort")
        ends = sp_.sb("ends", [P, 4, ROW], I32)
        pay = sp_.sb("pay", [P, LISTS, ROW], I32)
        beyond = sp_.sb("beyond", [P, ROW], I32)
        xy = [sp_.sb("x", [P, LISTS * ROW]), sp_.sb("y", [P, LISTS * ROW])]
        pad = sp_.sb("pad", [1, P], I32)
        no_rows = sp_.sb("no_rows", [(NPAD - N) // 2, 2 * D])
        flip = sp_.ps("flip", [P, LISTS * ROW])
        s_pad, s_load, s_none, s_x = sp_.sem("pad"), sp_.sem("load"), sp_.sem("none"), sp_.sem("x")
        s_dve, s_ready, s_flipped, s_half, s_out = (sp_.sem(x) for x in ("dve", "ready", "flipped", "half", "out"))
        HALF = LISTS * ROW // 2
        full = E1 // ROW * ROW // (16 * ROW) * 16
        rest = E1 - full * ROW
        block = sp_.block()

        @block.gpsimd
        def _(pool):
            nc.gpsimd.memset(no_rows[:, :], 0.0).then_inc(s_none, 1)
            nc.gpsimd.memset(ends[:, 0:2, :], N).then_inc(s_pad, 1)
            nc.gpsimd.memset(pad[:, :], CODE_BASE + (N << KEY_SHIFT)).then_inc(s_pad, 1)

        @block.sync
        def _(sp):
            for j in range(2):
                sp.dma_start(ends[:, 2 + j, :], edges2[1 - j, :].rearrange("(p c) -> p c", c=ROW)).then_inc(s_load, 16)
            sp.wait_ge(s_pad, 2)
            for j, a in ((0, dst), (1, src)):
                sp.dma_start(ends[0:full, j, :], a[0:full * ROW].rearrange("(p c) -> p c", c=ROW)).then_inc(s_load, 16)
                sp.dma_start(ends[full:full + rest // ROW, j, :],
                             a[full * ROW:full * ROW + rest // ROW * ROW].rearrange("(p c) -> p c", c=ROW)).then_inc(s_load, 16)
                sp.dma_start(ends[full + rest // ROW:full + rest // ROW + 1, j, 0:rest % ROW],
                             a[E1 - rest % ROW:E1].rearrange("(p c) -> p c", p=1)).then_inc(s_load, 16)
            for s in range(LISTS):
                sp.dma_start(rec[s][ET2:ET2 + 1, :], pad[:, :]).then_inc(s_out, 16)
            sp.wait_ge(s_ready, 15)
            for s in range(LISTS):
                sp.dma_start(rec[s][0:ET2, :].rearrange("(p a) b -> p (a b)", a=ROW // P),
                             xy[0][:, s * ROW:(s + 1) * ROW].bitcast(I32)).then_inc(s_out, 16)
            sp.wait_ge(s_out, 16 * 2 * LISTS)

        @block.vector
        def _(dve):
            done = Chain(dve, s_dve)
            at = [0]

            def swap():
                at[0] ^= 1
                return xy[at[0] ^ 1], xy[at[0]]

            dve.wait_ge(s_load, 16 * 8)
            for s, (k, v) in enumerate(((0, 1), (1, 0), (2, 3), (1, 0))):
                done.mark(nc.vector.tensor_scalar_min(pay[:, s, :], ends[:, v, :], float(N - 1)))
            done.wait()
            done(nc.vector.tensor_scalar_min(ends[:, :, :], ends[:, :, :], float(N)))
            done(nc.vector.tensor_scalar(beyond[:, :], ends[:, 0, :], float(NHYP), float(N), ALU.is_ge, ALU.mult))
            done(nc.vector.tensor_tensor(ends[:, 3, :], ends[:, 1, :], beyond[:, :], ALU.max))
            x = xy[0][:, :].bitcast(I32).rearrange("p (s c) -> p s c", s=LISTS)
            y = xy[1][:, :].bitcast(I32).rearrange("p (s c) -> p s c", s=LISTS)
            done(nc.vector.tensor_scalar(y, ends[:, :, :], KEY_SHIFT, CODE_BASE, ALU.logical_shift_left, ALU.bitwise_or))
            done(nc.vector.tensor_tensor(x, y, pay[:, :, :], ALU.bitwise_or))

            def exchange(gap):
                a, b = swap()
                a, b = (z[:, :].rearrange("p (m two j) -> p m two j", two=2, j=gap) for z in (a, b))
                done.mark(nc.vector.tensor_tensor(b[:, :, 0, :], a[:, :, 0, :], a[:, :, 1, :], ALU.min))
                done(nc.vector.tensor_tensor(b[:, :, 1, :], a[:, :, 0, :], a[:, :, 1, :], ALU.max))

            def exchange_both_ways(gap, run):
                a, b = swap()
                a, b = (z[:, :].rearrange("p (g d m two j) -> p g d m two j", d=2, m=run // (2 * gap), two=2, j=gap)
                        for z in (a, b))
                for d, lower, upper in ((0, ALU.min, ALU.max), (1, ALU.max, ALU.min)):
                    for half, op in ((0, lower), (1, upper)):
                        done.mark(nc.vector.tensor_tensor(b[:, :, d, :, half, :], a[:, :, d, :, 0, :],
                                                          a[:, :, d, :, 1, :], op))
                done.wait()

            def turn(b):
                a, z = swap()
                done(nc.vector.tensor_scalar(z[:, :], a[:, :], c["turn"][:, b:b + 1], None, ALU.mult))

            def change_layout(n):
                a, b = swap()
                dve.sem_inc(s_ready)
                dve.wait_ge(s_flipped, n)
                done(nc.vector.tensor_copy(b[:, 0:HALF], flip[:, 0:HALF]))
                dve.wait_ge(s_half, n)

            for k in range(1, 10):
                for j in range(k - 1, -1, -1):
                    exchange_both_ways(1 << j, 1 << k)
            turn(0)
            for j in range(9, -1, -1):
                exchange(1 << j)
            n = 0
            for k in range(11, 18):
                turn(k - 10)
                n += 1
                change_layout(n)
                for j in range(k - 1, 6, -1):
                    exchange(1 << (j - 10) if j >= 10 else P << (j - 7))
                n += 1
                change_layout(n)
                for j in range(6, -1, -1):
                    exchange(1 << j)
            if at[0]:
                a, b = swap()
                done(nc.vector.tensor_copy(b[:, :], a[:, :]))
            dve.sem_inc(s_ready)

        at = [0]

        @block.tensor
        def _(pe):
            for n, (x, _) in enumerate(layouts()):
                pe.wait_ge(s_ready, n + 1)
                for b in range(LISTS * ROW // P):
                    last = nc.tensor.transpose(flip[:, b * P:(b + 1) * P], xy[x][:, b * P:(b + 1) * P], c["ident"][:, :])
                last.then_inc(s_flipped, 1)

        @block.scalar
        def _(act):
            act.wait_ge(s_none, 1)
            act.dma_start(x_out[N:NPAD, :].rearrange("(p r) d -> p (r d)", r=2), no_rows[:, :]).then_inc(s_x, 16)
            act.dma_start(x_out[0:N, :], x_in[:, :]).then_inc(s_x, 16)
            for n, (_, y) in enumerate(layouts()):
                act.wait_ge(s_flipped, n + 1)
                nc.scalar.copy(xy[y][:, HALF:], flip[:, HALF:]).then_inc(s_half, 1)
            act.wait_ge(s_x, 32)


def layouts():
    at = sum(range(1, 10)) + 1 + 10
    for k in range(11, 18):
        at += 1
        yield at % 2, (at + 1) % 2
        at += 1 + (k - 7)
        yield at % 2, (at + 1) % 2
        at += 1 + 7


def make_items(nc, c, s, rec, local_rows, tables, node_rows):
    chunks, n_items = CHUNKS[s], CHUNKS[s] * P
    ctx = ExitStack()
    with ctx:
        sp_ = Space(nc, ctx, f"items{s}")
        last_code = sp_.sb("last_code", [P, ROW // P], I32)
        last_key_i = sp_.sb("last_key_i", [P, ROW // P], I32)
        last_key = sp_.sb("last_key", [P, ROW // P])
        bound = sp_.sb("bound", [P, NTP])
        below = sp_.sb("below", [P, NTP, ROW // P])
        count = sp_.sb("count", [P, NTP])
        first = sp_.sb("first", [1, NTP])
        items_i = sp_.sb("items_i", [1, NT], I32)
        items_f = sp_.sb("items_f", [1, NT])
        ones = sp_.sb("ones", [1, NT])
        start = sp_.sb("start", [1, NTP])
        ahead = sp_.sb("ahead", [1, NTP])
        step = sp_.sb("step", [1, NT])
        turns = sp_.sb("turns", [1, EXTRA])
        turns_i = sp_.sb("turns_i", [1, EXTRA], I32)
        start_c, step_c = sp_.sb("start_c", [NT, 1]), sp_.sb("step_c", [NT, 1])
        began = sp_.sb("began", [NT, n_items])
        node_of, off_of = sp_.sb("node_of", [P, chunks]), sp_.sb("off_of", [P, chunks])
        tile_f = sp_.sb("tile_f", [P, chunks])
        tile_i = sp_.sb("tile_i", [P, chunks], I32)
        rows = sp_.sb("rows", [P, chunks, P], I32)
        keys_r = sp_.sb("keys_r", [P, chunks, P], I32)
        local_r = sp_.sb("local_r", [P, chunks, P])
        code_t = sp_.sb("code_t", [P, n_items])
        keys_t = sp_.sb("keys_t", [P, n_items], I32)
        p_first = sp_.ps("p_first", [P, 512])
        p_node = sp_.ps("p_node", [P, 3, 512])
        p_flip = sp_.ps("p_flip", [P, 3, 512])
        s_load, s_dve, s_first, s_began, s_node, s_tile, s_out = (
            sp_.sem(x) for x in ("load", "dve", "first", "began", "node", "tile", "out"))
        s_flip, s_table, s_count, s_start, s_column = (sp_.sem(x) for x in ("flip", "table", "count", "start", "column"))
        s_rows = sp_.gathered(0)
        g = {"pay": sp_.sb("pay", [P, n_items], I32), "key": sp_.sb("key", [P, n_items]),
             "local": sp_.sb("local", [P, n_items]), "node_f": sp_.sb("node_f", [P, n_items]),
             "node_i": sp_.sb("node_i", [1, NODE_COLS[s]], I32), "packed": sp_.sb("packed", [1, n_items // GRP])}
        parts = [(a, min(a + 384, n_items)) for a in range(0, n_items, 384)]
        block = sp_.block()

        @block.sync
        def _(sp):
            with nc.allow_non_contiguous_dma(reason="the last code of every edge tile"):
                sp.dma_start(last_code[:, :], rec[s][0:ET2, P - 1].rearrange("(p a) -> p a", a=ROW // P)).then_inc(s_load, 16)
            sp.wait_ge(s_table, 1)
            for q in range(chunks):
                sp.dma_start(local_rows[s][q * P:(q + 1) * P, :], local_r[:, q, :]).then_inc(s_out, 16)
            sp.wait_ge(s_table, 2)
            sp.dma_start(tables[s][0, :, :], g["pay"][:, :]).then_inc(s_out, 16)
            sp.dma_start(tables[s][1, :, :], g["key"][:, :].bitcast(I32)).then_inc(s_out, 16)
            sp.dma_start(tables[s][2, :, :], g["local"][:, :].bitcast(I32)).then_inc(s_out, 16)
            sp.dma_start(tables[s][3, :, :], g["node_f"][:, :].bitcast(I32)).then_inc(s_out, 16)
            sp.dma_start(node_rows[s], g["node_i"][:, :]).then_inc(s_out, 16)
            sp.wait_ge(s_out, 16 * (chunks + 5))

        @block.vector
        def _(dve):
            done = Chain(dve, s_dve)
            dve.wait_ge(s_load, 16)
            done(nc.vector.tensor_scalar(last_key_i[:, :], last_code[:, :], KEY_SHIFT, FIELD,
                                         ALU.logical_shift_right, ALU.bitwise_and))
            done.mark(nc.vector.tensor_copy(last_key[:, :], last_key_i[:, :]))
            done(nc.vector.tensor_scalar(bound[:, :], c["ramp"][:, 0:NTP], float(P), float(N), ALU.mult, ALU.min))
            done(nc.vector.tensor_tensor(below[:, :, :], last_key[:, None, :].to_broadcast([P, NTP, ROW // P]),
                                         bound[:, :, None].to_broadcast([P, NTP, ROW // P]), ALU.is_lt))
            done(nc.vector.tensor_reduce(count[:, :], below[:, :, :], axis=AX.X, op=ALU.add))
            dve.sem_inc(s_count)
            dve.wait_ge(s_first, 1)
            done(nc.vector.tensor_copy(first[:, :], p_first[0:1, 0:NTP]))
            done(nc.vector.tensor_tensor(items_f[:, :], first[:, 1:], first[:, 0:NT], ALU.subtract))
            done(nc.vector.tensor_scalar(items_i[:, :], items_f[:, :], 2.0, None, ALU.add))
            done(nc.vector.tensor_scalar(items_i[:, :], items_i[:, :], 1, 1, ALU.logical_shift_right, ALU.logical_shift_left))
            done.mark(nc.vector.tensor_copy(items_f[:, :], items_i[:, :]))
            done.mark(nc.vector.memset(ones[:, :], 1.0))
            done(nc.vector.memset(start[:, 0:1], 0.0))
            done(nc.vector.tensor_tensor_scan(start[:, 1:], ones[:, :], items_f[:, :], 0.0, ALU.mult, ALU.add))
            done(nc.vector.tensor_tensor(ahead[:, :], start[:, :], first[:, :], ALU.subtract))
            done.mark(nc.vector.memset(step[:, 0:1], 0.0))
            done.mark(nc.vector.tensor_tensor(step[:, 1:], ahead[:, 1:NT], ahead[:, 0:NT - 1], ALU.subtract))
            done(nc.vector.tensor_scalar(start[:, NT:], start[:, NT:], LEAST_ITEMS[s], None, ALU.max))
            for at, b, more in ((TURNS_ALL, NT, ROUND - 1.0), (TURNS_HYPER, NHT, ROUND - 1.0), (LAST_TURN, NT, -1.0)):
                done.mark(nc.vector.tensor_scalar(turns[:, at:at + 1], start[:, b:b + 1], more, None, ALU.add))
            done.wait()
            done(nc.vector.tensor_copy(turns_i[:, :], turns[:, :]))
            done(nc.vector.tensor_scalar(g["node_i"][:, n_items:n_items + EXTRA], turns_i[:, :], ROUND.bit_length() - 1, None,
                                         ALU.logical_shift_right))
            dve.sem_inc(s_start)
            dve.wait_ge(s_column, 1)
            done.mark(nc.vector.tensor_copy(start_c[:, :], p_first[0:NT, 64:65]))
            done(nc.vector.tensor_copy(step_c[:, :], p_first[0:NT, 65:66]))
            done(nc.vector.tensor_scalar(began[:, :], c["ramp"][0:NT, 0:n_items], start_c[:, 0:1], None, ALU.is_ge))
            done(nc.vector.memset(began[0:1, :], 0.0))
            dve.sem_inc(s_began)
            dve.wait_ge(s_node, 1)
            done.mark(nc.vector.tensor_copy(node_of[:, :], p_first[:, 128:128 + chunks]))
            done(nc.vector.tensor_copy(off_of[:, :], p_first[:, 192:192 + chunks]))
            done(nc.vector.tensor_tensor(tile_f[:, :], c["item_of"][:, 0:chunks], off_of[:, :], ALU.subtract))
            done(nc.vector.tensor_scalar_min(tile_f[:, :], tile_f[:, :], float(ET2)))
            done(nc.vector.tensor_copy(tile_i[:, :], tile_f[:, :]))
            dve.sem_inc(s_tile)
            for n, (a, b) in enumerate(parts):
                done.mark(nc.vector.tensor_copy(g["node_f"][:, a:b], p_node[:, n, 0:b - a]))
            done.wait()
            done.mark(nc.vector.tensor_copy(g["node_i"][:, 0:n_items], g["node_f"][0:1, :]))
            of_pair = lambda j: g["node_f"][0:1, 2 * j::GRP]
            done(nc.vector.tensor_copy(g["packed"][:, :], of_pair(PAIRS - 1)))
            for j in range(PAIRS - 2, -1, -1):
                done(nc.vector.scalar_tensor_tensor(g["packed"][:, :], g["packed"][:, :], float(1 << PACKED), of_pair(j),
                                                    ALU.mult, ALU.add))
            done(nc.vector.tensor_copy(g["node_i"][:, n_items + EXTRA:], g["packed"][:, :]))
            dve.wait_ge(s_rows, 16 * chunks)
            done(nc.vector.tensor_scalar(keys_r[:, :, :], rows[:, :, :], KEY_SHIFT, FIELD,
                                         ALU.logical_shift_right, ALU.bitwise_and))
            done(nc.vector.tensor_copy(local_r[:, :, :], keys_r[:, :, :]))
            for q in range(chunks):
                done(nc.vector.scalar_tensor_tensor(local_r[:, q, :], node_of[:, q:q + 1].to_broadcast([P, P]), -float(P),
                                                    local_r[:, q, :], ALU.mult, ALU.add))
            dve.sem_inc(s_table)
            dve.wait_ge(s_flip, 1)
            for n, (a, b) in enumerate(parts):
                done.mark(nc.vector.tensor_copy(code_t[:, a:b], p_flip[:, n, 0:b - a]))
            done.wait()
            code = code_t[:, :].bitcast(I32)
            done.mark(nc.vector.tensor_scalar(g["pay"][:, :], code, FIELD, None, ALU.bitwise_and))
            done(nc.vector.tensor_scalar(keys_t[:, :], code, KEY_SHIFT, FIELD, ALU.logical_shift_right, ALU.bitwise_and))
            done(nc.vector.tensor_copy(g["key"][:, :], keys_t[:, :]))
            done(nc.vector.scalar_tensor_tensor(g["local"][:, :], g["node_f"][:, :], -float(P), g["key"][:, :],
                                                ALU.mult, ALU.add))
            dve.sem_inc(s_table)

        @block.tensor
        def _(pe):
            pe.wait_ge(s_count, 1)
            nc.tensor.matmul(p_first[:, 0:NTP], c["ones"][:, :], count[:, :], start=True, stop=True).then_inc(s_first, 1)
            pe.wait_ge(s_start, 1)
            nc.tensor.matmul(p_first[0:NT, 64:65], start[:, 0:NT], c["ones"][0:1, 0:1], start=True, stop=True)
            nc.tensor.matmul(p_first[0:NT, 65:66], step[:, :], c["ones"][0:1, 0:1], start=True, stop=True).then_inc(s_column, 1)
            pe.wait_ge(s_began, 1)
            for n, (a, b) in enumerate(parts):
                nc.tensor.matmul(p_node[:, n, 0:b - a], c["ones"][0:NT, :], began[:, a:b], start=True, stop=True)
            for q in range(chunks):
                nc.tensor.matmul(p_first[:, 128 + q:129 + q], began[:, q * P:(q + 1) * P], c["ones"][0:NT, 0:1],
                                 start=True, stop=True)
                last = nc.tensor.matmul(p_first[:, 192 + q:193 + q], began[:, q * P:(q + 1) * P], step_c[:, :],
                                        start=True, stop=True)
            last.then_inc(s_node, 1)
            pe.wait_ge(s_rows, 16 * chunks)
            for q in range(chunks):
                last = nc.tensor.transpose(p_flip[:, q // 3, q % 3 * P:(q % 3 + 1) * P],
                                           rows[:, q, :].bitcast(F32), c["ident"][:, :])
            last.then_inc(s_flip, 1)

        @block.gpsimd
        def _(pool):
            pool.wait_ge(s_tile, 1)
            for q in range(chunks):
                pool.indirect_dma_start(out=rows[:, q, :], out_offset=None, in_=rec[s][:, :],
                                        in_offset=bass.IndirectOffsetOnAxis(ap=tile_i[:, q:q + 1], axis=0)).then_inc(s_rows, 16)



def normalise(nc, c, name, x_in, xt, rows_out=None):
    ctx = ExitStack()
    with ctx:
        sp_ = Space(nc, ctx, name)
        STEPS, PIECE = NTP // 2, 10
        x = sp_.sb("x", [P, NTP, D])
        stats = sp_.sb("stats", [P, NTP, 6])
        mean, dev, var, rstd = (sp_.sb(n, [P, NTP]) for n in ("mean", "dev", "var", "rstd"))
        y = sp_.sb("y", [P, 4, 2, D])
        p_t = sp_.ps("p_t", [P, 4, 512])
        s_dve, s_stats, s_var, s_std = (sp_.sem(n) for n in ("dve", "stats", "var", "std"))
        s_y, s_t, s_xt = sp_.sem("y_ready"), sp_.sem("t_ready"), sp_.sem("t_free")
        s_load = [sp_.sem(f"load{p}") for p in range(NTP // PIECE)]
        s_out = [sp_.sem(f"out{h}") for h in range(4)]
        block = sp_.block()

        @block.sync
        def _(sp):
            for p, s_piece in enumerate(s_load):
                sp.dma_start(x[:, p * PIECE:(p + 1) * PIECE, :],
                             x_in[p * PIECE * P:(p + 1) * PIECE * P, :].rearrange("(t p) d -> p t d", p=P)).then_inc(s_piece, 16)
            if rows_out is not None:
                for u in range(STEPS):
                    sp.wait_ge(s_y, u + 1)
                    sp.dma_start(rows_out[2 * u * P:2 * (u + 1) * P, :].rearrange("(i p) d -> p i d", p=P),
                                 y[:, u % 4, :, :]).then_inc(s_out[u % 4], 16)
                for h in range(4):
                    sp.wait_ge(s_out[h], 16 * len(range(h, STEPS, 4)))

        @block.vector
        def _(dve):
            v = nc.vector
            for b in range(NTP):
                if b % PIECE == 0:
                    dve.wait_ge(s_load[b // PIECE], 16)
                last = v.bn_stats(stats[:, b, :], x[:, b, :])
            last.then_inc(s_stats, 1)
            done = Chain(dve, s_dve)
            dve.wait_ge(s_stats, 1)
            even, odd = stats[:, :, 1], stats[:, :, 4]
            done.mark(v.tensor_tensor(mean[:, :], even, odd, ALU.add))
            done.mark(v.tensor_tensor(dev[:, :], even, odd, ALU.subtract))
            done(v.tensor_tensor(var[:, :], stats[:, :, 2], stats[:, :, 5], ALU.add))
            done.mark(v.tensor_scalar(mean[:, :], mean[:, :], 0.5, None, ALU.mult))
            done.mark(v.tensor_scalar(var[:, :], var[:, :], 1.0 / D, EPS, ALU.mult, ALU.add))
            done(v.tensor_tensor(dev[:, :], dev[:, :], dev[:, :], ALU.mult))
            done(v.scalar_tensor_tensor(var[:, :], dev[:, :], 0.25, var[:, :], ALU.mult, ALU.add))
            dve.sem_inc(s_var)
            dve.wait_ge(s_std, 1)
            done(v.reciprocal(rstd[:, :], rstd[:, :]))
            for u in range(STEPS):
                if u >= 4:
                    dve.wait_ge(s_t, u - 3)
                    if rows_out is not None:
                        dve.wait_ge(s_out[u % 4], 16 * (u // 4))
                for i in range(2):
                    b = 2 * u + i
                    last = v.tensor_scalar(y[:, u % 4, i, :], x[:, b, :], mean[:, b:b + 1], rstd[:, b:b + 1],
                                           ALU.subtract, ALU.mult)
                last.then_inc(s_y, 1)

        @block.tensor
        def _(pe):
            for u in range(STEPS):
                if u >= 4:
                    pe.wait_ge(s_xt, u - 3)
                pe.wait_ge(s_y, u + 1)
                for k in range(2):
                    for i in range(2):
                        last = nc.tensor.transpose(p_t[:, u % 4, (2 * k + i) * P:(2 * k + i + 1) * P],
                                                   y[:, u % 4, i, k * P:(k + 1) * P], c["ident"][:, :])
                last.then_inc(s_t, 1)

        @block.scalar
        def _(act):
            act.wait_ge(s_var, 1)
            nc.scalar.activation(rstd[:, :], var[:, :], ACT.Sqrt).then_inc(s_std, 1)
            for u in range(STEPS):
                act.wait_ge(s_t, u + 1)
                nc.scalar.copy(xt[:, :, 2 * u * P:2 * (u + 1) * P],
                               p_t[:, u % 4, :].rearrange("p (k e) -> p k e", k=2)).then_inc(s_xt, 1)


def project(nc, c, name, xt, weights, graphs):
    ctx = ExitStack()
    with ctx:
        sp_ = Space(nc, ctx, name)
        STEPS = NTP // 2
        width = graphs[0]["width"]
        n_g = len(graphs)
        w = sp_.sb("w", [P, 2, n_g * width])
        att = sp_.sb("att", [P, 2, n_g * width])
        prod = sp_.sb("prod", [P, 2, 2, n_g * width])
        rows = sp_.sb("rows", [P, 2, 2, n_g, width + HEADS])
        scores = sp_.sb("scores", [P, 2, 2, 2, n_g * HEADS])
        nodes = [sp_.sb(f"nodes{i}", [P, NTP, 2 * HEADS]) for i in range(n_g)]
        p_x = sp_.ps("p_x", [P, 4, 512])
        s_load, s_dve, s_x, s_scores, s_rows, s_fin = (
            sp_.sem(n) for n in ("load", "dve", "x_ready", "scores", "rows", "fin"))
        s_out = [sp_.sem("out0"), sp_.sem("out1")]
        by_graph = lambda a: a.rearrange("p (g c) -> p g c", g=n_g)
        block = sp_.block()

        @block.sync
        def _(sp):
            for i, g in enumerate(graphs):
                for k in range(2):
                    sp.dma_start(w[:, k, i * width:(i + 1) * width], weights[i][k * P:(k + 1) * P, :]).then_inc(s_load, 16)
                for j, a in enumerate((g["a_dst"], g["a_src"])):
                    sp.dma_start(att[:, j, i * width:(i + 1) * width],
                                 a.rearrange("h c -> (h c)").partition_broadcast(P)).then_inc(s_load, 16)
            for u in range(STEPS):
                sp.wait_ge(s_scores, u + 1)
                for i, g in enumerate(graphs):
                    sp.dma_start(g["table"][2 * u * P:2 * (u + 1) * P, :].rearrange("(i p) c -> p i c", p=P),
                                 rows[:, u % 2, :, i, :]).then_inc(s_out[u % 2], 16)
            for h in range(2):
                sp.wait_ge(s_out[h], 16 * n_g * len(range(h, STEPS, 2)))
            for i, g in enumerate(graphs):
                sp.dma_start(g["nodes"], nodes[i][:, :, :]).then_inc(s_fin, 16)
            sp.wait_ge(s_fin, 16 * n_g)

        @block.tensor
        def _(pe):
            pe.wait_ge(s_load, 16 * 4 * n_g)
            for u in range(STEPS):
                if u >= 2:
                    pe.wait_ge(s_rows, u - 1)
                for i in range(2):
                    for k in range(2):
                        last = nc.tensor.matmul(p_x[:, u % 2 * 2 + i, 0:n_g * width],
                                                xt[:, k, (2 * u + i) * P:(2 * u + i + 1) * P], w[:, k, :],
                                                start=(k == 0), stop=(k == 1))
                last.then_inc(s_x, 1)

        @block.scalar
        def _(act):
            for u in range(STEPS):
                h = u % 2
                if u >= 2:
                    act.wait_ge(s_out[h], 16 * n_g * (u // 2))
                act.wait_ge(s_x, u + 1)
                for i in range(2):
                    last = nc.scalar.copy(rows[:, h, i, :, 0:width], by_graph(p_x[:, 2 * h + i, 0:n_g * width]))
                last.then_inc(s_rows, 1)

        @block.vector
        def _(dve):
            v = nc.vector
            done = Chain(dve, s_dve)
            dve.wait_ge(s_load, 16 * 4 * n_g)
            for u in range(STEPS):
                h = u % 2
                dve.wait_ge(s_rows, u + 1)
                for j in range(2):
                    for i in range(2):
                        done.mark(v.tensor_tensor(by_graph(prod[:, j, i, :]), rows[:, h, i, :, 0:width],
                                                  by_graph(att[:, j, :]), ALU.mult))
                done.wait()
                done(v.tensor_reduce(scores[:, h, :, :, :].rearrange("p j i e -> p (j i e)"),
                                     prod[:, :, :, :].rearrange("p j i (e c) -> p (j i e) c", e=n_g * HEADS),
                                     axis=AX.X, op=ALU.add))
                for i in range(n_g):
                    v.tensor_copy(nodes[i][:, 2 * u:2 * u + 2, :].rearrange("p i (j e) -> p i j e", j=2),
                                  scores[:, h, :, :, i * HEADS:(i + 1) * HEADS].rearrange("p j i e -> p i j e"))
                last = v.tensor_copy(rows[:, h, :, :, width:],
                                     scores[:, h, 1, :, :].rearrange("p i (g e) -> p i g e", g=n_g))
                last.then_inc(s_scores, 1)


def turns_of(eng, node_i, s, which=TURNS_ALL):
    at = CHUNKS[s] * P + which
    least = (BESIDE + 1 if s == 2 else 1) - (which == LAST_TURN)
    return eng.value_load(node_i[0:1, at:at + 1], min_val=least, max_val=ITEMS[s] // ROUND)


def pair_tiles(eng, node_i, s, t, h):
    at = CHUNKS[s] * P + EXTRA
    word = eng.value_load(node_i[0:1, bass.ds(2 * t + (h + at), 1)], min_val=0, max_val=(1 << PACKED * PAIRS) - 1)
    return [eng.snap((word >> (PACKED * j)) & ((1 << PACKED) - 1)).with_bounds(min_val=0, max_val=NT - 1)
            for j in range(PAIRS)]


def attend_pass(nc, c, name, width, tables, local_rows, node_rows, gather=None, add=None, experts=None):
    ctx = ExitStack()
    with ctx:
        sp_ = Space(nc, ctx, name)
        w, m, ch = width + HEADS, width + 2 * HEADS + 1, width // HEADS
        if gather:
            s, table, nodes_in, rows_out, al, ard = gather
            cols = CHUNKS[s] * P
            pay = sp_.sb("pay", [P, cols], I32)
            node_g = sp_.sb("node_g", [1, NODE_COLS[s]], I32)
            nodes = sp_.sb("nodes", [P, NTP, 2 * HEADS])
            index = sp_.sb("index", [P, 2, GRP], I32)
            got = sp_.sb("got", [P, 2, GRP, w])
            local_r = sp_.sb("local_r", [P, 2, GRP * P])
            spread = sp_.sb("spread", [P, 2, GRP * P])
            mine = sp_.sb("mine", [P, 2, PAIRS, 2 * HEADS])
            p_ard = sp_.ps("p_ard", [P, 2, 512])
        if add:
            s_a, rows_in, weights, acc = add
            s, cols = (s, cols) if gather else (s_a, CHUNKS[s_a] * P)
            local_c = sp_.sb("local_c", [P, cols], I32)
            node_a = sp_.sb("node_a", [1, NODE_COLS[s_a]], I32)
            kept = sp_.sb("kept", [P, 2, GRP, w])
            hot = sp_.sb("hot", [P, 2, GRP, P])
            msg = sp_.sb("msg", [P, 2, GRP, m])
            p_sum = sp_.ps("p_sum", [P, PAIRS, 512])
        ring = add and not gather
        if ring:
            running = sp_.sb("running", [P, 2, PAIRS, m])
            tile_f = sp_.sb("tile_f", [P, cols], I32)
            same = sp_.sb("same", [P, cols // 2])
        ffn = GatedExperts(nc, c, sp_, *experts) if experts else None

        def each_turn(eng, turns, body):
            if not ffn:
                with eng.Fori(0, turns) as t:
                    for h in range(2):
                        body(t, h, None)
                return
            with eng.Fori(0, BESIDE // 2) as n:
                for e in range(NEXP):
                    body(2 * n + e // 2, e % 2, (n, e))
            with eng.Fori(BESIDE, turns) as t:
                for h in range(2):
                    body(t, h, None)
        bank = lambda h, j: p_sum[:, h * PAIRS // 2 + j // 2:h * PAIRS // 2 + j // 2 + 1, j % 2 * 256:j % 2 * 256 + m]
        s_load, s_zero, s_index, s_turn, s_kept, s_spread, s_sfree, s_ard, s_pfree, s_mine = (
            sp_.sem(n) for n in ("load", "zero", "index", "turn", "kept", "spread", "sfree", "ard", "pfree", "mine"))
        s_acc, s_mfree, s_hot, s_side, s_sum, s_ran, s_stored = (
            sp_.sem(n) for n in ("acc", "mfree", "hot", "side", "sum", "ran", "stored"))
        s_local, s_out, s_rows = ([sp_.sem(f"{n}{h}") for h in range(2)] for n in ("local", "out", "rows"))
        s_got = [sp_.gathered(0), sp_.gathered(1)] if gather else None
        LOADS = 16 * (3 * bool(gather) + 2 * bool(add) + bool(ring))
        MOST_TURNS = ITEMS[s] // ROUND

        def turns_for(eng, which=TURNS_ALL):
            eng.wait_ge(s_load, LOADS)
            if s < 2:
                return MOST_TURNS - (which == LAST_TURN)
            return turns_of(eng, node_g if gather else node_a, s, which)

        block = sp_.block()

        @block.sync
        def _(sp):
            if gather:
                sp.dma_start(pay[:, :], tables[s][0, :, :]).then_inc(s_load, 16)
                sp.dma_start(node_g[:, :], node_rows[s]).then_inc(s_load, 16)
                sp.dma_start(nodes[:, :, :], nodes_in).then_inc(s_load, 16)
            if add:
                sp.dma_start(local_c[:, :], tables[s_a][2, :, :]).then_inc(s_load, 16)
                sp.dma_start(node_a[:, :], node_rows[s_a]).then_inc(s_load, 16)
            if ring:
                sp.dma_start(tile_f[:, :], tables[s_a][3, :, :]).then_inc(s_load, 16)
            turns = turns_for(sp)
            if ffn:
                ffn.load(sp)

            def body(t, h, beside):
                if add:
                    sp.wait_ge(s_hot, 2 * t + (h + 1))
                    sp.dma_start(kept[:, h, :, :], rows_in[bass.ds(2 * t + h, 1), :, :]).then_inc(s_rows[h], 16)
                if gather:
                    sp.wait_ge(s_spread, 2 * t + (h + 1))
                    sp.dma_start(local_r[:, h, :], local_rows[s][bass.ds((2 * t + h) * GRP, GRP), :]
                                 .rearrange("i e -> (i e)").partition_broadcast(P)).then_inc(s_local[h], 16)
                if beside:
                    ffn.store(sp, *beside)
            each_turn(sp, turns, body)
            if ffn:
                ffn.stored(sp)

        @block.gpsimd
        def _(pool):
            if not gather:
                return
            turns = turns_for(pool)

            def body(t, h, beside):
                pool.wait_ge(s_index, 2 * t + (h + 1))
                pool.wait_ge(s_kept, 2 * t + (h + 1))
                pool.wait_ge(s_out[h], 16 * t + 16)
                pool.sem_inc(s_turn)
                for i in range(GRP):
                    pool.indirect_dma_start(
                        out=got[:, h, i, :], out_offset=None, in_=table[:, :],
                        in_offset=bass.IndirectOffsetOnAxis(ap=index[:, h, i:i + 1], axis=0)).then_inc(s_got[h], 16)
            each_turn(pool, turns, body)

        @block.scalar
        def _(act):
            turns = turns_for(act)
            if gather:
                for h in range(2):
                    act.sem_inc(s_out[h], 16)
                    nc.scalar.copy(index[:, h, :], pay[:, h * GRP:(h + 1) * GRP]).then_inc(s_index, 1)
                act.sem_inc(s_pfree, 2)
                act.sem_inc(s_kept, 2)
                act.wait_ge(s_zero, 2)

            def side(t, h):
                act.wait_ge(s_mfree, 2 * t + (h + 1))
                nc.scalar.copy(msg[:, h, :, width:width + 2 * HEADS],
                               weights[:, bass.ds((2 * t + h) * GRP, GRP), :]).then_inc(s_side, 1)

            if ring:
                side(0, 0)
                side(0, 1)
            if ffn:
                ffn.start(act)

            def body(t, h, beside):
                if ring:
                    tiles = pair_tiles(act, node_a, s_a, t, h)
                    for j in range(PAIRS):
                        act.wait_ge(s_ran, (2 * t + h) * PAIRS + (j + 1))
                        act.wait_ge(s_stored, (2 * t + h) * PAIRS + (j + 2 * PAIRS))
                        nc.scalar.copy(acc[:, bass.ds(tiles[j], 1), :], running[:, h, j:j + 1, :]).then_inc(s_stored, 1)
                    side(t + 1, h)
                    return
                if add:
                    side(t, h)
                if beside:
                    ffn.gelu(act, *beside)
                tiles = pair_tiles(act, node_g, s, t, h)
                act.wait_ge(s_sfree, 2 * t + (h + 1))
                for j in range(PAIRS):
                    last = nc.scalar.copy(mine[:, h, j:j + 1, :], nodes[:, bass.ds(tiles[j], 1), :])
                last.then_inc(s_mine, 1)
                act.wait_ge(s_got[h], 16 * GRP * t + 16 * GRP)
                nc.scalar.copy(index[:, h, :], pay[:, bass.ds((2 * t + h + 2) * GRP, GRP)]).then_inc(s_index, 1)
                act.dma_start(rows_out[bass.ds(2 * t + h, 1), :, :], got[:, h, :, :]).then_inc(s_out[h], 16)
                nc.scalar.copy(al[:, bass.ds((2 * t + h) * GRP, GRP), :], got[:, h, :, width:]).then_inc(s_kept, 1)
                act.wait_ge(s_ard, 2 * t + (h + 1))
                nc.scalar.copy(ard[:, bass.ds((2 * t + h) * GRP, GRP), :],
                               p_ard[:, h, 0:GRP * 2 * HEADS].rearrange("p (i e) -> p i e", i=GRP)).then_inc(s_pfree, 1)
            each_turn(act, turns, body)
            for h in range(2) if gather else ():
                act.wait_ge(s_out[h], 16 * turns + 16)
                act.sem_inc(s_turn)

        @block.tensor
        def _(pe):
            turns = turns_for(pe)
            if gather:
                pe.sem_inc(s_sfree, 2)
            if ffn:
                ffn.ready(pe)

            def body(t, h, beside):
                if add:
                    pe.wait_ge(s_hot, 2 * t + (h + 3))
                    pe.wait_ge(s_side, 2 * t + (h + 1))
                    for j in range(PAIRS):
                        for i in (2 * j, 2 * j + 1):
                            last = nc.tensor.matmul(bank(h, j), hot[:, h, i, :], msg[:, h, i, :],
                                                    start=(i == 2 * j), stop=(i > 2 * j))
                        last.then_inc(s_sum, 1)
                if beside:
                    ffn.products(pe, *beside)
                if gather:
                    pe.wait_ge(s_mine, 2 * t + (h + 1))
                    pe.wait_ge(s_pfree, 2 * t + (h + 1))
                    pe.wait_ge(s_spread, 2 * t + (h + 3))
                    for i in range(GRP):
                        last = nc.tensor.matmul(p_ard[:, h, i * 8:(i + 1) * 8], spread[:, h, i * P:(i + 1) * P],
                                                mine[:, h, i // 2, :], start=True, stop=True)
                    last.then_inc(s_ard, 1)
                    pe.wait_ge(s_ard, 2 * t + (h + 1))
                    pe.sem_inc(s_sfree)
            each_turn(pe, turns, body)

        @block.vector
        def _(dve):
            v = nc.vector
            done = Chain(dve, s_acc)
            if gather:
                v.memset(al[:, :, :], 0.0).then_inc(s_zero, 1)
                v.memset(ard[:, :, :], 0.0).then_inc(s_zero, 1)
                dve.wait_ge(s_zero, 2)
                dve.sem_inc(s_spread, 2)
            if add:
                done.mark(v.memset(acc[:, :, :], 0.0))
                if ring:
                    done.mark(v.memset(running[:, :, :, :], 0.0))
                    done.mark(v.memset(same[:, 0:1], 0.0))
                done(v.memset(msg[:, :, :, :], 1.0))
                dve.sem_inc(s_mfree, 2)
                dve.sem_inc(s_hot, 2)
            turns = turns_for(dve)
            if ring:
                f = tile_f[:, :].bitcast(F32)
                done(v.tensor_tensor(same[:, 1:], f[:, 2::2], f[:, 0:cols - 2:2], ALU.is_equal))
                dve.sem_inc(s_stored, 2 * PAIRS)

            def spread_out(t, h):
                dve.wait_ge(s_local[h], 16 * t + 16)
                dve.wait_ge(s_sfree, 2 * t + (h + 1))
                v.tensor_scalar(spread[:, h, :], local_r[:, h, :], c["part"][:, 0:1], None, ALU.is_equal).then_inc(s_spread, 1)

            def messages(t, h):
                at = bass.ds((2 * t + h) * GRP, GRP)
                dve.wait_ge(s_mfree, 2 * t + (h + 1))
                v.tensor_tensor(hot[:, h, :, :], c["ramp"][:, None, 0:P].to_broadcast([P, GRP, P]),
                                local_c[:, at].bitcast(F32)[:, :, None].to_broadcast([P, GRP, P]), ALU.is_equal)
                dve.wait_ge(s_rows[h], 16 * t + 16)
                for e in range(HEADS):
                    last = v.tensor_tensor(msg[:, h, :, e * ch:(e + 1) * ch], kept[:, h, :, e * ch:(e + 1) * ch],
                                           weights[:, at, e:e + 1].to_broadcast([P, GRP, ch]), ALU.mult)
                last.then_inc(s_hot, 1)

            def add_half(t, h):
                if ring:
                    dve.wait_ge(s_stored, (2 * t + h) * PAIRS + PAIRS)
                    for j in range(PAIRS):
                        if j % 2 == 0:
                            dve.wait_ge(s_sum, (2 * t + h) * PAIRS + (j + 2))
                        before = running[:, h, j - 1:j, :] if j else running[:, 1 - h, PAIRS - 1:, :]
                        ran(v.scalar_tensor_tensor(running[:, h, j:j + 1, :], before,
                                                   same[:, bass.ds((2 * t + h) * PAIRS + j, 1)], bank(h, j),
                                                   ALU.mult, ALU.add))
                    dve.sem_inc(s_mfree)
                    return
                tiles = pair_tiles(dve, node_a, s_a, t, h)
                for j in range(PAIRS):
                    if j % 2 == 0:
                        dve.wait_ge(s_sum, (2 * t + h) * PAIRS + (j + 2))
                    to = acc[:, bass.ds(tiles[j], 1), :]
                    done(v.tensor_tensor(to, to, bank(h, j), ALU.add))
                dve.sem_inc(s_mfree)

            if not add:
                def body(t, h, beside):
                    spread_out(t, h)
                    if beside:
                        ffn.take(dve, *beside)
                if ffn:
                    ffn.free(dve)
                each_turn(dve, turns, body)
                return
            messages(0, 0)
            messages(0, 1)
            last_turn = turns_for(dve, LAST_TURN)
            ran = Chain(dve, s_ran)
            if ring:
                done = ran
            with dve.Fori(0, last_turn) as t:
                done.enter(t, 2 * PAIRS)
                for h in range(2):
                    if gather:
                        spread_out(t, h)
                    add_half(t, h)
                    messages(t + 1, h)
            done.enter_last(last_turn)
            for h in range(2):
                if gather:
                    spread_out(last_turn, h)
                add_half(last_turn, h)


def attend_weights(nc, c, name, s, tables, al, ard):
    ctx = ExitStack()
    with ctx:
        sp_ = Space(nc, ctx, name)
        ch = CHUNKS[s]
        cols = ch * P
        key = sp_.sb("key", [P, cols], I32)
        local = sp_.sb("local", [P, cols], I32)
        valid = sp_.sb("valid", [P, cols])
        gid = sp_.sb("gid", [P, cols])
        masked = sp_.sb("masked", [P, cols])
        line = [sp_.sb(f"line{i}", [P, cols]) for i in range(HEADS + 1)]
        begin, end = sp_.sb("begin", [P, cols]), sp_.sb("end", [P, cols])
        fwd, bwd = sp_.sb("fwd", [P, cols]), sp_.sb("bwd", [P, cols])
        ends = sp_.sb("ends", [P, 4, HEADS])
        row = sp_.sb("row", [HEADS, 4, P])
        same, whole, step = (sp_.sb(n, [HEADS, P + 1]) for n in ("same", "whole", "step"))
        chain = sp_.sb("chain", [HEADS, 2, P + 2])
        carry_row = sp_.sb("carry_row", [HEADS, 2, P])
        carry = sp_.sb("carry", [P, 2, HEADS])
        top = sp_.sb("top", [P, cols, HEADS])
        p_line = sp_.ps("p_line", [P, 3, 512])
        p_row = sp_.ps("p_row", [P, 512])
        s_load, s_dve, s_in, s_flip, s_copied, s_ends, s_row, s_carry, s_carried, s_exp = (
            sp_.sem(n) for n in ("load", "dve", "in", "flip", "copied", "ends", "row", "carry", "carried", "exp"))
        block = sp_.block()
        bank = lambda i: p_line[:, i // 3, i % 3 * P:(i % 3 + 1) * P]

        @block.sync
        def _(sp):
            sp.dma_start(key[:, :], tables[s][1, :, :]).then_inc(s_load, 16)
            sp.dma_start(local[:, :], tables[s][2, :, :]).then_inc(s_load, 16)

        @block.tensor
        def _(pe):
            for a in range(HEADS + 1):
                pe.wait_ge(s_in, a + 1)
                src = gid if a == 0 else masked
                for i in range(ch):
                    last = nc.tensor.transpose(bank(i), src[:, i::ch], c["ident"][:, :])
                last.then_inc(s_flip, 1)
            pe.wait_ge(s_ends, 1)
            for j in range(4):
                last = nc.tensor.transpose(p_row[0:HEADS, j * P:(j + 1) * P], ends[:, j, :], c["ident"][:, :])
            last.then_inc(s_row, 1)
            pe.wait_ge(s_carry, 1)
            for j in range(2):
                last = nc.tensor.transpose(p_row[:, j * HEADS:(j + 1) * HEADS], carry_row[:, j, :],
                                           c["ident"][0:HEADS, 0:HEADS])
            last.then_inc(s_carried, 1)
            for a in range(HEADS):
                pe.wait_ge(s_in, HEADS + 2 + a)
                for i in range(ch):
                    last = nc.tensor.transpose(bank(i), line[a + 1][:, i * P:(i + 1) * P], c["ident"][:, :])
                last.then_inc(s_flip, 1)

        @block.scalar
        def _(act):
            act.wait_ge(s_exp, 1)
            nc.scalar.activation(ard[:, :, :], ard[:, :, :], ACT.Exp).then_inc(s_exp, 1)

        @block.vector
        def _(dve):
            done = Chain(dve, s_dve)
            v = nc.vector
            dve.wait_ge(s_load, 32)
            loc, k = local[:, :].bitcast(F32), key[:, :].bitcast(F32)
            done(v.tensor_scalar(gid[:, :], loc, 0.0, None, ALU.is_ge))
            done(v.scalar_tensor_tensor(valid[:, :], loc, float(P), gid[:, :], ALU.is_lt, ALU.mult))
            done(v.scalar_tensor_tensor(gid[:, :], k, 1.0, valid[:, :], ALU.add, ALU.mult))
            dve.sem_inc(s_in)
            for a in range(HEADS + 1):
                if a:
                    done(v.tensor_tensor(masked[:, :], al[:, :, a - 1], valid[:, :], ALU.mult))
                    done(v.tensor_scalar(bwd[:, :], valid[:, :], BIG, -BIG, ALU.mult, ALU.add))
                    done(v.tensor_tensor(masked[:, :], masked[:, :], bwd[:, :], ALU.add))
                    dve.sem_inc(s_in)
                dve.wait_ge(s_flip, a + 1)
                full = ch // 3 * 3
                done.mark(v.tensor_copy(line[a][:, 0:full * P].rearrange("p (b e) -> p b e", b=ch // 3),
                                        p_line[:, 0:ch // 3, 0:3 * P]))
                if ch % 3:
                    done.mark(v.tensor_copy(line[a][:, full * P:], p_line[:, ch // 3, 0:ch % 3 * P]))
                done.wait()
            g = line[0]
            done(v.tensor_tensor(begin[:, 1:], g[:, 1:], g[:, 0:cols - 1], ALU.not_equal))
            done.mark(v.memset(end[:, cols - 1:], 0.0))
            done.mark(v.tensor_scalar(end[:, 0:cols - 1], begin[:, 1:], -BIG, None, ALU.mult))
            done.mark(v.memset(begin[:, 0:1], 0.0))
            done(v.tensor_scalar(begin[:, 1:], begin[:, 1:], -BIG, None, ALU.mult))
            for h in range(HEADS):
                done(v.tensor_tensor_scan(fwd[:, :], begin[:, :], line[h + 1][:, :], -BIG, ALU.add, ALU.max))
                done(v.tensor_tensor_scan(bwd[:, ::-1], end[:, ::-1], line[h + 1][:, ::-1], -BIG, ALU.add, ALU.max))
                done.mark(v.tensor_copy(ends[:, 0, h:h + 1], fwd[:, cols - 1:]))
                done.mark(v.tensor_copy(ends[:, 1, h:h + 1], bwd[:, 0:1]))
                done.mark(v.tensor_copy(ends[:, 2, h:h + 1], g[:, 0:1]))
                done(v.tensor_copy(ends[:, 3, h:h + 1], g[:, cols - 1:]))
            dve.sem_inc(s_ends)
            dve.wait_ge(s_row, 1)
            done.mark(v.tensor_copy(row[:, :, :], p_row[0:HEADS, :].rearrange("p (j q) -> p j q", j=4)))
            done.mark(v.memset(same[:, :], 0.0))
            done(v.memset(chain[:, :, :], -BIG))
            done.mark(v.tensor_tensor(same[:, 1:P], row[:, 2, 1:], row[:, 3, 0:P - 1], ALU.is_equal))
            done(v.tensor_tensor(whole[:, 0:P], row[:, 2, :], row[:, 3, :], ALU.is_equal))
            for j in range(2):
                nxt = same[:, 0:P] if j == 0 else same[:, 1:P + 1]
                done(v.tensor_tensor(step[:, 0:P], whole[:, 0:P], nxt, ALU.mult))
                done(v.tensor_scalar(step[:, 0:P], step[:, 0:P], BIG, -BIG, ALU.mult, ALU.add))
                if j == 0:
                    done(v.tensor_tensor_scan(chain[:, 0, 1:P + 1], step[:, 0:P], row[:, 0, :], -BIG, ALU.add, ALU.max))
                    prev = chain[:, 0, 0:P]
                else:
                    done(v.tensor_tensor_scan(chain[:, 1, 1:P + 1][:, ::-1], step[:, 0:P][:, ::-1], row[:, 1, ::-1], -BIG,
                                              ALU.add, ALU.max))
                    prev = chain[:, 1, 2:P + 2]
                done(v.tensor_scalar(step[:, 0:P], nxt, BIG, -BIG, ALU.mult, ALU.add))
                done(v.tensor_tensor(carry_row[:, j, :], prev, step[:, 0:P], ALU.add))
            dve.sem_inc(s_carry)
            dve.wait_ge(s_carried, 1)
            done(v.tensor_copy(carry[:, :, :], p_row[:, 0:2 * HEADS].rearrange("p (j h) -> p j h", j=2)))
            for h in range(HEADS):
                done.mark(v.tensor_tensor_scan(fwd[:, :], begin[:, :], line[h + 1][:, :], carry[:, 0, h:h + 1],
                                               ALU.add, ALU.max))
                done(v.tensor_tensor_scan(bwd[:, ::-1], end[:, ::-1], line[h + 1][:, ::-1], carry[:, 1, h:h + 1],
                                          ALU.add, ALU.max))
                done(v.tensor_tensor(line[h + 1][:, :], fwd[:, :], bwd[:, :], ALU.max))
                dve.sem_inc(s_in)
                dve.wait_ge(s_flip, HEADS + 2 + h)
                for i in range(ch):
                    done.mark(v.tensor_copy(top[:, i::ch, h], bank(i)))
                done.wait()
            d_score, s_score = ard[:, :, 0:HEADS], ard[:, :, HEADS:]
            done(v.tensor_tensor(top[:, :, :], top[:, :, :], s_score, ALU.max))
            done(v.tensor_tensor(top[:, :, :], top[:, :, :], d_score, ALU.add))
            done.mark(v.tensor_tensor(s_score, s_score, d_score, ALU.add))
            done(v.tensor_tensor(d_score, al[:, :, :], d_score, ALU.add))
            for x in (top[:, :, :], ard[:, :, :]):
                done.mark(v.scalar_tensor_tensor(x, x, 0.2, x, ALU.mult, ALU.max))
            done.wait()
            done.mark(v.tensor_tensor(d_score, d_score, top[:, :, :], ALU.subtract))
            done(v.tensor_tensor(s_score, s_score, top[:, :, :], ALU.subtract))
            done(v.tensor_tensor(ard[:, :, :], ard[:, :, :],
                                 valid[:, :, None].to_broadcast([P, cols, 2 * HEADS]), ALU.mult))
            dve.sem_inc(s_exp)
            dve.wait_ge(s_exp, 2)


def attend_finish(nc, c, name, width, table, bias, acc, out, counts):
    ctx = ExitStack()
    with ctx:
        sp_ = Space(nc, ctx, name)
        w, m, ch = width + HEADS, width + 2 * HEADS + 1, width // HEADS
        own = sp_.sb("own", [P, NTP, w])
        bias_b = sp_.sb("bias", [P, width])
        has, inv, cnt = (sp_.sb(n, [P, NTP]) for n in ("has", "inv", "cnt"))
        w_own, den = sp_.sb("w_own", [P, NTP, HEADS]), sp_.sb("den", [P, NTP, HEADS])
        s_load, s_dve, s_out, s_fin = (sp_.sem(n) for n in ("load", "dve", "out", "fin"))
        block = sp_.block()

        @block.sync
        def _(sp):
            sp.dma_start(own[:, :, :], table.rearrange("(t p) c -> p t c", p=P)).then_inc(s_load, 16)
            sp.dma_start(bias_b[:, :], bias.partition_broadcast(P)).then_inc(s_load, 16)
            sp.wait_ge(s_out, 1)
            sp.dma_start(out.rearrange("(t p) c -> p t c", p=P), acc[:, :, 0:width]).then_inc(s_fin, 16)
            sp.dma_start(counts, cnt[:, :]).then_inc(s_fin, 16)
            sp.wait_ge(s_fin, 32)

        @block.vector
        def _(dve):
            v = nc.vector
            done = Chain(dve, s_dve)
            done(v.tensor_copy(cnt[:, :], acc[:, :, m - 1]))
            done.mark(v.tensor_scalar(has[:, :], cnt[:, :], 1.0, None, ALU.min))
            done(v.tensor_scalar(inv[:, :], cnt[:, :], 1.0, None, ALU.max))
            done.mark(v.reciprocal(inv[:, :], inv[:, :]))
            done(v.tensor_scalar(has[:, :], has[:, :], -1.0, 1.0, ALU.mult, ALU.add))
            done(v.tensor_tensor(w_own[:, :, :], acc[:, :, width + HEADS:width + 2 * HEADS],
                                 inv[:, :, None].to_broadcast([P, NTP, HEADS]), ALU.mult))
            done(v.tensor_tensor(w_own[:, :, :], w_own[:, :, :], has[:, :, None].to_broadcast([P, NTP, HEADS]), ALU.add))
            done(v.scalar_tensor_tensor(den[:, :, :], w_own[:, :, :], 1e-16, acc[:, :, width:width + HEADS],
                                        ALU.add, ALU.add))
            done(v.reciprocal(den[:, :, :], den[:, :, :]))
            dve.wait_ge(s_load, 32)
            for e in range(HEADS):
                o, a = own[:, :, e * ch:(e + 1) * ch], acc[:, :, e * ch:(e + 1) * ch]
                done(v.tensor_tensor(o, o, w_own[:, :, e:e + 1].to_broadcast([P, NTP, ch]), ALU.mult))
                done(v.tensor_tensor(a, a, o, ALU.add))
                done(v.tensor_tensor(a, a, den[:, :, e:e + 1].to_broadcast([P, NTP, ch]), ALU.mult))
            done(v.tensor_tensor(acc[:, :, 0:width], acc[:, :, 0:width],
                                 bias_b[:, None, :].to_broadcast([P, NTP, width]), ALU.add))
            dve.sem_inc(s_out)


def both_attentions(nc, c, lists, wide, scores, biases, kept, att, counts):
    tables, local_rows, node_rows = lists
    cols, m = CHUNKS[0] * P, HC + 2 * HEADS + 1
    gather = lambda s, al, ard: (s, wide[s], scores[s], kept[s], al, ard)
    ctx = ExitStack()
    with ctx:
        ard1 = Space(nc, ctx, "att1").sb("ard", [P, cols, 2 * HEADS])
        inner = ExitStack()
        with inner:
            al1 = Space(nc, inner, "att1").sb("al", [P, cols, HEADS])
            first = ExitStack()
            with first:
                ard0 = Space(nc, first, "att0").sb("ard", [P, cols, 2 * HEADS])
                scores0 = ExitStack()
                with scores0:
                    al0 = Space(nc, scores0, "att0").sb("al", [P, cols, HEADS])
                    attend_pass(nc, c, "att0g", HC, *lists, gather=gather(0, al0, ard0))
                    attend_weights(nc, c, "att0w", 0, tables, al0, ard0)
                acc0 = Space(nc, first, "att0").sb("acc", [P, NTP, m])
                attend_pass(nc, c, "att01", HC, *lists, gather=gather(1, al1, ard1), add=(0, kept[0], ard0, acc0))
                attend_finish(nc, c, "att0f", HC, wide[0], biases[0], acc0, att[0], counts[0])
            attend_weights(nc, c, "att1w", 1, tables, al1, ard1)
        acc1 = Space(nc, ctx, "att1").sb("acc", [P, NTP, m])
        attend_pass(nc, c, "att1s", HC, *lists, add=(1, kept[1], ard1, acc1))
        attend_finish(nc, c, "att1f", HC, wide[1], biases[1], acc1, att[1], counts[1])


def rows_product(nc, c, name, rows_in, w_in, out, tiles, bn=None, x_in=None):
    ctx = ExitStack()
    with ctx:
        sp_ = Space(nc, ctx, name)
        part = D // len(rows_in)
        G = 5
        turns = tiles // (2 * G)
        w = sp_.sb("w", [P, 2, D])
        rows = sp_.sb("rows", [P, 2, G, D])
        x = sp_.sb("x", [P, 2, G, D])
        rows_t = sp_.sb("rows_t", [P, 2, 2, P])
        y = sp_.sb("y", [P, 2, G, D])
        par = sp_.sb("par", [P, 5, D])
        scale, shift = sp_.sb("scale", [P, D]), sp_.sb("shift", [P, D])
        p_t = sp_.ps("p_t", [P, 2, 512])
        p_y = sp_.ps("p_y", [P, G, 512])
        s_w, s_dve, s_std, s_t, s_rt, s_m, s_y, s_done = (
            sp_.sem(n) for n in ("w", "dve", "std", "t", "rt", "m", "y", "done"))
        s_in, s_out = ([sp_.sem(f"{n}{h}") for h in range(2)] for n in ("in", "out"))
        n_in = 16 * (len(rows_in) + (bn is not None))
        n_w = 16 * (2 + 5 * (bn is not None))
        block = sp_.block()

        @block.sync
        def _(sp):
            for k in range(2):
                sp.dma_start(w[:, k, :], w_in[k * P:(k + 1) * P, :]).then_inc(s_w, 16)
            if bn is not None:
                for i, a in enumerate(bn):
                    sp.dma_start(par[:, i, :], a.partition_broadcast(P)).then_inc(s_w, 16)

            def load(t, h):
                at = bass.ds((2 * t + h) * G * P, G * P)
                for i, a in enumerate(rows_in):
                    sp.dma_start(rows[:, h, :, i * part:(i + 1) * part],
                                 a[at, :].rearrange("(g p) d -> p g d", p=P)).then_inc(s_in[h], 16)
                if bn is not None:
                    sp.dma_start(x[:, h, :, :], x_in[at, :].rearrange("(g p) d -> p g d", p=P)).then_inc(s_in[h], 16)

            def store(t, h):
                sp.wait_ge(s_done, 2 * t + (h + 1))
                sp.dma_start(out[bass.ds((2 * t + h) * G * P, G * P), :].rearrange("(g p) d -> p g d", p=P),
                             y[:, h, :, :]).then_inc(s_out[h], 16)
            for h in range(2):
                sp.sem_inc(s_out[h], 16)
                load(0, h)
            with sp.Fori(0, turns - 1) as t:
                for h in range(2):
                    store(t, h)
                    load(t + 1, h)
            for h in range(2):
                store(turns - 1, h)
            for h in range(2):
                sp.wait_ge(s_out[h], 16 * turns + 16)

        @block.tensor
        def _(pe):
            pe.wait_ge(s_w, n_w)
            with pe.Fori(0, turns) as t:
                for q in range(2 * G + 1):
                    if q < 2 * G:
                        h, i = q // G, q % G
                        if i == 0:
                            pe.wait_ge(s_in[h], n_in * t + n_in)
                        pe.wait_ge(s_rt, 2 * G * t + (q + 1))
                        for k in range(2):
                            last = nc.tensor.transpose(p_t[:, q % 2, k * P:(k + 1) * P], rows[:, h, i, k * P:(k + 1) * P],
                                                       c["ident"][:, :])
                        last.then_inc(s_t, 1)
                    if q:
                        n = q - 1
                        pe.wait_ge(s_rt, 2 * G * t + (n + 3))
                        pe.wait_ge(s_y, 2 * G * t + (n + 1))
                        for k in range(2):
                            last = nc.tensor.matmul(p_y[:, n % G, 0:D], rows_t[:, n % 2, k, :], w[:, k, :],
                                                    start=(k == 0), stop=(k == 1))
                        last.then_inc(s_m, 1)

        @block.scalar
        def _(act):
            if bn is not None:
                act.wait_ge(s_dve, 1)
                nc.scalar.activation(scale[:, :], shift[:, :], ACT.Sqrt).then_inc(s_std, 1)
            act.sem_inc(s_rt, 2)
            with act.Fori(0, turns) as t:
                for q in range(2 * G):
                    act.wait_ge(s_t, 2 * G * t + (q + 1))
                    nc.scalar.copy(rows_t[:, q % 2, :, :], p_t[:, q % 2, 0:D].rearrange("p (k e) -> p k e", k=2)).then_inc(s_rt, 1)

        @block.vector
        def _(dve):
            v = nc.vector
            done = Chain(dve, s_dve)
            dve.sem_inc(s_y, G)
            if bn is not None:
                b_fuse, gamma, beta, mean, var = (par[:, i, :] for i in range(5))
                dve.wait_ge(s_w, n_w)
                done(v.tensor_scalar(shift[:, :], var, EPS, None, ALU.add))
                dve.wait_ge(s_std, 1)
                done(v.reciprocal(scale[:, :], scale[:, :]))
                done.mark(v.tensor_tensor(shift[:, :], b_fuse, mean, ALU.subtract))
                done(v.tensor_tensor(scale[:, :], scale[:, :], gamma, ALU.mult))
                done(v.tensor_tensor(shift[:, :], shift[:, :], scale[:, :], ALU.mult))
                done(v.tensor_tensor(shift[:, :], shift[:, :], beta, ALU.add))
            with dve.Fori(0, turns) as t:
                done.enter(t, 2 if bn is not None else 0)
                for h in range(2):
                    dve.wait_ge(s_out[h], 16 * t + 16)
                    for i in range(G):
                        dve.wait_ge(s_m, 2 * G * t + (G * h + i + 1))
                        if bn is None:
                            v.tensor_copy(y[:, h, i, :], p_y[:, i, 0:D]).then_inc(s_y, 1)
                        else:
                            v.tensor_tensor(y[:, h, i, :], p_y[:, i, 0:D], scale[:, :], ALU.mult).then_inc(s_y, 1)
                    dve.wait_ge(s_y, 2 * G * t + (G * h + 2 * G))
                    if bn is not None:
                        a = y[:, h, :, :]
                        done(v.tensor_tensor(a, a, shift[:, None, :].to_broadcast([P, G, D]), ALU.add))
                        dve.wait_ge(s_in[h], n_in * t + n_in)
                        v.scalar_tensor_tensor(a, a, 0.0, x[:, h, :, :], ALU.max, ALU.add).then_inc(s_done, 1)
                    else:
                        dve.sem_inc(s_done)
            if bn is not None:
                done.leave(turns)


def choose_experts(nc, c, agg, gamma, beta, gates_out):
    ctx = ExitStack()
    with ctx:
        sp_ = Space(nc, ctx, "gates")
        w = HEADS * NEXP
        a = sp_.sb("a", [P, NTP, w])
        sq = sp_.sb("sq", [P, NTP, w])
        par = sp_.sb("par", [P, 2, w])
        mean, var = sp_.sb("mean", [P, NTP]), sp_.sb("var", [P, NTP])
        score, rank, gate = (sp_.sb(n, [P, NTP, NEXP]) for n in ("score", "rank", "gate"))
        cmp, top, total = (sp_.sb(n, [P, NTP]) for n in ("cmp", "top", "total"))
        s_load, s_dve, s_act, s_var, s_exp, s_out, s_done = (
            sp_.sem(n) for n in ("load", "dve", "act", "var", "exp", "out", "done"))
        block = sp_.block()

        @block.sync
        def _(sp):
            sp.dma_start(a[:, :, :], agg.rearrange("(t p) c -> p t c", p=P)).then_inc(s_load, 16)
            sp.dma_start(par[:, 0, :], gamma.partition_broadcast(P)).then_inc(s_load, 16)
            sp.dma_start(par[:, 1, :], beta.partition_broadcast(P)).then_inc(s_load, 16)
            sp.wait_ge(s_done, 1)
            sp.dma_start(gates_out, gate[:, :, :]).then_inc(s_out, 16)
            sp.wait_ge(s_out, 16)

        @block.scalar
        def _(act):
            act.wait_ge(s_var, 1)
            nc.scalar.activation(var[:, :], var[:, :], ACT.Sqrt).then_inc(s_act, 1)
            act.wait_ge(s_exp, 1)
            nc.scalar.activation(gate[:, :, :], score[:, :, :], ACT.Exp).then_inc(s_act, 1)

        @block.vector
        def _(dve):
            v = nc.vector
            done = Chain(dve, s_dve)
            wide = lambda m, n: m[:, :, None].to_broadcast([P, NTP, n])
            dve.wait_ge(s_load, 48)
            done(v.tensor_reduce(mean[:, :], a[:, :, :], axis=AX.X, op=ALU.add))
            done(v.tensor_scalar(mean[:, :], mean[:, :], 1.0 / w, None, ALU.mult))
            done(v.tensor_tensor(a[:, :, :], a[:, :, :], wide(mean, w), ALU.subtract))
            done(v.tensor_tensor(sq[:, :, :], a[:, :, :], a[:, :, :], ALU.mult))
            done(v.tensor_reduce(var[:, :], sq[:, :, :], axis=AX.X, op=ALU.add))
            done(v.tensor_scalar(var[:, :], var[:, :], 1.0 / w, EPS, ALU.mult, ALU.add))
            dve.sem_inc(s_var)
            dve.wait_ge(s_act, 1)
            done(v.reciprocal(var[:, :], var[:, :]))
            done(v.tensor_tensor(a[:, :, :], a[:, :, :], wide(var, w), ALU.mult))
            done(v.tensor_tensor(a[:, :, :], a[:, :, :], par[:, 0:1, :].to_broadcast([P, NTP, w]), ALU.mult))
            done(v.tensor_tensor(a[:, :, :], a[:, :, :], par[:, 1:2, :].to_broadcast([P, NTP, w]), ALU.add))
            done(v.tensor_tensor(score[:, :, :], a[:, :, 0:NEXP], a[:, :, NEXP:2 * NEXP], ALU.add))
            for h in range(2, HEADS):
                done(v.tensor_tensor(score[:, :, :], score[:, :, :], a[:, :, h * NEXP:(h + 1) * NEXP], ALU.add))
            done(v.tensor_scalar(score[:, :, :], score[:, :, :], 1.0 / HEADS, None, ALU.mult))
            done(v.memset(rank[:, :, :], 0.0))
            for e in range(NEXP):
                for j in range(NEXP):
                    if j != e:
                        done(v.tensor_tensor(cmp[:, :], score[:, :, j], score[:, :, e], ALU.is_ge if j < e else ALU.is_gt))
                        done(v.tensor_tensor(rank[:, :, e], rank[:, :, e], cmp[:, :], ALU.add))
            done(v.tensor_reduce(top[:, :], score[:, :, :], axis=AX.X, op=ALU.max))
            done(v.tensor_tensor(score[:, :, :], score[:, :, :], wide(top, NEXP), ALU.subtract))
            dve.sem_inc(s_exp)
            dve.wait_ge(s_act, 2)
            done(v.scalar_tensor_tensor(gate[:, :, :], rank[:, :, :], 2.0, gate[:, :, :], ALU.is_lt, ALU.mult))
            done(v.tensor_reduce(total[:, :], gate[:, :, :], axis=AX.X, op=ALU.add))
            done(v.reciprocal(total[:, :], total[:, :]))
            done(v.tensor_tensor(gate[:, :, :], gate[:, :, :], wide(total, NEXP), ALU.mult))
            dve.sem_inc(s_done)


def apply_gates(nc, c, x_in, gates_in, done_in, out):
    ctx = ExitStack()
    with ctx:
        sp_ = Space(nc, ctx, "apply")
        G = 5
        turns = NTP // (2 * G)
        gates = sp_.sb("gates", [P, NTP, NEXP])
        gate = sp_.sb("gate", [P, 2, G, NEXP])
        y = sp_.sb("y", [P, 2, NEXP, G, D])
        x = sp_.sb("x", [P, 2, G, D])
        s_gates, s_gate, s_gfree, s_dve, s_done = (sp_.sem(n) for n in ("gates", "gate", "gfree", "dve", "done"))
        s_in, s_out = ([sp_.sem(f"{n}{h}") for h in range(2)] for n in ("in", "out"))
        block = sp_.block()

        @block.sync
        def _(sp):
            sp.dma_start(gates[:, :, :], gates_in).then_inc(s_gates, 16)

            def load(t, h):
                at = bass.ds((2 * t + h) * G * P, G * P)
                for e in range(NEXP):
                    sp.dma_start(y[:, h, e, :, :], done_in[e][at, :].rearrange("(g p) d -> p g d", p=P)).then_inc(s_in[h], 16)
                sp.dma_start(x[:, h, :, :], x_in[at, :].rearrange("(g p) d -> p g d", p=P)).then_inc(s_in[h], 16)

            def store(t, h):
                sp.wait_ge(s_done, 2 * t + (h + 1))
                sp.dma_start(out[bass.ds((2 * t + h) * G * P, G * P), :].rearrange("(g p) d -> p g d", p=P),
                             x[:, h, :, :]).then_inc(s_out[h], 16)
            load(0, 0)
            load(0, 1)
            with sp.Fori(0, turns - 1) as t:
                for h in range(2):
                    store(t, h)
                    sp.wait_ge(s_out[h], 16 * t + 16)
                    load(t + 1, h)
            for h in range(2):
                store(turns - 1, h)
            for h in range(2):
                sp.wait_ge(s_out[h], 16 * turns)

        @block.scalar
        def _(act):
            act.wait_ge(s_gates, 16)
            act.sem_inc(s_gfree, 2)
            with act.Fori(0, turns) as t:
                for h in range(2):
                    act.wait_ge(s_gfree, 2 * t + (h + 1))
                    nc.scalar.copy(gate[:, h, :, :], gates[:, bass.ds((2 * t + h) * G, G), :]).then_inc(s_gate, 1)

        @block.vector
        def _(dve):
            v = nc.vector
            done = Chain(dve, s_dve)
            with dve.Fori(0, turns) as t:
                done.enter(t, 2 * (NEXP - 1) * G)
                for h in range(2):
                    dve.wait_ge(s_in[h], 16 * (NEXP + 1) * t + 16 * (NEXP + 1))
                    dve.wait_ge(s_gate, 2 * t + (h + 1))
                    for e in range(NEXP):
                        for g in range(G):
                            ins = v.scalar_tensor_tensor(x[:, h, g, :], y[:, h, e, g, :], gate[:, h, g, e:e + 1], x[:, h, g, :],
                                                         ALU.mult, ALU.add)
                            if e < NEXP - 1:
                                done.mark(ins)
                        if e < NEXP - 1:
                            done.wait()
                    ins.then_inc(s_done, 1)
                    dve.wait_ge(s_done, 2 * t + (h + 1))
                    dve.sem_inc(s_gfree)
            done.leave(turns)


class GatedExperts:

    FB = FH // P
    N_W = 16 * (3 * NEXP + 2)

    def __init__(self, nc, c, sp_, xt, w1_in, b1_in, w2_in, b2_in, out):
        self.nc, self.c, self.xt, self.ins, self.out = nc, c, xt, (w1_in, b1_in, w2_in, b2_in), out
        self.w1 = sp_.sb("w1", [P, 2, NEXP, FH])
        self.w2 = sp_.sb("w2", [P, NEXP, self.FB, D])
        self.b1 = sp_.sb("b1", [P, NEXP, self.FB])
        self.b2 = sp_.sb("b2", [1, NEXP, D])
        self.y = sp_.sb("y", [P, 2, 2, D])
        self.hid = sp_.sb("hid", [P, self.FB, 2 * P])
        self.p_h = sp_.ps("p_h", [P, self.FB, 512])
        self.p_y = sp_.ps("p_y", [P, 2, 512])
        self.s_w, self.s_h, self.s_a, self.s_y, self.s_copy = (sp_.sem(n) for n in ("w", "h", "a", "y_made", "copy"))
        self.s_y_out = [sp_.sem(f"y_out{h}") for h in range(2)]

    def load(self, sp):
        w1_in, b1_in, w2_in, b2_in = self.ins
        with self.nc.allow_non_contiguous_dma(reason="a bias per partition"):
            for e in range(NEXP):
                for k in range(2):
                    sp.dma_start(self.w1[:, k, e, :], w1_in[e, k * P:(k + 1) * P, :]).then_inc(self.s_w, 16)
                sp.dma_start(self.w2[:, e, :, :], w2_in[e, :, :].rearrange("(f p) d -> p f d", p=P)).then_inc(self.s_w, 16)
            sp.dma_start(self.b1[:, :, :].rearrange("p e f -> p (e f)"),
                         b1_in.rearrange("e (f p) -> p (e f)", p=P)).then_inc(self.s_w, 16)
        sp.dma_start(self.b2[:, :, :], b2_in.rearrange("(a e) d -> a e d", a=1)).then_inc(self.s_w, 16)
        for h in range(2):
            sp.sem_inc(self.s_y_out[h], 16)

    def store(self, sp, n, e):
        sp.wait_ge(self.s_copy, (NEXP * 2) * n + (2 * e + 4))
        sp.dma_start(self.out[e][bass.ds(n * 2 * P, 2 * P), :].rearrange("(i p) d -> p i d", p=P),
                     self.y[:, e % 2, :, :]).then_inc(self.s_y_out[e % 2], 16)

    def stored(self, sp):
        for h in range(2):
            sp.wait_ge(self.s_y_out[h], 16 * (NTP // 2 * NEXP // 2) + 16)

    def ready(self, pe):
        pe.wait_ge(self.s_w, self.N_W)

    def products(self, pe, n, e):
        nc, c, FB = self.nc, self.c, self.FB
        for f in range(FB):
            pe.wait_ge(self.s_a, (NEXP * FB) * n + (e * FB + f + 1))
            for k in range(2):
                last = nc.tensor.matmul(self.p_h[:, f, 0:2 * P], self.w1[:, k, e, f * P:(f + 1) * P],
                                        self.xt[:, k, bass.ds(n * 2 * P, 2 * P)], start=(k == 0), stop=(k == 1))
            last.then_inc(self.s_h, 1)
        for i in range(2):
            pe.wait_ge(self.s_copy, (NEXP * 2) * n + (2 * e + i + 1))
            nc.tensor.matmul(self.p_y[:, i, 0:D], c["ones"][0:1, :], self.b2[0:1, e, :], start=True, stop=False)
            for f in range(FB):
                if i == 0:
                    pe.wait_ge(self.s_a, (NEXP * FB) * n + (e * FB + f + 1 + FB))
                last = nc.tensor.matmul(self.p_y[:, i, 0:D], self.hid[:, f, i * P:(i + 1) * P], self.w2[:, e, f, :],
                                        start=False, stop=(f == FB - 1))
            last.then_inc(self.s_y, 1)

    def start(self, act):
        act.sem_inc(self.s_a, self.FB)
        act.wait_ge(self.s_w, self.N_W)

    def gelu(self, act, n, e):
        for f in range(self.FB):
            act.wait_ge(self.s_h, (NEXP * self.FB) * n + (e * self.FB + f + 1))
            self.nc.scalar.activation(self.hid[:, f, :], self.p_h[:, f, 0:2 * P], ACT.Gelu,
                                      bias=self.b1[:, e, f:f + 1]).then_inc(self.s_a, 1)

    def free(self, dve):
        dve.sem_inc(self.s_copy, 2)

    def take(self, dve, n, e):
        dve.wait_ge(self.s_y_out[e % 2], 32 * n + (16 * (e // 2) + 16))
        for i in range(2):
            dve.wait_ge(self.s_y, (NEXP * 2) * n + (2 * e + i + 1))
            self.nc.vector.tensor_copy(self.y[:, e % 2, i, :], self.p_y[:, i, 0:D]).then_inc(self.s_copy, 1)


def hyper_sum(nc, c, name, s, table, tables, node_rows, out, counts_in, x_in=None):
    ctx = ExitStack()
    with ctx:
        sp_ = Space(nc, ctx, name)
        back = s == 3
        cols, which = CHUNKS[s] * P, TURNS_ALL if back else TURNS_HYPER
        tiles_out, m = (NTP, D + 1) if back else (NHT, D)
        pay = sp_.sb("pay", [P, cols], I32)
        local = sp_.sb("local", [P, cols], I32)
        node_i = sp_.sb("node_i", [1, NODE_COLS[s]], I32)
        cnt, rest, inv = (sp_.sb(n, [P, NTP]) for n in ("cnt", "rest", "inv"))
        index = sp_.sb("index", [P, 2, GRP], I32)
        got = sp_.sb("got", [P, 2, GRP, D])
        hot = sp_.sb("hot", [P, 2, GRP, P])
        acc = sp_.sb("acc", [P, NTP, m])
        x = sp_.sb("x", [P, NTP, D]) if x_in is not None else None
        last_row = sp_.sb("last_row", [P, D])
        p_sum = sp_.ps("p_sum", [P, 2 * PAIRS, 512])
        s_load, s_clamp, s_index, s_turn, s_hot, s_sum, s_acc, s_tail, s_out, s_fin, s_x = (
            sp_.sem(n) for n in ("load", "clamp", "index", "turn", "hot", "sum", "acc", "tail", "out", "fin", "x"))
        s_got = [sp_.gathered(0), sp_.gathered(1)]
        LOADS = 16 * 5
        PIECE = 10
        block = sp_.block()

        @block.sync
        def _(sp):
            sp.dma_start(pay[:, :], tables[s][0, :, :]).then_inc(s_load, 16)
            sp.dma_start(local[:, :], tables[s][2, :, :]).then_inc(s_load, 16)
            sp.dma_start(node_i[:, :], node_rows[s]).then_inc(s_load, 16)
            sp.dma_start(cnt[:, :], counts_in).then_inc(s_load, 16)
            sp.dma_start(last_row[:, :], table[NHYP - 1, :].partition_broadcast(P)).then_inc(s_load, 16)
            if x_in is not None:
                sp.dma_start(x[:, :, :], x_in.rearrange("(t p) d -> p t d", p=P)).then_inc(s_x, 16)
            for p in range(tiles_out // PIECE):
                sp.wait_ge(s_out, p + 1)
                sp.dma_start(out[p * PIECE * P:(p + 1) * PIECE * P, :].rearrange("(t p) d -> p t d", p=P),
                             acc[:, p * PIECE:(p + 1) * PIECE, 0:D]).then_inc(s_fin, 16)
            sp.wait_ge(s_fin, 16 * (tiles_out // PIECE))

        @block.gpsimd
        def _(pool):
            pool.wait_ge(s_load, LOADS)
            turns = turns_of(pool, node_i, s, which)
            with pool.Fori(0, turns) as t:
                for h in range(2):
                    pool.wait_ge(s_index, 2 * t + (h + 1))
                    pool.wait_ge(s_sum, (2 * t + h) * PAIRS + PAIRS)
                    pool.sem_inc(s_turn)
                    for i in range(GRP):
                        pool.indirect_dma_start(
                            out=got[:, h, i, :], out_offset=None, in_=table[:, :],
                            in_offset=bass.IndirectOffsetOnAxis(ap=index[:, h, i:i + 1], axis=0)).then_inc(s_got[h], 16)

        @block.scalar
        def _(act):
            act.wait_ge(s_load, LOADS)
            act.wait_ge(s_clamp, 1)
            for h in range(2):
                nc.scalar.copy(index[:, h, :], pay[:, h * GRP:(h + 1) * GRP]).then_inc(s_index, 1)
            turns = turns_of(act, node_i, s, which)
            with act.Fori(0, turns) as t:
                for h in range(2):
                    act.wait_ge(s_got[h], 16 * GRP * t + 16 * GRP)
                    nc.scalar.copy(index[:, h, :], pay[:, bass.ds((2 * t + h + 2) * GRP, GRP)]).then_inc(s_index, 1)

        @block.tensor
        def _(pe):
            pe.sem_inc(s_sum, 2 * PAIRS)
            pe.wait_ge(s_load, LOADS)
            turns = turns_of(pe, node_i, s, which)
            with pe.Fori(0, turns) as t:
                for h in range(2):
                    pe.wait_ge(s_hot, 2 * t + (h + 1))
                    pe.wait_ge(s_got[h], 16 * GRP * t + 16 * GRP)
                    for j in range(PAIRS):
                        at = h * PAIRS + j
                        for i in (2 * j, 2 * j + 1):
                            last = nc.tensor.matmul(p_sum[:, at, 0:D], hot[:, h, i, :], got[:, h, i, :],
                                                    start=(i == 2 * j), stop=(i > 2 * j))
                        for i in (2 * j, 2 * j + 1) if back else ():
                            last = nc.tensor.matmul(p_sum[:, at, D:D + 1], hot[:, h, i, :], c["ones"][:, 0:1],
                                                    start=(i == 2 * j), stop=(i > 2 * j))
                        last.then_inc(s_sum, 1)

        @block.vector
        def _(dve):
            v = nc.vector
            done = Chain(dve, s_acc)
            dve.wait_ge(s_load, LOADS)
            done(v.tensor_scalar_min(pay[:, :], pay[:, :], float(NHYP - 1 if back else N - 1)))
            dve.sem_inc(s_clamp)
            loc = local[:, :].bitcast(F32)
            turns = turns_of(dve, node_i, s, which)

            def one_hot(t, h):
                at = bass.ds((2 * t + h) * GRP, GRP)
                v.tensor_tensor(hot[:, h, :, :], c["ramp"][:, None, 0:P].to_broadcast([P, GRP, P]),
                                loc[:, at][:, :, None].to_broadcast([P, GRP, P]), ALU.is_equal).then_inc(s_hot, 1)

            one_hot(0, 0)
            one_hot(0, 1)
            done(v.memset(acc[:, :, :], 0.0))
            with dve.Fori(0, turns) as t:
                done.enter(t, 2 * PAIRS)
                for h in range(2):
                    tiles = pair_tiles(dve, node_i, s, t, h)
                    for j in range(PAIRS):
                        dve.wait_ge(s_sum, (2 * t + h) * PAIRS + (j + 1 + 2 * PAIRS))
                        to = acc[:, bass.ds(tiles[j], 1), :]
                        done(v.tensor_tensor(to, to, p_sum[:, h * PAIRS + j:h * PAIRS + j + 1, 0:m], ALU.add))
                    one_hot(t + 1, h)
            done = Chain(dve, s_tail)
            if back:
                done.mark(v.tensor_tensor(rest[:, :], cnt[:, :], acc[:, :, D], ALU.subtract))
            done(v.tensor_scalar(inv[:, :], cnt[:, :], 1.0, None, ALU.max))
            done(v.reciprocal(inv[:, :], inv[:, :]))
            if x_in is not None:
                dve.wait_ge(s_x, 16)
            for p in range(tiles_out // PIECE):
                piece = range(p * PIECE, (p + 1) * PIECE)
                if back:
                    for b in piece:
                        done.mark(v.scalar_tensor_tensor(acc[:, b, 0:D], last_row[:, :], rest[:, b:b + 1], acc[:, b, 0:D],
                                                         ALU.mult, ALU.add))
                    done.wait()
                for b in piece:
                    if x_in is not None:
                        done.mark(v.scalar_tensor_tensor(acc[:, b, 0:D], acc[:, b, 0:D], inv[:, b:b + 1], x[:, b, :],
                                                         ALU.mult, ALU.add))
                    else:
                        done.mark(v.tensor_scalar(acc[:, b, 0:D], acc[:, b, 0:D], inv[:, b:b + 1], 0.0, ALU.mult, ALU.max))
                done.wait()
                dve.sem_inc(s_out)


def route(nc, c, xt, rows_in, gate_w, gate_b, slots, done_out, coef_out, index_out, units_out):
    ctx = ExitStack()
    with ctx:
        sp_ = Space(nc, ctx, "route")
        M = MEXP
        gw = sp_.sb("gw", [P, 2, M])
        gb = sp_.sb("gb", [M, 1])
        zero = sp_.sb("zero", [P, 4096])
        rows = sp_.sb("rows", [P, NTP, D])
        logit_t = sp_.sb("logit_t", [M, NPAD])
        prob, one, tmp, place = (sp_.sb(n, [P, NTP, M]) for n in ("prob", "one", "tmp", "place"))
        top, total, taken, pos, expert, token, kept, coef, slot = (
            sp_.sb(n, [P, NTP]) for n in ("top", "total", "taken", "pos", "expert", "token", "kept", "coef", "slot"))
        before = sp_.sb("before", [P, P])
        per_tile, ahead = sp_.sb("per_tile", [P, NTP, M]), sp_.sb("ahead", [P, M, NTP + 1])
        index = sp_.sb("index", [P, NTP], I32)
        back = sp_.sb("back", [P, NTP], I32)
        n_units, until, unused = (sp_.sb(n, [1, M]) for n in ("n_units", "until", "unused"))
        n_units_i = sp_.sb("n_units_i", [1, M], I32)
        behind = sp_.sb("behind", [1, MOST_UNITS, M])
        unit = sp_.sb("unit", [1, 2 * MOST_UNITS + 1])
        unit_i = sp_.sb("unit_i", [1, 2 * MOST_UNITS + 1], I32)
        p_log = sp_.ps("p_log", [P, 2, 512])
        p_tok = sp_.ps("p_tok", [P, 512])
        p_pre = sp_.ps("p_pre", [P, 2, 512])
        s_load, s_zero, s_fill, s_dve, s_log, s_logged, s_tok, s_exp, s_one, s_pre, s_index, s_done, s_out, s_tri = (
            sp_.sem(n) for n in ("load", "zero", "fill", "dve", "log", "logged", "tok", "exp", "one", "pre", "index",
                                 "done", "out", "tri"))
        s_rows, s_sent = sp_.sem("rows_in"), sp_.gathered(0)
        pieces = [(a, min(a + 512, NPAD)) for a in range(0, NPAD, 512)]
        block = sp_.block()

        @block.sync
        def _(sp):
            for k in range(2):
                sp.dma_start(gw[:, k, :], gate_w[k * P:(k + 1) * P, :]).then_inc(s_load, 16)
            sp.dma_start(gb[:, :], gate_b.rearrange("(e a) -> e a", a=1)).then_inc(s_load, 16)
            sp.wait_ge(s_zero, 1)
            n = MEXP * CAPP * D // P // 4096
            for a in (slots, done_out):
                flat = a[0:MEXP * CAPP, :].rearrange("(n p r) d -> n p (r d)", n=n, p=P)
                for i in range(n):
                    sp.dma_start(flat[i, :, :], zero[:, :]).then_inc(s_fill, 16)
                sp.dma_start(a[MEXP * CAPP:SLOTS, :].rearrange("(p r) d -> p (r d)", p=P),
                             zero[:, 0:SPARE * UNIT * D // P]).then_inc(s_fill, 16)
            sp.dma_start(rows[:, :, :], rows_in.rearrange("(t p) d -> p t d", p=P)).then_inc(s_rows, 16)
            sp.wait_ge(s_done, 1)
            sp.dma_start(coef_out, coef[:, :]).then_inc(s_out, 16)
            sp.dma_start(index_out, back[:, :]).then_inc(s_out, 16)
            sp.dma_start(units_out, unit_i[:, :]).then_inc(s_out, 16)
            sp.wait_ge(s_out, 48)
            sp.wait_ge(s_fill, 16 * 2 * (n + 1))

        @block.gpsimd
        def _(pool):
            nc.gpsimd.memset(zero[:, :], 0.0).then_inc(s_zero, 1)
            pool.wait_ge(s_zero, 1)
            nc.gpsimd.affine_select(out=before[:, :], in_=c["ones"][:, :], compare_op=ALU.is_gt, fill=0.0, base=0,
                                    pattern=[[1, P]], channel_multiplier=-1).then_inc(s_tri, 1)
            pool.wait_ge(s_rows, 16)
            pool.wait_ge(s_fill, 16 * 2 * (MEXP * CAPP * D // P // 4096 + 1))
            pool.wait_ge(s_index, 1)
            for t in range(NTP):
                pool.indirect_dma_start(out=slots[:, :], out_offset=bass.IndirectOffsetOnAxis(ap=index[:, t:t + 1], axis=0),
                                        in_=rows[:, t, :], in_offset=None,
                                        bounds_check=MEXP * CAPP - 1, oob_is_err=False).then_inc(s_sent, 16)
            pool.wait_ge(s_sent, 16 * NTP)

        @block.tensor
        def _(pe):
            pe.wait_ge(s_load, 48)
            for n, (a, b) in enumerate(pieces):
                if n >= 2:
                    pe.wait_ge(s_logged, n - 1)
                for k in range(2):
                    last = nc.tensor.matmul(p_log[0:M, n % 2, 0:b - a], gw[:, k, :], xt[:, k, a:b],
                                            start=(k == 0), stop=(k == 1))
                last.then_inc(s_log, 1)
            pe.wait_ge(s_logged, len(pieces))
            for t in range(NTP):
                last = nc.tensor.transpose(p_tok[:, t * M:(t + 1) * M], logit_t[:, t * P:(t + 1) * P], c["ident"][0:M, 0:M])
            last.then_inc(s_tok, 1)
            pe.wait_ge(s_tri, 1)
            pe.wait_ge(s_one, 1)
            flat = one[:, :, :].rearrange("p t e -> p (t e)")
            nc.tensor.matmul(p_pre[:, 0, 0:NTP * M], before[:, :], flat, start=True, stop=True)
            nc.tensor.matmul(p_pre[:, 1, 0:NTP * M], c["ones"][:, :], flat, start=True, stop=True).then_inc(s_pre, 1)

        @block.scalar
        def _(act):
            for n, (a, b) in enumerate(pieces):
                act.wait_ge(s_log, n + 1)
                nc.scalar.activation(logit_t[:, a:b], p_log[0:M, n % 2, 0:b - a], ACT.Identity, bias=gb[:, 0:1]).then_inc(s_logged, 1)
            act.wait_ge(s_exp, 1)
            nc.scalar.activation(prob[:, :, :], prob[:, :, :], ACT.Exp).then_inc(s_exp, 1)

        @block.vector
        def _(dve):
            v = nc.vector
            done = Chain(dve, s_dve)
            wide = lambda m: m[:, :, None].to_broadcast([P, NTP, M])
            dve.wait_ge(s_tok, 1)
            done(v.tensor_copy(prob[:, :, :], p_tok[:, 0:NTP * M].rearrange("p (t e) -> p t e", e=M)))
            done(v.tensor_reduce(top[:, :], prob[:, :, :], axis=AX.X, op=ALU.max))
            done(v.tensor_tensor(prob[:, :, :], prob[:, :, :], wide(top), ALU.subtract))
            dve.sem_inc(s_exp)
            dve.wait_ge(s_exp, 2)
            done(v.tensor_reduce(total[:, :], prob[:, :, :], axis=AX.X, op=ALU.add))
            done(v.reciprocal(total[:, :], total[:, :]))
            done(v.tensor_tensor(prob[:, :, :], prob[:, :, :], wide(total), ALU.mult))
            done(v.tensor_reduce(top[:, :], prob[:, :, :], axis=AX.X, op=ALU.max))
            done(v.tensor_tensor(one[:, :, :], prob[:, :, :], wide(top), ALU.is_ge))
            done(v.tensor_scalar(token[:, :], c["ramp"][:, 0:NTP], float(P), c["part"][:, 0:1], ALU.mult, ALU.add))
            done(v.tensor_scalar(taken[:, :], token[:, :], float(N), None, ALU.is_ge))
            for e in range(M):
                done(v.scalar_tensor_tensor(one[:, :, e], taken[:, :], 0.5, one[:, :, e], ALU.is_lt, ALU.mult))
                done(v.tensor_tensor(taken[:, :], taken[:, :], one[:, :, e], ALU.add))
            dve.sem_inc(s_one)
            dve.wait_ge(s_pre, 1)
            done.mark(v.tensor_copy(place[:, :, :], p_pre[:, 0, 0:NTP * M].rearrange("p (t e) -> p t e", e=M)))
            done.mark(v.tensor_copy(per_tile[:, :, :], p_pre[:, 1, 0:NTP * M].rearrange("p (t e) -> p t e", e=M)))
            done(v.memset(ahead[:, :, :], 0.0))
            for e in range(M):
                done(v.tensor_tensor_scan(ahead[:, e, 1:], c["ones"][:, 0:NTP], per_tile[:, :, e], 0.0, ALU.mult, ALU.add))
            done(v.tensor_tensor(place[:, :, :], place[:, :, :], ahead[:, :, 0:NTP].rearrange("p e t -> p t e"), ALU.add))
            done(v.tensor_tensor(tmp[:, :, :], place[:, :, :], one[:, :, :], ALU.mult))
            done(v.tensor_reduce(pos[:, :], tmp[:, :, :], axis=AX.X, op=ALU.add))
            done(v.tensor_tensor(tmp[:, :, :], one[:, :, :], c["ramp"][:, None, 0:M].to_broadcast([P, NTP, M]), ALU.mult))
            done(v.tensor_reduce(expert[:, :], tmp[:, :, :], axis=AX.X, op=ALU.add))
            done(v.tensor_scalar(kept[:, :], pos[:, :], float(CAP), None, ALU.is_lt))
            done(v.tensor_scalar(token[:, :], token[:, :], float(N), None, ALU.is_lt))
            done(v.tensor_tensor(kept[:, :], kept[:, :], token[:, :], ALU.mult))
            done(v.tensor_tensor(coef[:, :], top[:, :], kept[:, :], ALU.mult))
            done(v.scalar_tensor_tensor(slot[:, :], expert[:, :], float(CAPP), pos[:, :], ALU.mult, ALU.add))
            done(v.tensor_scalar(kept[:, :], kept[:, :], -float(MEXP * CAPP), float(MEXP * CAPP), ALU.mult, ALU.add))
            done(v.tensor_tensor(slot[:, :], slot[:, :], kept[:, :], ALU.add))
            done(v.tensor_copy(index[:, :], slot[:, :]))
            dve.sem_inc(s_index)
            done(v.tensor_scalar(slot[:, :], slot[:, :], float(MEXP * CAPP), None, ALU.min))
            done(v.tensor_copy(back[:, :], slot[:, :]))
            done(v.tensor_scalar(n_units[:, :], ahead[0:1, :, NTP], float(CAP), UNIT - 1.0, ALU.min, ALU.add))
            done(v.tensor_copy(n_units_i[:, :], n_units[:, :]))
            done(v.tensor_scalar(n_units_i[:, :], n_units_i[:, :], UNIT.bit_length() - 1, None, ALU.logical_shift_right))
            done(v.tensor_copy(n_units[:, :], n_units_i[:, :]))
            done.mark(v.tensor_scalar(unused[:, :], n_units[:, :], -1.0, float(EXPERT_UNITS), ALU.mult, ALU.add))
            done(v.tensor_tensor_scan(until[:, :], c["ones"][0:1, 0:M], n_units[:, :], 0.0, ALU.mult, ALU.add))
            done(v.tensor_tensor(behind[:, :, :], c["ramp"][0:1, 0:MOST_UNITS, None].to_broadcast([1, MOST_UNITS, M]),
                                 until[:, None, :].to_broadcast([1, MOST_UNITS, M]), ALU.is_ge))
            done(v.tensor_reduce(unit[:, MOST_UNITS:2 * MOST_UNITS], behind[:, :, :], axis=AX.X, op=ALU.add))
            done(v.tensor_tensor(behind[:, :, :], behind[:, :, :], unused[:, None, :].to_broadcast([1, MOST_UNITS, M]), ALU.mult))
            done(v.tensor_reduce(unit[:, 0:MOST_UNITS], behind[:, :, :], axis=AX.X, op=ALU.add))
            done(v.tensor_tensor(unit[:, 0:MOST_UNITS], unit[:, 0:MOST_UNITS], c["ramp"][0:1, 0:MOST_UNITS], ALU.add))
            done.mark(v.tensor_scalar(unit[:, 0:MOST_UNITS], unit[:, 0:MOST_UNITS], MOST_UNITS - 1.0, None, ALU.min))
            done.mark(v.tensor_scalar(unit[:, MOST_UNITS:2 * MOST_UNITS], unit[:, MOST_UNITS:2 * MOST_UNITS], M - 1.0, None, ALU.min))
            done(v.tensor_scalar(unit[:, 2 * MOST_UNITS:], until[:, M - 1:], 2.0, None, ALU.add))
            done(v.tensor_copy(unit_i[:, :], unit[:, :]))
            done(v.tensor_scalar(unit_i[:, 2 * MOST_UNITS:], unit_i[:, 2 * MOST_UNITS:], 1, None, ALU.logical_shift_right))
            dve.sem_inc(s_done)


def routed_experts(nc, c, slots, units_in, w1_in, b1_in, w2_in, b2_in, out):
    ctx = ExitStack()
    with ctx:
        sp_ = Space(nc, ctx, "moe")
        FB = MF // P
        units = sp_.sb("units", [1, 2 * MOST_UNITS + 1], I32)
        w1 = sp_.sb("w1", [P, 2, 2, MF])
        w2 = sp_.sb("w2", [P, 2, FB, D])
        b1 = sp_.sb("b1", [P, 2, FB])
        b2 = sp_.sb("b2", [1, 2, D])
        x = sp_.sb("x", [P, 2, 2, D])
        xt = sp_.sb("xt", [P, 2, 2, 2 * P])
        hid = sp_.sb("hid", [P, FB, 2 * P])
        y = sp_.sb("y", [P, 2, 2, D])
        p_t = sp_.ps("p_t", [P, 2, 512])
        p_h = sp_.ps("p_h", [P, 4, 512])
        p_y = sp_.ps("p_y", [P, 2, 512])
        s_units, s_t, s_xt, s_h, s_a, s_y, s_copy, s_last = (
            sp_.sem(n) for n in ("units", "t", "xt", "h", "a", "y", "copy", "last"))
        s_in, s_out, s_w = ([sp_.sem(f"{n}{h}") for h in range(2)] for n in ("in", "out", "w"))
        NW = 16 * 5
        by_unit = lambda a: a.rearrange("(u i p) d -> u p i d", i=2, p=P)
        block = sp_.block()

        def each_unit(eng, body):
            eng.wait_ge(s_units, 16)
            turns = eng.value_load(units[0:1, 2 * MOST_UNITS:2 * MOST_UNITS + 1], min_val=1, max_val=MOST_UNITS // 2)
            with eng.Fori(0, turns) as t:
                for h in range(2):
                    body(t, h)
            return turns

        def unit_of(eng, t, h):
            return eng.value_load(units[0:1, bass.ds(2 * t + h, 1)], min_val=0, max_val=MOST_UNITS - 1)

        @block.sync
        def _(sp):
            sp.dma_start(units[:, :], units_in).then_inc(s_units, 16)

            def body(t, h):
                unit = unit_of(sp, t, h)
                expert = sp.value_load(units[0:1, bass.ds(2 * t + (h + MOST_UNITS), 1)], min_val=0, max_val=MEXP - 1)
                sp.wait_ge(s_t, 2 * t + (h + 1))
                sp.dma_start(x[:, h, :, :], by_unit(slots)[bass.ds(unit, 1), :, :, :]
                             .rearrange("a p i d -> p (a i) d")).then_inc(s_in[h], 16)
                sp.wait_ge(s_y, 4 * t + (2 * h + 2))
                with nc.allow_non_contiguous_dma(reason="a bias per partition"):
                    for k in range(2):
                        sp.dma_start(w1[:, h, k, :], w1_in[bass.ds(expert, 1), k * P:(k + 1) * P, :]
                                     .rearrange("a p f -> p (a f)")).then_inc(s_w[h], 16)
                    sp.dma_start(w2[:, h, :, :], w2_in[bass.ds(expert, 1), :, :]
                                 .rearrange("a (f p) d -> p (a f) d", p=P)).then_inc(s_w[h], 16)
                    sp.dma_start(b1[:, h, :], b1_in[bass.ds(expert, 1), :].rearrange("a (f p) -> p (a f)", p=P)).then_inc(s_w[h], 16)
                    sp.dma_start(b2[:, h, :], b2_in[bass.ds(expert, 1), :]).then_inc(s_w[h], 16)
            each_unit(sp, body)

        @block.tensor
        def _(pe):
            pe.sem_inc(s_t, 2)
            pe.sem_inc(s_y, 4)

            def body(t, h):
                pe.wait_ge(s_in[h], 16 * t + 16)
                for k in range(2):
                    for i in range(2):
                        last = nc.tensor.transpose(p_t[:, k, i * P:(i + 1) * P], x[:, h, i, k * P:(k + 1) * P], c["ident"][:, :])
                last.then_inc(s_t, 1)
                pe.wait_ge(s_w[h], NW * t + NW)
                pe.wait_ge(s_xt, 2 * t + (h + 1))
                for f in range(FB):
                    pe.wait_ge(s_a, 2 * FB * t + (h * FB + f + 1))
                    for k in range(2):
                        last = nc.tensor.matmul(p_h[:, f % 4, 0:2 * P], w1[:, h, k, f * P:(f + 1) * P], xt[:, h, k, :],
                                                start=(k == 0), stop=(k == 1))
                    last.then_inc(s_h, 1)
                for i in range(2):
                    pe.wait_ge(s_copy, 4 * t + (2 * h + i + 1))
                    nc.tensor.matmul(p_y[:, i, 0:D], c["ones"][0:1, :], b2[0:1, h, :], start=True, stop=False)
                    for f in range(FB):
                        if i == 0:
                            pe.wait_ge(s_a, 2 * FB * t + (h * FB + f + 1 + 4))
                        last = nc.tensor.matmul(p_y[:, i, 0:D], hid[:, f, i * P:(i + 1) * P], w2[:, h, f, :],
                                                start=False, stop=(f == FB - 1))
                    last.then_inc(s_y, 1)
            each_unit(pe, body)

        @block.scalar
        def _(act):
            act.sem_inc(s_a, 4)

            def body(t, h):
                unit = unit_of(act, t, h)
                for f in range(FB):
                    act.wait_ge(s_h, 2 * FB * t + (h * FB + f + 1))
                    nc.scalar.activation(hid[:, f, :], p_h[:, f % 4, 0:2 * P], ACT.Relu, bias=b1[:, h, f:f + 1]).then_inc(s_a, 1)
                act.wait_ge(s_copy, 4 * t + (2 * h + 4))
                act.dma_start(by_unit(out)[bass.ds(unit, 1), :, :, :].rearrange("a p i d -> p (a i) d"),
                              y[:, h, :, :]).then_inc(s_out[h], 16)
            turns = each_unit(act, body)
            for h in range(2):
                act.wait_ge(s_out[h], 16 * turns + 16)
                act.sem_inc(s_last)

        @block.vector
        def _(dve):
            dve.sem_inc(s_copy, 2)
            for h in range(2):
                dve.sem_inc(s_out[h], 16)

            def body(t, h):
                dve.wait_ge(s_t, 2 * t + (h + 3))
                nc.vector.tensor_copy(xt[:, h, :, :], p_t[:, :, 0:2 * P]).then_inc(s_xt, 1)
                dve.wait_ge(s_out[h], 16 * t + 16)
                for i in range(2):
                    dve.wait_ge(s_y, 4 * t + (2 * h + i + 1 + 4))
                    nc.vector.tensor_copy(y[:, h, i, :], p_y[:, i, 0:D]).then_inc(s_copy, 1)
            each_unit(dve, body)


def combine(nc, c, expert_out, coef_in, index_in, x_in, out):
    ctx = ExitStack()
    with ctx:
        sp_ = Space(nc, ctx, "combine")
        got = sp_.sb("got", [P, NTP, D])
        x = sp_.sb("x", [P, NTP, D])
        coef = sp_.sb("coef", [P, NTP])
        index = sp_.sb("index", [P, NTP], I32)
        mask = sp_.sb("mask", [P, 5, D], I32)
        fill = sp_.sb("fill", [P, 3, D])
        s_load, s_index, s_dve, s_done, s_out = (sp_.sem(n) for n in ("load", "index", "dve", "done", "out"))
        s_got = [sp_.gathered(0), sp_.gathered(1)]
        EARLY = NTP // 2
        whole = N // P
        block = sp_.block()

        @block.sync
        def _(sp):
            sp.dma_start(index[:, :], index_in).then_inc(s_index, 16)
            sp.dma_start(coef[:, :], coef_in).then_inc(s_load, 16)
            sp.dma_start(x[:, :, :], x_in.rearrange("(t p) d -> p t d", p=P)).then_inc(s_load, 16)
            for n, (a, b) in enumerate(((0, EARLY), (EARLY, whole))):
                sp.wait_ge(s_done, n + 1)
                sp.dma_start(out[a * P:b * P, :].rearrange("(t p) d -> p t d", p=P), x[:, a:b, :]).then_inc(s_out, 16)
            sp.dma_start(out[whole * P:N, :], x[0:N - whole * P, whole, :]).then_inc(s_out, 16)
            sp.wait_ge(s_out, 48)

        @block.gpsimd
        def _(pool):
            pool.wait_ge(s_index, 16)
            for t in range(NTP):
                pool.indirect_dma_start(out=got[:, t, :], out_offset=None, in_=expert_out[:, :],
                                        in_offset=bass.IndirectOffsetOnAxis(ap=index[:, t:t + 1], axis=0)).then_inc(s_got[t >= EARLY], 16)

        @block.vector
        def _(dve):
            v = nc.vector
            done = Chain(dve, s_dve)
            for i, a in enumerate((0.0, 1e4, -1e4)):
                done.mark(v.memset(fill[:, i, :], a))
            done.wait()
            dve.wait_ge(s_load, 32)
            for a in range(0, NTP, 5):
                if a in (0, EARLY):
                    dve.wait_ge(s_got[a > 0], 16 * (NTP // 2))
                g = got[:, a:a + 5, :]
                done(v.tensor_tensor(g, g, coef[:, a:a + 5, None].to_broadcast([P, 5, D]), ALU.mult))
                for i, (value, op) in enumerate(((None, ALU.not_equal), (3.4028234e38, ALU.is_gt), (-3.4028234e38, ALU.is_lt))):
                    if value is None:
                        done(v.tensor_tensor(mask[:, :, :], g, g, op))
                    else:
                        done(v.tensor_scalar(mask[:, :, :], g, value, None, op))
                    for j in range(5):
                        done.mark(v.copy_predicated(got[:, a + j, :], mask[:, j, :], fill[:, i, :]))
                    done.wait()
                done(v.tensor_tensor(x[:, a:a + 5, :], x[:, a:a + 5, :], g, ALU.add))
                if a + 5 == EARLY:
                    dve.sem_inc(s_done)
            dve.sem_inc(s_done)


def build(nc, a, out):
    def dram(name, shape, dt=F32):
        return nc.dram_tensor(name, shape, dt).ap()

    rec = [dram(f"rec{s}", [ET2 + 1, P], I32) for s in range(LISTS)]
    local_rows = [dram(f"local_rows{s}", [CHUNKS[s] * P, P]) for s in range(LISTS)]
    tables = [dram(f"tables{s}", [4, P, CHUNKS[s] * P], I32) for s in range(LISTS)]
    node_rows = [dram(f"node_rows{s}", [1, NODE_COLS[s]], I32) for s in range(LISTS)]
    lists = (tables, local_rows, node_rows)
    x0, x1, x2, x3 = (dram(f"x{i}", [NPAD, D]) for i in range(4))
    scores = [dram(f"scores{s}", [P, NTP, 2 * HEADS]) for s in range(3)]
    wide = [dram(f"wide{s}", [NPAD, HC + HEADS]) for s in range(2)]
    slim = dram("slim", [NPAD, HEADS * NEXP + HEADS])
    att = [dram(f"att{s}", [NPAD, HC]) for s in range(2)] + [dram("att2", [NPAD, HEADS * NEXP])]
    counts = [dram(f"counts{s}", [P, NTP]) for s in range(3)]
    kept = [dram(f"kept{s}", [ITEMS1 // GRP, P, GRP * (HC + HEADS)]) for s in range(2)]
    kept2 = dram("kept_slim", [ITEMS2 // GRP, P, GRP * (HEADS * NEXP + HEADS)])
    gates = dram("gates", [P, NTP, NEXP])
    ctx = ExitStack()
    with ctx:
        sp_ = Space(nc, ctx, "main")
        c = {"ident": sp_.sb("ident", [P, P]), "ones": sp_.sb("ones", [P, P]), "ramp": sp_.sb("ramp", [P, CHM * P]),
             "part": sp_.sb("part", [P, 1]), "item_of": sp_.sb("item_of", [P, CHM]),
             "sign": sp_.sb("sign", [P, 8]), "turn": sp_.sb("turn", [P, 8])}
        GATHERED[:] = [sp_.sem("gathered0"), sp_.sem("gathered1")]
        constants(nc, c)
        sort_edges(nc, c, a["src"], a["dst"], a["L0_ffn_edge_index"], rec, a["x"], x0)
        for s in range(LISTS):
            make_items(nc, c, s, rec, local_rows, tables, node_rows)

        inner = ExitStack()
        with inner:
            xt = Space(nc, inner, "l0g").sb("xt", [P, 2, NPAD])
            normalise(nc, c, "norm0", x0, xt)
            project(nc, c, "proj0", xt, [a["L0_gnn_W_f"], a["L0_gnn_W_b"]],
                    [dict(width=HC, a_src=a[f"L0_gnn_a_src_{x}"], a_dst=a[f"L0_gnn_a_dst_{x}"], table=wide[s],
                          nodes=scores[s]) for s, x in enumerate("fb")])
        both_attentions(nc, c, lists, wide, scores, [a["L0_gnn_b_f"], a["L0_gnn_b_b"]], kept, att, counts)
        rows_product(nc, c, "fuse", att[0:2], a["L0_gnn_W_fuse"], x1, NTP,
                     bn=[a[f"L0_gnn_{n}"] for n in ("b_fuse", "gamma", "beta", "run_mean", "run_var")], x_in=x0)

        expert_out = [dram(f"expert_out{e}", [NPAD, D]) for e in range(NEXP)]
        outer = ExitStack()
        with outer:
            sp2 = Space(nc, outer, "att2")
            ard = sp2.sb("ard", [P, CHUNKS[2] * P, 2 * HEADS])
            inner = ExitStack()
            with inner:
                al = Space(nc, inner, "att2").sb("al", [P, CHUNKS[2] * P, HEADS])
                rows = ExitStack()
                with rows:
                    xt = Space(nc, rows, "l0f").sb("xt", [P, 2, NPAD])
                    normalise(nc, c, "norm1", x1, xt)
                    project(nc, c, "proj1", xt, [a["L0_ffn_W_gat"]],
                            [dict(width=HEADS * NEXP, a_src=a["L0_ffn_att_src"], a_dst=a["L0_ffn_att_dst"], table=slim,
                                  nodes=scores[2])])
                    attend_pass(nc, c, "att2g", HEADS * NEXP, *lists, gather=(2, slim, scores[2], kept2, al, ard),
                                experts=(xt, a["L0_ffn_W1"], a["L0_ffn_b1"], a["L0_ffn_W2"], a["L0_ffn_b2"], expert_out))
                attend_weights(nc, c, "att2w", 2, tables, al, ard)
            acc = sp2.sb("acc", [P, NTP, HEADS * NEXP + 2 * HEADS + 1])
            attend_pass(nc, c, "att2s", HEADS * NEXP, *lists, add=(2, kept2, ard, acc))
            attend_finish(nc, c, "att2f", HEADS * NEXP, slim, a["L0_ffn_b_gat"], acc, att[2], counts[2])
        choose_experts(nc, c, att[2], a["L0_ffn_ln_gamma"], a["L0_ffn_ln_beta"], gates)
        apply_gates(nc, c, x1, gates, expert_out, x2)

        xn, h1, e1, h2, n1, h3, e2, h4 = (
            dram(n, [NPAD if n in ("xn", "h1", "n1", "h3") else NHT * P, D]) for n in ("xn", "h1", "e1", "h2", "n1", "h3", "e2", "h4"))
        inner = ExitStack()
        with inner:
            xt = Space(nc, inner, "l1g").sb("xt", [P, 2, NPAD])
            normalise(nc, c, "norm2", x2, xt, rows_out=xn)
        rows_product(nc, c, "n2e0", [xn], a["L1_gnn_W0_n2e"], h1, NTP)
        hyper_sum(nc, c, "hyp0", 0, h1, tables, node_rows, e1, counts[0])
        rows_product(nc, c, "e2n0", [e1], a["L1_gnn_W0_e2n"], h2, NHT)
        hyper_sum(nc, c, "hyp1", 3, h2, tables, node_rows, n1, counts[1])
        rows_product(nc, c, "n2e1", [n1], a["L1_gnn_W1_n2e"], h3, NTP)
        hyper_sum(nc, c, "hyp2", 0, h3, tables, node_rows, e2, counts[0])
        rows_product(nc, c, "e2n1", [e2], a["L1_gnn_W1_e2n"], h4, NHT)
        hyper_sum(nc, c, "hyp3", 3, h4, tables, node_rows, x3, counts[1], x_in=x2)

        slots, done = dram("slots", [SLOTS, D]), dram("done", [SLOTS, D])
        units = dram("units", [1, 2 * MOST_UNITS + 1], I32)
        coef, back, xm = dram("coef", [P, NTP]), dram("back", [P, NTP], I32), dram("xm", [NPAD, D])
        inner = ExitStack()
        with inner:
            xt = Space(nc, inner, "l1f").sb("xt", [P, 2, NPAD])
            normalise(nc, c, "norm3", x3, xt, rows_out=xm)
            route(nc, c, xt, xm, a["L1_ffn_gate_w"], a["L1_ffn_gate_b"], slots, done, coef, back, units)
        routed_experts(nc, c, slots, units, a["L1_ffn_w1"], a["L1_ffn_b1"], a["L1_ffn_w2"], a["L1_ffn_b2"], done)
        combine(nc, c, done, coef, back, x3, out)


_INS = (["x", "src", "dst"]
        + ["L0_gnn_" + n for n in ("W_f", "a_src_f", "a_dst_f", "b_f", "W_b", "a_src_b", "a_dst_b", "b_b", "W_fuse",
                                   "b_fuse", "gamma", "beta", "run_mean", "run_var")]
        + ["L0_ffn_" + n for n in ("W_gat", "att_src", "att_dst", "b_gat", "ln_gamma", "ln_beta", "W1", "b1", "W2",
                                   "b2", "edge_index")]
        + ["L1_gnn_" + n for n in ("W0_n2e", "W0_e2n", "W1_n2e", "W1_e2n")]
        + ["L1_ffn_" + n for n in ("gate_w", "gate_b", "w1", "b1", "w2", "b2")])


def kernel(**inputs):
    import numpy as np
    import concourse.bacc as bacc
    from concourse.bass_utils import run_bass_kernel_spmd

    nc = bacc.Bacc("TRN2", target_bir_lowering=False, num_devices=1)
    arrays, args = {}, {}
    for name in _INS:
        arr = np.ascontiguousarray(inputs[name])
        arrays[f"in_{name}"] = arr
        args[name] = nc.dram_tensor(f"in_{name}", arr.shape, mybir.dt.from_np(arr.dtype), kind="ExternalInput").ap()
    out = nc.dram_tensor("out_x", (N, D), F32, kind="ExternalOutput").ap()
    build(nc, args, out)
    r = run_bass_kernel_spmd(nc, [arrays], core_ids=[0])
    return r.results[0]["out_x"]
```
